# Optimizing a Trainium2 kernel written in Bass

```python
import numpy as np
import jax
import jax.numpy as jnp

def _softmax(x, axis=-1):
    return jax.nn.softmax(x, axis=axis)

def _gelu(x):
    return jax.nn.gelu(x, approximate=True)

def _silu(x):
    return jax.nn.silu(x)

def _sigmoid(x):
    return jax.nn.sigmoid(x)

def _layernorm(x, axis=-1, eps=1e-05):
    m = jnp.mean(x, axis=axis, keepdims=True)
    v = jnp.var(x, axis=axis, keepdims=True)
    return (x - m) / jnp.sqrt(v + eps)

def _scatter_add(tgt, idx, src, axis=0):
    return tgt.at[idx].add(src)

def _segment_sum(src, seg, n):
    return jax.ops.segment_sum(src, seg, n)
kernel_name = 'mk_xattn_ffn_d1_seqx_r4_1f0990'

def setup_inputs(seed: int=0):
    np.random.seed(seed)
    _w = jnp.asarray

    def _rec_inputs():
        import jax
        import jax.numpy as jnp
        _rk = jax.random.key(seed)
        x = -0.000125 + 0.9999 * jax.random.normal(jax.random.fold_in(_rk, 1), (16, 256, 512), jnp.float32)
        _lenS = 256 - jax.random.randint(jax.random.fold_in(_rk, 7), (16,), 0, max(1, 256 // 4) + 1, jnp.int32)
        _lenS2 = 256 - jax.random.randint(jax.random.fold_in(_rk, 8), (16,), 0, max(1, 256 // 4) + 1, jnp.int32)
        _ctx_2048P = jax.random.normal(jax.random.fold_in(_rk, 11), (16, 16, 512), jnp.float32)
        _ctx_2048c = jax.random.dirichlet(jax.random.fold_in(_rk, 511), 0.3 * jnp.ones((16,), jnp.float32), (16, 256))
        _ctx_2048t = jnp.einsum('bsk,bkd->bsd', _ctx_2048c, _ctx_2048P)
        _ctx_2048t = _ctx_2048t * jax.lax.rsqrt(jnp.mean(jnp.square(_ctx_2048t)) + 1e-12) * 0.953939
        ctx_2048 = -1.52775e-05 + 0.999936 * (_ctx_2048t + 0.3 * jax.random.normal(jax.random.fold_in(_rk, 611), (16, 256, 512), jnp.float32))
        return (x, ctx_2048)
    x, ctx_2048 = _rec_inputs()

    def _L0_xattn_setup():
        import jax, jax.numpy as jnp
        import numpy as np
        B, S, D, H = (4, 1024, 512, 16)
        HD = D // H
        key = jax.random.key(seed)
        ks = jax.random.split(key, 12)
        sc = 1.0 / np.sqrt(D)
        inp = {'q': jax.random.normal(ks[0], (B, S, D), jnp.float32), 'k': jax.random.normal(ks[1], (B, S, D), jnp.float32), 'v': jax.random.normal(ks[2], (B, S, D), jnp.float32), 'Wq': jax.random.normal(ks[3], (D, D), jnp.float32) * sc, 'bq': jnp.zeros((D,), jnp.float32), 'Wk': jax.random.normal(ks[4], (D, D), jnp.float32) * sc, 'bk': jnp.zeros((D,), jnp.float32), 'Wv': jax.random.normal(ks[5], (D, D), jnp.float32) * sc, 'bv': jnp.zeros((D,), jnp.float32), 'Wo': jax.random.normal(ks[6], (D, D), jnp.float32) * sc, 'bo': jnp.zeros((D,), jnp.float32)}
        return inp
    _L0_xattn_all = _L0_xattn_setup()
    _L0_xattn_in = {k: v for k, v in _L0_xattn_all.items() if k in ('Wq', 'bq', 'Wk', 'bk', 'Wv', 'bv', 'Wo', 'bo')}
    del _L0_xattn_all

    def _L0_ffn_setup():
        import jax, jax.numpy as jnp
        import numpy as np
        TOP_K = 2
        key = jax.random.key(seed)
        ks = jax.random.split(key, 6)
        B, S, H, F, E = (1, 512, 512, 352, 8)
        Fs = 2 * F
        std = jnp.float32(0.02)
        return {'hidden_states': jax.random.normal(ks[0], (B, S, H), jnp.float32), 'gate_weight': jax.random.normal(ks[1], (E, H), jnp.float32) * std, 'gate_up_weights': jax.random.normal(ks[2], (E, 2 * F, H), jnp.float32) * std, 'down_weights': jax.random.normal(ks[3], (E, H, F), jnp.float32) * std, 'shared_gate_up': jax.random.normal(ks[4], (2 * Fs, H), jnp.float32) * std, 'shared_down': jax.random.normal(ks[5], (H, Fs), jnp.float32) * std}
    _L0_ffn_all = _L0_ffn_setup()
    _L0_ffn_in = {k: v for k, v in _L0_ffn_all.items() if k in ('gate_weight', 'gate_up_weights', 'down_weights', 'shared_gate_up', 'shared_down')}
    del _L0_ffn_all
    return {'x': x, 'ctx_2048': ctx_2048, 'L0_xattn_Wq': _L0_xattn_in['Wq'], 'L0_xattn_bq': _L0_xattn_in['bq'], 'L0_xattn_Wk': _L0_xattn_in['Wk'], 'L0_xattn_bk': _L0_xattn_in['bk'], 'L0_xattn_Wv': _L0_xattn_in['Wv'], 'L0_xattn_bv': _L0_xattn_in['bv'], 'L0_xattn_Wo': _L0_xattn_in['Wo'], 'L0_xattn_bo': _L0_xattn_in['bo'], 'L0_ffn_gate_weight': _L0_ffn_in['gate_weight'], 'L0_ffn_gate_up_weights': _L0_ffn_in['gate_up_weights'], 'L0_ffn_down_weights': _L0_ffn_in['down_weights'], 'L0_ffn_shared_gate_up': _L0_ffn_in['shared_gate_up'], 'L0_ffn_shared_down': _L0_ffn_in['shared_down']}

def reference(x, ctx_2048, L0_xattn_Wq, L0_xattn_bq, L0_xattn_Wk, L0_xattn_bk, L0_xattn_Wv, L0_xattn_bv, L0_xattn_Wo, L0_xattn_bo, L0_ffn_gate_weight, L0_ffn_gate_up_weights, L0_ffn_down_weights, L0_ffn_shared_gate_up, L0_ffn_shared_down):
    import jax
    import jax.numpy as jnp

    def _L0_xattn_ref(q, k, v, Wq, bq, Wk, bk, Wv, bv, Wo, bo):
        import jax, jax.numpy as jnp
        import numpy as np
        B, S, D, H = (4, 1024, 512, 16)
        HD = D // H
        bs, sl, nf = q.shape
        Q = (q @ Wq.T + bq).reshape(bs, sl, H, HD)
        K = (k @ Wk.T + bk).reshape(bs, sl, H, HD)
        V = (v @ Wv.T + bv).reshape(bs, sl, H, HD)
        score = jnp.einsum('bshd,bsgd->bshg', Q, K)
        weight = jax.nn.softmax(score, axis=-1)
        attn = jnp.einsum('bshg,bsgd->bshd', weight, V).reshape(bs, sl, nf)
        return attn @ Wo.T + bo

    def _L0_ffn_ref(hidden_states, gate_weight, gate_up_weights, down_weights, shared_gate_up, shared_down):
        import jax, jax.numpy as jnp
        import numpy as np
        TOP_K = 2
        B, S, H = hidden_states.shape
        E, twoF, _ = gate_up_weights.shape
        F = twoF // 2
        T = B * S
        x = hidden_states.reshape(T, H)
        logits = x @ gate_weight.T
        scores = jax.nn.softmax(logits, axis=-1)
        topk_w, topk_idx = jax.lax.top_k(scores, TOP_K)
        combine = jnp.zeros((T, E), x.dtype).at[jnp.arange(T)[:, None], topk_idx].add(topk_w)
        gu = jnp.einsum('th,efh->tef', x, gate_up_weights)
        act = jax.nn.silu(gu[..., :F]) * gu[..., F:]
        y = jnp.einsum('tef,te,ehf->th', act, combine, down_weights)
        Fs = shared_gate_up.shape[0] // 2
        sgu = x @ shared_gate_up.T
        sact = jax.nn.silu(sgu[:, :Fs]) * sgu[:, Fs:]
        y = y + sact @ shared_down.T
        return y.reshape(B, S, H)
    x = x + _L0_xattn_ref(_layernorm(x, axis=-1), ctx_2048, ctx_2048, L0_xattn_Wq, L0_xattn_bq, L0_xattn_Wk, L0_xattn_bk, L0_xattn_Wv, L0_xattn_bv, L0_xattn_Wo, L0_xattn_bo)
    x = x + _L0_ffn_ref(_layernorm(x, axis=-1), L0_ffn_gate_weight, L0_ffn_gate_up_weights, L0_ffn_down_weights, L0_ffn_shared_gate_up, L0_ffn_shared_down)
    return x

_drawn_inputs = setup_inputs


def setup_inputs(seed=0):
    import zlib

    import numpy as np

    out = dict(_drawn_inputs(seed))
    spreads = {'L0_xattn_bq': (0.0, 0.1),
     'L0_xattn_bk': (0.0, 0.1),
     'L0_xattn_bv': (0.0, 0.1),
     'L0_xattn_bo': (0.0, 0.1)}
    factors = {'L0_ffn_gate_weight': 7.282,
     'L0_ffn_gate_up_weights': 6.254,
     'L0_ffn_down_weights': 6.263,
     'L0_ffn_shared_gate_up': 8.0,
     'L0_ffn_shared_down': 8.0}
    for name, (base, spread) in spreads.items():
        noise = np.random.default_rng([zlib.crc32(name.encode()), seed]).standard_normal(out[name].shape)
        drawn = base * np.exp(spread * noise) if base else spread * noise
        out[name] = jnp.asarray(drawn.astype(out[name].dtype))
    for name, factor in factors.items():
        out[name] = (out[name] * factor).astype(out[name].dtype)
    return out
```

```python
from contextlib import ExitStack

import concourse.bass as bass
from concourse import mybir

F32 = mybir.dt.float32
BF16 = mybir.dt.bfloat16
U32 = mybir.dt.uint32
I32 = mybir.dt.int32
ALU = mybir.AluOpType
ACT = mybir.ActivationFunctionType
X = mybir.AxisListType.X

P = 128
D = 512
KC = D // P
H, HD = 16, 32
T = 16 * 256
NT = T // P
SUB = 2
BT = SUB * P
NB = T // BT
GT = P // H
NG = P // GT
UG = 4
NU = NG // UG
E, F = 8, 352
FS = 704
TOPK = 2
EPS = 1e-5
BANK = 512
SLOTS = T * TOPK // P + E
F_CH = [(0, 128), (128, 128), (256, 96)]
FS_CH = [(i * P, min(P, FS - i * P)) for i in range((FS + P - 1) // P)]
GB = 3
STAGES = 4
MASKED = -(2.0 ** 120)

ATTN_HEAD = [("X0", "B0"), ("X1", "B1"), ("Q0", "B2"), ("Q1", "B3"), ("K0", "B0"), ("K1", "B1"),
             ("V0", "B2"), ("V1", "B3")]
FFN_OPEN = [("Z0", "B0"), ("Z1", "B1"), ("L", "B2"), ("G0", "B3"), ("G1", "B0"), ("G2", "B1")]
SCORES = [[(f"S{s}{u}", f"A{u}") for u in range(NU)] for s in range(SUB)]
BODY = (ATTN_HEAD + FFN_OPEN + SCORES[0] + [("G3", "B2")] + SCORES[1] + [("G4", "B3"), ("G5", "B0")]
        + [("VT0", "B1"), ("VT1", "B2")]
        + [(f"T{s}{u}", f"A{u}") for s in range(SUB) for u in range(NU)]
        + [("P0", "A0"), ("D0", "B3"), ("P1", "A0"), ("D1", "B0"), ("O0", "B1"), ("O1", "B2")])
BANK_OF = dict(BODY)
FFN_STEPS = {"Z0", "Z1", "L", "G0", "G1", "G2", "G3", "G4", "G5", "D0", "D1"}


def earlier_fills(step, block):
    bank = BANK_OF[step]
    mine = [s for s, b in BODY if b == bank]
    per_block = len(mine)
    first = sum(s not in FFN_STEPS for s in mine)
    if isinstance(block, int) and block == 0:
        return sum(s not in FFN_STEPS for s in mine[:mine.index(step)])
    if isinstance(block, int) and block == NB:
        return first + (NB - 1) * per_block + sum(s in FFN_STEPS for s in mine[:mine.index(step)])
    return (block - 1) * per_block + (first + mine.index(step))


class Chain:

    def __init__(self, engine, sem):
        self.engine, self.sem, self.n, self.passes = engine, sem, 0, 0

    def enter(self, passes, per_pass):
        self.passes, self.start, self.per_pass = passes * per_pass, self.n, per_pass

    def leave(self, count):
        assert self.n - self.start == self.per_pass, (self.n - self.start, self.per_pass)
        self.n, self.passes = self.start + count * self.per_pass, 0

    def mark(self, instruction):
        self.n += 1
        return instruction.then_inc(self.sem, 1)

    def wait(self):
        self.engine.wait_ge(self.sem, self.passes + self.n)

    def link(self, instruction):
        self.mark(instruction)
        self.wait()


def build(nc, x, ctx_t, wq_t, bq, wk_t, bk, wv_t, bv, wo_t, bo, wgate_t, wgu_t, wdn_t, wsgu_t, wsdn_t, out):
    with ExitStack() as whole:
        def sem(name):
            return whole.enter_context(nc.semaphore(name))

        def dram(name, shape, dt):
            return nc.dram_tensor(name, shape, dt).ap()

        z_d = dram("z_rows", [T, D], F32)
        base_d = dram("base_rows", [T, D], F32)
        y_d = dram("expert_rows", [SLOTS * P, D], F32)
        token_d = dram("slot_tokens", [SLOTS * P, 1], I32)

        def sb(name, shape, dt, stack=whole):
            return stack.enter_context(nc.sbuf_tensor(name, shape, dt))

        psum_a = whole.enter_context(nc.psum_tensor("psum_a", [P, NU * BANK], F32))
        psum_b = [whole.enter_context(nc.psum_tensor(f"psum_b{i}", [P, BANK], F32)) for i in range(4)]

        def bank_ap(step):
            kind, i = BANK_OF[step][0], int(BANK_OF[step][1])
            return psum_a[:, i * BANK:(i + 1) * BANK] if kind == "A" else psum_b[i][:, :]

        ident = sb("ident", [P, P], F32)
        tok_scores = sb("tok_scores", [P, NT, E], F32)
        ids_col = sb("ids_col", [P, SLOTS], I32)
        pos = sb("pos", [P, TOPK, NT], U32)
        top_w = sb("top_w", [P, NT, 8], F32)
        slot_expert = sb("slot_expert", [P, SLOTS], I32)

        one = ExitStack()
        wq = sb("wq", [P, KC, D], F32, one)
        wk = sb("wk", [P, KC, D], F32, one)
        wv = sb("wv", [P, KC, D], F32, one)
        wo = sb("wo", [P, KC, D], F32, one)
        wsgu = sb("wsgu", [P, KC, 2 * FS], F32, one)
        wsdn = sb("wsdn", [P, len(FS_CH), D], F32, one)
        wgate = sb("wgate", [P, KC, E], F32, one)
        bo_rows = sb("bo_rows", [P, D], F32, one)
        bias3 = sb("bias3", [P, 3 * D], BF16, one)
        ones3 = sb("ones3", [P, BT], BF16, one)
        onehot = sb("onehot", [GT, P], BF16, one)
        other = sb("other", [GT, UG, P], BF16, one)
        own = sb("own", [P, GT], F32, one)
        neg_half = sb("neg_half", [P, 1], F32, one)
        x_sb = sb("x_sb", [P, SUB, D], F32, one)
        xbo = sb("xbo", [P, SUB, D], F32, one)
        xn = sb("xn", [P, SUB, D], F32, one)
        xn_t = sb("xn_t", [P, KC, BT], F32, one)
        cx_t = sb("cx_t", [P, KC, BT], F32, one)
        q_t = sb("q_t", [HD, BT, H], F32, one)
        k_t = sb("k_t", [HD, BT, H], F32, one)
        v_t = sb("v_t", [HD, BT, H], F32, one)
        v_p = sb("v_p", [P, SUB * NG, HD], F32, one)
        sc = sb("sc", [P, SUB, NG, H], F32, one)
        ex = sc
        pr = sb("pr", [P, SUB, NG, H], F32, one)
        row_max = sb("row_max", [P, SUB, NG], F32, one)
        row_sum = sb("row_sum", [P, SUB, NG], F32, one)
        row_inv = sb("row_inv", [P, SUB, NG], F32, one)
        spread = sb("spread", [P, SUB, NG, P], F32, one)
        spread_t = sb("spread_t", [P, SUB, NG * P], F32, one)
        at_t = xn_t
        x1 = sb("x1", [P, SUB, D], F32, one)
        z = sb("z", [P, SUB, D], F32, one)
        z_t = sb("z_t", [P, KC, BT], F32, one)
        gate_act = sb("gate_act", [P, GB, BT], F32, one)
        sh_t = sb("sh_t", [P, len(FS_CH), BT], F32, one)
        base = z_t[:, :, :].rearrange("p c t -> p (c t)").rearrange("p (s d) -> p s d", s=SUB)
        stats = sb("stats", [P, 2 * SUB, 6], F32, one)
        mv = sb("mv", [P, 2 * SUB, 2], F32, one)
        var_eps = sb("var_eps", [P, 2 * SUB], F32, one)
        rstd = sb("rstd", [P, 2 * SUB], F32, one)
        b_raw = spread[0:3, 0].rearrange("p g n -> p (g n)")[:, 0:3 * D]
        b_rest = spread[0:3, 1].rearrange("p g n -> p (g n)")[:, 0:3 * D]
        b_part = [spread_t[0:3, 0, 0:3 * D], spread_t[0:3, 1, 0:3 * D], v_t[0:3].rearrange("p t h -> p (t h)")[:, 0:3 * D]]
        b_bf = q_t[0:3].rearrange("p t h -> p (t h)")[:, 0:3 * D].bitcast(BF16)[:, 0:3 * D]
        one.close()

        two = ExitStack()
        wgu = sb("wgu", [P, KC, E * 2 * F], F32, two)
        wdn = sb("wdn", [P, len(F_CH), E * D], F32, two)
        zg = sb("zg", [P, 2, D], F32, two)
        zg_t = sb("zg_t", [P, 2, D], F32, two)
        silu = sb("silu", [P, 2, F], F32, two)
        act_g = sb("act_g", [P, 2, F], F32, two)
        act_t = sb("act_t", [P, 2, 3 * P], F32, two)
        y_sb = sb("y_sb", [P, 2, D], F32, two)
        comb = [sb(f"comb{i}", [P, 2, D], F32, two) for i in range(3)]
        comb_out = sb("comb_out", [P, 2, D], F32, two)
        gather_ix = sb("gather_ix", [P, 2], I32, two)
        pos_ix = sb("pos_ix", [P, STAGES, TOPK], U32, two)
        tok_ix = sb("tok_ix", [P, STAGES], I32, two)
        iota_e = sb("iota_e", [P, E], F32, two)
        iota_slot = sb("iota_slot", [P, SLOTS], F32, two)
        iota_rows = sb("iota_rows", [P, NT], F32, two)
        tok_id = sb("tok_id", [P, NT], I32, two)
        zero_id = sb("zero_id", [SLOTS, P], I32, two)
        id_rows = sb("id_rows", [SLOTS, P], F32, two)
        upper = sb("upper", [P, P], BF16, two)
        ones_b = sb("ones_b", [P, P], BF16, two)
        d_m = sb("d_m", [P, NT], F32, two)
        d_s = sb("d_s", [P, NT, E], F32, two)
        d_ix = sb("d_ix", [P, NT, 8], U32, two)
        d_ixf = sb("d_ixf", [P, TOPK, NT], F32, two)
        picked = sb("picked", [P, TOPK, NT, E], F32, two)
        cnt = sb("cnt", [P, NT, E], F32, two)
        cnt_b = sb("cnt_b", [P, NT, E], BF16, two)
        tot = sb("tot", [P, NT, E], F32, two)
        run = sb("run", [P, NT, E], F32, two)
        rank = sb("rank", [P, NT, E], F32, two)
        tiles_of = sb("tiles_of", [P, 4, E], F32, two)
        posf = sb("posf", [P, TOPK, NT], F32, two)
        slot_f = sb("slot_f", [P, SLOTS], F32, two)
        ones_f = sb("ones_f", [P, NT], F32, two)
        wide = sb("wide", [P, SLOTS, E], F32, two)
        two.close()

        const_ready = sem("const_ready")
        w_loaded = [sem(f"w_loaded{i}") for i in range(3)]
        bias_loaded = sem("bias_loaded")
        bias_ready = sem("bias_ready")
        x_loaded = sem("x_loaded")
        cx_loaded = sem("cx_loaded")
        full = {b: sem(f"full_{b}") for b in sorted(set(BANK_OF.values()))}
        drained = {b: sem(f"drained_{b}") for b in full}
        xn_ready = sem("xn_ready")
        xbo_ready = sem("xbo_ready")
        stat_ready = sem("stat_ready")
        rstd_ready = sem("rstd_ready")
        shifted = sem("shifted")
        exp_ready = sem("exp_ready")
        pr_ready = sem("pr_ready")
        spread_ready = sem("spread_ready")
        silu_ready = sem("silu_ready")
        z_ready = sem("z_ready")
        z_stored = sem("z_stored")
        base_stored = sem("base_stored")
        dve_own = sem("dve_own")
        pool_own = sem("pool_own")

        def wait_full(eng, step, block):
            eng.wait_ge(full[BANK_OF[step]], earlier_fills(step, block) + 1)

        def wait_free(eng, step, block):
            n = earlier_fills(step, block)
            if not (isinstance(n, int) and n == 0):
                eng.wait_ge(drained[BANK_OF[step]], n)

        def wait_drained(eng, step, block):
            eng.wait_ge(drained[BANK_OF[step]], earlier_fills(step, block) + 1)

        waits_met = sem("waits_met")

        def settle(eng):
            eng.sem_inc(waits_met, 1)

        w2_loaded = sem("w2_loaded")
        const2_ready = sem("const2_ready")
        r_shift = sem("r_shift")
        r_exp = sem("r_exp")
        r_cnt = sem("r_cnt")
        r_rank = sem("r_rank")
        r_pos = sem("r_pos")
        zero_stored = sem("zero_stored")
        ids_scattered = [sem(f"ids_scattered{b}") for b in range(STAGES)]
        ids_loaded = sem("ids_loaded")
        ids_float, ids_turned = sem("ids_float"), sem("ids_turned")
        g_ix = sem("g_ix")
        g_loaded = [sem("g_loaded0"), sem("g_loaded1")]
        t_full, t_out = sem("t_full"), sem("t_out")
        g_full, g_silu, g_out = sem("g_full"), sem("g_silu"), sem("g_out")
        a_full, a_out = sem("a_full"), sem("a_out")
        d_full, d_out = sem("d_full"), sem("d_out")
        y_stored = [sem("y_stored0"), sem("y_stored1")]
        c_loaded = [sem("c_loaded0"), sem("c_loaded1")]
        cb_loaded = [sem("cb_loaded0"), sem("cb_loaded1")]
        c_done = sem("c_done")
        out_stored = [sem("out_stored0"), sem("out_stored1")]
        bo_loaded = sem("bo_loaded")

        block = whole.enter_context(nc.Block())

        x_v = x.rearrange("(n s p) d -> n p s d", p=P, s=SUB)
        cx_v = ctx_t.rearrange("(c p) t -> p c t", p=P)

        def rows(dram_ap, i):
            return dram_ap[bass.ds(i * BT, BT), :].rearrange("(s p) d -> p s d", p=P)

        @block.sync
        def _(sp):
            def load_x(i):
                sp.dma_start(x_sb[:, :, :], rows(x, i)).then_inc(x_loaded, 16)

            def load_cx(i):
                sp.dma_start(cx_t[:, :, :], cx_v[:, :, bass.ds(i * BT, BT)]).then_inc(cx_loaded, 16)

            load_x(0)
            for w, src in ((wq, wq_t), (wk, wk_t), (wv, wv_t)):
                sp.dma_start(w[:, :, :], src.rearrange("(c p) n -> p c n", p=P)).then_inc(w_loaded[0], 16)
                if w is wq:
                    load_cx(0)
            sp.dma_start(wo[:, :, :], wo_t.rearrange("(c p) n -> p c n", p=P)).then_inc(w_loaded[1], 16)
            sp.dma_start(wgate[:, :, :], wgate_t.rearrange("(c p) n -> p c n", p=P)).then_inc(w_loaded[1], 16)
            sp.dma_start(wsgu[:, :, :], wsgu_t.rearrange("(c p) n -> p c n", p=P)).then_inc(w_loaded[2], 16)
            whole_ch = FS // P
            sp.dma_start(wsdn[:, 0:whole_ch, :], wsdn_t[0:whole_ch * P, :].rearrange("(c p) n -> p c n", p=P)).then_inc(w_loaded[2], 16)
            sp.dma_start(wsdn[0:FS - whole_ch * P, whole_ch, :], wsdn_t[whole_ch * P:FS, :]).then_inc(w_loaded[2], 16)

            def body(i, more, ffn):
                if more:
                    sp.wait_ge(xbo_ready, i + 1)
                    sp.wait_ge(xn_ready, i * SUB + SUB)
                    load_x(i + 1)
                    wait_full(sp, "V1", i)
                    settle(sp)
                    load_cx(i + 1)
                if ffn:
                    wait_drained(sp, "D1", i)
                    settle(sp)
                    sp.dma_start(rows(base_d, i - 1), base[:, :, :]).then_inc(base_stored, 16)
                sp.wait_ge(z_ready, i * SUB + SUB)
                settle(sp)
                sp.dma_start(rows(z_d, i), z[:, :, :]).then_inc(z_stored, 16)

            body(0, True, False)
            with sp.Fori(1, NB - 1) as i:
                body(i, True, True)
            body(NB - 1, False, True)
            wait_drained(sp, "D1", NB)
            wait_drained(sp, "D0", NB)
            sp.dma_start(rows(base_d, NB - 1), base[:, :, :]).then_inc(base_stored, 16)
            sp.wait_ge(base_stored, 16 * NB)
            sp.wait_ge(z_stored, 16 * NB)

            sp.dma_start(wgu[:, :, :], wgu_t.rearrange("(c p) e n -> p c (e n)", p=P)).then_inc(w2_loaded, 16)
            for f, (f0, fn) in enumerate(F_CH):
                sp.dma_start(wdn[0:fn, f, :], wdn_t[f0:f0 + fn].rearrange("p e n -> p (e n)")).then_inc(w2_loaded, 16)
            sp.wait_ge(const2_ready, 1)
            sp.dma_start(token_d.rearrange("(j p) o -> j (p o)", p=P), zero_id[:, :]).then_inc(zero_stored, 16)
            for b in range(STAGES):
                sp.wait_ge(ids_scattered[b], 16 * TOPK * NT // STAGES)
            sp.dma_start(zero_id[:, :], token_d.rearrange("(j p) o -> j (p o)", p=P)).then_inc(ids_loaded, 16)
            with sp.Fori(0, SLOTS // 2) as k:
                for b in range(2):
                    j = k * 2 + b
                    sp.wait_ge(d_out, j + 1)
                    settle(sp)
                    sp.dma_start(y_d[bass.ds(j * P, P), :], y_sb[:, b, :]).then_inc(y_stored[b], 16)
            with sp.Fori(0, NT // 2) as k:
                for b in range(2):
                    n = k * 2 + b
                    sp.wait_ge(c_done, n + 1)
                    settle(sp)
                    sp.dma_start(out[bass.ds(n * P, P), :], comb_out[:, b, :]).then_inc(out_stored[b], 16)
            for b in range(2):
                sp.wait_ge(out_stored[b], 16 * (NT // 2))

        @block.tensor
        def _(pe):
            def mm(o, l, r, start, stop):
                return nc.tensor.matmul(o, l, r, start=start, stop=stop)

            def project(name, w, src, part, i):
                for b in range(2):
                    step = f"{name}{b}"
                    o = bank_ap(step)
                    wait_free(pe, step, i)
                    for c2 in range(2):
                        c = 2 * b + c2
                        oc = o[:, c2 * BT:(c2 + 1) * BT]
                        mm(oc, bias3[:, part * D + c * P:part * D + (c + 1) * P], ones3[:, :], True, False)
                        for kc in range(KC):
                            last = mm(oc, w[:, kc, c * P:(c + 1) * P], src[:, kc, :], False, kc == KC - 1)
                    last.then_inc(full[BANK_OF[step]], 1)

            def attn_head(i):
                for s in range(SUB):
                    step = f"X{s}"
                    wait_free(pe, step, i)
                    pe.wait_ge(xn_ready, i * SUB + s + 1)
                    for kc in range(KC):
                        last = nc.tensor.transpose(bank_ap(step)[:, kc * P:(kc + 1) * P], xn[:, s, kc * P:(kc + 1) * P], ident[:, :])
                    last.then_inc(full[BANK_OF[step]], 1)
                wait_drained(pe, "X0", i)
                wait_drained(pe, "X1", i)
                project("Q", wq, xn_t, 0, i)
                pe.wait_ge(cx_loaded, i * 16 + 16)
                project("K", wk, cx_t, 1, i)
                project("V", wv, cx_t, 2, i)

            def ffn_open(i):
                for s in range(SUB):
                    step = f"Z{s}"
                    wait_free(pe, step, i)
                    pe.wait_ge(z_ready, (i - 1) * SUB + (s + 1))
                    for kc in range(KC):
                        last = nc.tensor.transpose(bank_ap(step)[:, kc * P:(kc + 1) * P], z[:, s, kc * P:(kc + 1) * P], ident[:, :])
                    last.then_inc(full[BANK_OF[step]], 1)
                wait_free(pe, "L", i)
                wait_drained(pe, "Z0", i)
                wait_drained(pe, "Z1", i)
                for s in range(SUB):
                    for kc in range(KC):
                        last = mm(bank_ap("L")[:, s * E:(s + 1) * E], z_t[:, kc, s * P:(s + 1) * P], wgate[:, kc, :], kc == 0, kc == KC - 1)
                last.then_inc(full[BANK_OF["L"]], 1)

            def gate_up(f, i):
                step = f"G{f}"
                f0, fn = FS_CH[f]
                wait_free(pe, step, i)
                for half in range(2):
                    for kc in range(KC):
                        last = mm(bank_ap(step)[0:fn, half * BT:(half + 1) * BT], wsgu[:, kc, half * FS + f0:half * FS + f0 + fn],
                                  z_t[:, kc, :], kc == 0, kc == KC - 1)
                last.then_inc(full[BANK_OF[step]], 1)

            def scores(s, i):
                for u in range(NU):
                    step = f"S{s}{u}"
                    o = bank_ap(step)
                    wait_free(pe, step, i)
                    mm(o, onehot[:, :], other[:, :, :], True, False)
                    for g in range(UG):
                        t0 = s * P + (u * UG + g) * GT
                        last = mm(o[:, g * P:(g + 1) * P], q_t[:, t0:t0 + GT, :], k_t[:, t0:t0 + GT, :], False, g == UG - 1)
                    last.then_inc(full[BANK_OF[step]], 1)

            def v_pairs(i):
                for s in range(SUB):
                    step = f"VT{s}"
                    wait_free(pe, step, i)
                    settle(pe)
                    for g in range(NG):
                        t0 = s * P + g * GT
                        last = nc.tensor.transpose(bank_ap(step)[:, g * HD:(g + 1) * HD], v_t[:, t0:t0 + GT, :], ident[0:HD, 0:HD])
                    last.then_inc(full[BANK_OF[step]], 1)

            def transpose_weights(s, i):
                for u in range(NU):
                    step = f"T{s}{u}"
                    wait_free(pe, step, i)
                    pe.wait_ge(spread_ready, i * (SUB * NU) + (s * NU + u + 1))
                    for g in range(UG):
                        last = nc.tensor.transpose(bank_ap(step)[:, g * P:(g + 1) * P], spread[:, s, u * UG + g, :], ident[:, :])
                    last.then_inc(full[BANK_OF[step]], 1)

            def attend(s, i):
                step = f"P{s}"
                wait_free(pe, step, i)
                if s == 0:
                    for u in range(NU):
                        wait_drained(pe, f"T1{u}", i)
                    wait_drained(pe, "VT0", i)
                    wait_drained(pe, "VT1", i)
                for g in range(NG):
                    last = mm(psum_a[0:HD, g * P:(g + 1) * P], v_p[:, s * NG + g, :], spread_t[:, s, g * P:(g + 1) * P], True, True)
                last.then_inc(full["A0"], 1)

            def down(s, i):
                step = f"D{s}"
                wait_free(pe, step, i)
                for f, (f0, fn) in enumerate(FS_CH):
                    last = mm(bank_ap(step), sh_t[0:fn, f, s * P:(s + 1) * P], wsdn[0:fn, f, :], f == 0, f == len(FS_CH) - 1)
                last.then_inc(full[BANK_OF[step]], 1)

            def project_out(s, i):
                step = f"O{s}"
                wait_free(pe, step, i)
                wait_drained(pe, f"P{s}", i)
                for kc in range(KC):
                    last = mm(bank_ap(step), at_t[:, kc, s * P:(s + 1) * P], wo[:, kc, :], kc == 0, kc == KC - 1)
                last.then_inc(full[BANK_OF[step]], 1)

            def body(i, ffn):
                attn_head(i)
                if ffn:
                    ffn_open(i)
                    for f in range(3):
                        gate_up(f, i)
                wait_drained(pe, "Q0", i)
                wait_drained(pe, "Q1", i)
                wait_drained(pe, "K0", i)
                wait_drained(pe, "K1", i)
                scores(0, i)
                if ffn:
                    gate_up(3, i)
                scores(1, i)
                if ffn:
                    gate_up(4, i)
                    gate_up(5, i)
                wait_drained(pe, "V0", i)
                wait_drained(pe, "V1", i)
                v_pairs(i)
                transpose_weights(0, i)
                transpose_weights(1, i)
                attend(0, i)
                if ffn:
                    for f in range(6):
                        wait_drained(pe, f"G{f}", i)
                    down(0, i)
                attend(1, i)
                if ffn:
                    down(1, i)
                project_out(0, i)
                project_out(1, i)

            pe.wait_ge(const_ready, 1)
            pe.wait_ge(bias_ready, 1)
            pe.wait_ge(w_loaded[0], 48)
            pe.wait_ge(w_loaded[1], 32)
            body(0, False)
            pe.wait_ge(w_loaded[2], 48)
            with pe.Fori(1, NB) as i:
                body(i, True)
            ffn_open(NB)
            for f in range(6):
                gate_up(f, NB)
            for f in range(6):
                wait_drained(pe, f"G{f}", NB)
            down(0, NB)
            down(1, NB)

            pe.wait_ge(r_cnt, 1)
            pe.wait_ge(const2_ready, 1)
            flat = cnt_b[:, :, :].rearrange("p n e -> p (n e)")
            mm(psum_a[:, 0:NT * E], upper[:, :], flat, True, True)
            mm(psum_a[:, BANK:BANK + NT * E], ones_b[:, :], flat, True, True).then_inc(r_rank, 1)

            t_bank, a_bank, d_bank = psum_b[0], psum_b[1], psum_b[2]

            def g_bank(b, half):
                return psum_a[:, (2 * b + half) * BANK:(2 * b + half) * BANK + F]

            def turn_rows(j, b, k):
                pe.wait_ge(g_loaded[b], k * 16 + 16)
                if not (isinstance(j, int) and j == 0):
                    pe.wait_ge(t_out, j)
                for kc in range(KC):
                    last = nc.tensor.transpose(t_bank[:, kc * P:(kc + 1) * P], zg[:, b, kc * P:(kc + 1) * P], ident[:, :])
                last.then_inc(t_full, 1)

            def open_expert(j, b):
                e = pe.value_load(slot_expert[0:1, bass.ds(j, 1)], min_val=0, max_val=E - 1)
                pe.wait_ge(t_out, j + 1)
                if not (isinstance(j, int) and j < 2):
                    pe.wait_ge(g_out, j - 1)
                for half in range(2):
                    for kc in range(KC):
                        last = mm(g_bank(b, half), zg_t[:, b, kc * P:(kc + 1) * P], wgu[:, kc, bass.ds(e * (2 * F) + half * F, F)],
                                  kc == 0, kc == KC - 1)
                last.then_inc(g_full, 1)
                return e

            def turn_act(j, b):
                pe.wait_ge(g_out, j + 1)
                if not (isinstance(j, int) and j == 0):
                    pe.wait_ge(a_out, j)
                for f, (f0, fn) in enumerate(F_CH):
                    last = nc.tensor.transpose(a_bank[0:fn, f * P:(f + 1) * P], act_g[:, b, f0:f0 + fn], ident[:, :])
                last.then_inc(a_full, 1)

            def close_expert(j, b):
                e = pe.value_load(slot_expert[0:1, bass.ds(j, 1)], min_val=0, max_val=E - 1)
                pe.wait_ge(a_out, j + 1)
                if not (isinstance(j, int) and j == 0):
                    pe.wait_ge(d_out, j)
                for f, (f0, fn) in enumerate(F_CH):
                    last = mm(d_bank[:, :], act_t[0:fn, b, f * P:(f + 1) * P], wdn[0:fn, f, bass.ds(e * D, D)],
                              f == 0, f == len(F_CH) - 1)
                last.then_inc(d_full, 1)

            pe.wait_ge(ids_float, 1)
            nc.tensor.transpose(psum_b[3][:, 0:SLOTS], id_rows[:, :], ident[0:SLOTS, 0:SLOTS]).then_inc(ids_turned, 1)
            pe.wait_ge(w2_loaded, 16 * (1 + len(F_CH)))
            pe.wait_ge(r_pos, 1)
            turn_rows(0, 0, 0)
            open_expert(0, 0)
            turn_rows(1, 1, 0)
            turn_act(0, 0)
            open_expert(1, 1)
            turn_rows(2, 0, 1)
            close_expert(0, 0)
            turn_act(1, 1)
            with pe.Fori(1, SLOTS // 2 - 1) as k:
                for b in range(2):
                    j = k * 2 + b
                    open_expert(j, b)
                    turn_rows(j + 1, 1 - b, k + b)
                    close_expert(j - 1, 1 - b)
                    turn_act(j, b)
            j = SLOTS - 2
            open_expert(j, 0)
            turn_rows(j + 1, 1, SLOTS // 2 - 1)
            close_expert(j - 1, 1)
            turn_act(j, 0)
            open_expert(j + 1, 1)
            close_expert(j, 0)
            turn_act(j + 1, 1)
            close_expert(j + 1, 1)

        @block.scalar
        def _(act):
            def copy(o, i_):
                return nc.scalar.activation(o, i_, ACT.Copy)

            def heads_out(step, dst, b):
                view = dst[:, :, :].rearrange("p t (b c l) -> p b l c t", b=2, c=2)
                for l in range(4):
                    last = copy(view[:, b, l], bank_ap(step)[HD * l:HD * (l + 1), :].rearrange("p (c t) -> p c t", c=2))
                last.then_inc(drained[BANK_OF[step]], 1)

            def silus(i, fs):
                for f in fs:
                    fn = FS_CH[f][1]
                    wait_full(act, f"G{f}", i)
                    if f >= GB:
                        wait_drained(act, f"G{f - GB}", i)
                    nc.scalar.activation(gate_act[0:fn, f % GB, :], bank_ap(f"G{f}")[0:fn, 0:BT], ACT.Silu).then_inc(silu_ready, 1)

            def z_out(i):
                if not (isinstance(i, int) and i == 1):
                    act.wait_ge(base_stored, (i - 1) * 16)
                for s in range(SUB):
                    wait_full(act, f"Z{s}", i)
                    copy(z_t[:, :, s * P:(s + 1) * P], bank_ap(f"Z{s}").rearrange("p (c t) -> p c t", c=KC)).then_inc(drained[BANK_OF[f"Z{s}"]], 1)

            def body(i, ffn):
                for s in range(SUB):
                    wait_full(act, f"X{s}", i)
                    copy(xn_t[:, :, s * P:(s + 1) * P], bank_ap(f"X{s}").rearrange("p (c t) -> p c t", c=KC)).then_inc(drained[BANK_OF[f"X{s}"]], 1)
                for step, dst, b in (("K0", k_t, 0), ("K1", k_t, 1), ("V1", v_t, 1)):
                    wait_full(act, step, i)
                    heads_out(step, dst, b)
                if ffn:
                    z_out(i)
                    silus(i, range(4))
                for s in range(SUB):
                    act.wait_ge(shifted, i * SUB + (s + 1))
                    nc.scalar.activation(ex[:, s], sc[:, s], ACT.Exp).then_inc(exp_ready, 1)
                if ffn:
                    silus(i, range(4, 6))
                for s in range(SUB):
                    wait_full(act, f"VT{s}", i)
                    copy(v_p[:, s * NG:(s + 1) * NG, :], bank_ap(f"VT{s}").rearrange("p (g d) -> p g d", d=HD)).then_inc(drained[BANK_OF[f"VT{s}"]], 1)
                for s in range(SUB):
                    for u in range(NU):
                        step = f"T{s}{u}"
                        wait_full(act, step, i)
                        copy(spread_t[:, s, u * BANK:(u + 1) * BANK], bank_ap(step)).then_inc(drained[BANK_OF[step]], 1)
                wait_full(act, "P1", i)
                view = psum_a[0:HD, :].rearrange("p (t c l) -> p l c t", c=KC, l=4)
                for l in range(4):
                    last = copy(at_t[HD * l:HD * (l + 1), :, P:2 * P], view[:, l])
                last.then_inc(drained["A0"], 1)

            body(0, False)
            with act.Fori(1, NB) as i:
                body(i, True)
            z_out(NB)
            silus(NB, range(6))
            act.wait_ge(r_shift, 1)
            nc.scalar.activation(d_s[:, :, :], d_s[:, :, :], ACT.Exp).then_inc(r_exp, 1)

            a_bank, d_bank = psum_b[1], psum_b[2]

            def step(j, b, k):
                act.wait_ge(g_full, j + 1)
                nc.scalar.activation(silu[:, b, :], psum_a[:, 2 * b * BANK:2 * b * BANK + F], ACT.Silu).then_inc(g_silu, 1)
                if not (isinstance(j, int) and j == 0):
                    rows_out(j - 1, 1 - b, k - 1 + b)
                act.wait_ge(a_full, j + 1)
                copy(act_t[:, b, 0:2 * P], a_bank[:, 0:2 * P])
                copy(act_t[0:F_CH[2][1], b, 2 * P:3 * P], a_bank[0:F_CH[2][1], 2 * P:3 * P]).then_inc(a_out, 1)

            def rows_out(j, b, k):
                act.wait_ge(d_full, j + 1)
                if not (isinstance(j, int) and j < 2):
                    act.wait_ge(y_stored[b], k * 16)
                copy(y_sb[:, b, :], d_bank[:, :]).then_inc(d_out, 1)

            for j in range(4):
                step(j, j % 2, j // 2)
            with act.Fori(2, SLOTS // 2) as k:
                for b in range(2):
                    step(k * 2 + b, b, k)
            rows_out(SLOTS - 1, 1, SLOTS // 2 - 1)

            def load_base(n, b):
                if not (isinstance(n, int) and n < 2):
                    act.wait_ge(c_done, n - 1)
                act.dma_start(comb[2][:, b, :], base_d[bass.ds(n * P, P), :]).then_inc(cb_loaded[b], 16)

            load_base(0, 0)
            load_base(1, 1)
            with act.Fori(1, NT // 2) as k:
                for b in range(2):
                    load_base(k * 2 + b, b)

        @block.vector
        def _(dve):
            own_ = Chain(dve, dve_own)
            link, mark = own_.link, own_.mark
            V = nc.vector

            dve.wait_ge(bias_loaded, 16 * 9)
            dve.wait_ge(const_ready, 1)
            link(V.tensor_copy(b_bf, b_raw))
            link(V.tensor_copy(b_part[0], b_bf))
            link(V.tensor_tensor(b_rest, b_raw, b_part[0], ALU.subtract))
            link(V.tensor_copy(b_bf, b_rest))
            link(V.tensor_copy(b_part[1], b_bf))
            link(V.tensor_tensor(b_part[2], b_rest, b_part[1], ALU.subtract))
            link(V.tensor_scalar(b_raw, b_part[0], ident[0:3, 0:1], None, ALU.mult))
            link(V.scalar_tensor_tensor(out=b_rest, in0=b_part[1], scalar=ident[0:3, 1:2], in1=b_raw, op0=ALU.mult, op1=ALU.add))
            link(V.scalar_tensor_tensor(out=b_raw, in0=b_part[2], scalar=ident[0:3, 2:3], in1=b_rest, op0=ALU.mult, op1=ALU.add))
            V.tensor_copy(bias3[0:3, :], b_raw).then_inc(bias_ready, 1)

            def normalise_x(i, first):
                dve.wait_ge(x_loaded, i * 16 + 16)
                for s in range(SUB):
                    mark(V.bn_stats(stats[:, s, :], x_sb[:, s, :]))
                own_.wait()
                for s in range(SUB):
                    settle(dve)
                    V.bn_aggr(mv[:, s, :], stats[:, s, :]).then_inc(stat_ready, 1)
                for s in range(SUB):
                    dve.wait_ge(rstd_ready, i * (2 * SUB) + (s + 1))
                    V.tensor_scalar(xn[:, s, :], x_sb[:, s, :], mv[:, s, 0:1], rstd[:, s:s + 1], ALU.subtract, ALU.mult).then_inc(xn_ready, 1)

            def heads_out(step, dst, b):
                view = dst[:, :, :].rearrange("p t (b c l) -> p b l c t", b=2, c=2)
                for l in range(4):
                    last = V.tensor_copy(view[:, b, l], bank_ap(step)[HD * l:HD * (l + 1), :].rearrange("p (c t) -> p c t", c=2))
                last.then_inc(drained[BANK_OF[step]], 1)

            def gate_times_up(i, f, i_ffn):
                fn = FS_CH[f][1]
                dve.wait_ge(silu_ready, i_ffn * 6 + (f + 1))
                V.tensor_tensor(sh_t[0:fn, f, :], gate_act[0:fn, f % GB, :], bank_ap(f"G{f}")[0:fn, BT:2 * BT], ALU.mult).then_inc(drained[BANK_OF[f"G{f}"]], 1)

            def own_scores(i, s):
                for u in range(NU):
                    step = f"S{s}{u}"
                    wait_full(dve, step, i)
                    ins = V.tensor_reduce(out=sc[:, s, u * UG:(u + 1) * UG, :],
                                          in_=bank_ap(step).rearrange("p (r t g) -> p r g t", r=UG, t=GT), axis=X, op=ALU.max)
                    ins.then_inc(drained[BANK_OF[step]], 1)
                for u in range(NU):
                    wait_drained(dve, f"S{s}{u}", i)
                link(V.tensor_reduce(out=row_max[:, s, :], in_=sc[:, s], axis=X, op=ALU.max))
                V.tensor_tensor(sc[:, s], sc[:, s], row_max[:, s, :].unsqueeze(2).broadcast_to([P, NG, H]), ALU.subtract).then_inc(shifted, 1)

            def softmax(i, s):
                dve.wait_ge(exp_ready, i * SUB + (s + 1))
                link(V.tensor_reduce(out=row_sum[:, s, :], in_=ex[:, s], axis=X, op=ALU.add))
                link(V.reciprocal(row_inv[:, s, :], row_sum[:, s, :]))
                V.tensor_tensor(pr[:, s], ex[:, s], row_inv[:, s, :].unsqueeze(2).broadcast_to([P, NG, H]), ALU.mult).then_inc(pr_ready, 1)

            def logits_out(i, i_ffn):
                wait_full(dve, "L", i)
                V.tensor_copy(tok_scores[:, bass.ds(i_ffn * SUB, SUB), :], bank_ap("L")[:, 0:SUB * E].rearrange("p (s e) -> p s e", s=SUB)).then_inc(drained[BANK_OF["L"]], 1)

            def add_shared(i, s, i_ffn):
                wait_full(dve, f"D{s}", i)
                V.tensor_tensor(base[:, s, :], bank_ap(f"D{s}"), x1[:, s, :], ALU.add).then_inc(drained[BANK_OF[f"D{s}"]], 1)

            def body(i, ffn, more):
                i_ffn = i - 1
                for step, dst, b in (("Q0", q_t, 0), ("Q1", q_t, 1), ("V0", v_t, 0)):
                    wait_full(dve, step, i)
                    heads_out(step, dst, b)
                if ffn:
                    logits_out(i, i_ffn)
                    for f in range(3):
                        gate_times_up(i, f, i_ffn)
                own_scores(i, 0)
                if ffn:
                    gate_times_up(i, 3, i_ffn)
                own_scores(i, 1)
                softmax(i, 0)
                softmax(i, 1)
                if ffn:
                    gate_times_up(i, 4, i_ffn)
                    gate_times_up(i, 5, i_ffn)
                wait_full(dve, "P0", i)
                view = psum_a[0:HD, :].rearrange("p (t c l) -> p l c t", c=KC, l=4)
                for l in range(4):
                    last = V.tensor_copy(at_t[HD * l:HD * (l + 1), :, 0:P], view[:, l])
                last.then_inc(drained["A0"], 1)
                if ffn:
                    add_shared(i, 0, i_ffn)
                    add_shared(i, 1, i_ffn)
                for s in range(SUB):
                    wait_full(dve, f"O{s}", i)
                    if ffn:
                        wait_drained(dve, f"D{s}", i)
                    dve.wait_ge(xbo_ready, i + 1)
                    V.tensor_tensor(x1[:, s, :], bank_ap(f"O{s}"), xbo[:, s, :], ALU.add).then_inc(drained[BANK_OF[f"O{s}"]], 1)
                    wait_drained(dve, f"O{s}", i)
                    link(V.bn_stats(stats[:, SUB + s, :], x1[:, s, :]))
                    settle(dve)
                    V.bn_aggr(mv[:, SUB + s, :], stats[:, SUB + s, :]).then_inc(stat_ready, 1)
                if not (isinstance(i, int) and i == 0):
                    dve.wait_ge(z_stored, i * 16)
                for s in range(SUB):
                    dve.wait_ge(rstd_ready, i * (2 * SUB) + (SUB + s + 1))
                    V.tensor_scalar(z[:, s, :], x1[:, s, :], mv[:, SUB + s, 0:1], rstd[:, SUB + s:SUB + s + 1], ALU.subtract, ALU.mult).then_inc(z_ready, 1)
                if more:
                    normalise_x(i + 1, False)

            normalise_x(0, True)
            body(0, False, True)
            DVE_SIGNALS = 10
            with dve.Fori(1, NB - 1) as i:
                own_.enter(i - 1, DVE_SIGNALS)
                body(i, True, True)
            own_.leave(NB - 2)
            body(NB - 1, True, False)
            logits_out(NB, NB - 1)
            for f in range(6):
                gate_times_up(NB, f, NB - 1)
            add_shared(NB, 0, NB - 1)
            add_shared(NB, 1, NB - 1)
            for step in ("L", "D0", "D1"):
                wait_drained(dve, step, NB)
            dve.wait_ge(z_stored, 16 * NB)
            dve.wait_ge(base_stored, 16 * NB)
            link(V.tensor_reduce(out=d_m[:, :], in_=tok_scores[:, :, :], axis=X, op=ALU.max))
            V.tensor_tensor(d_s[:, :, :], tok_scores[:, :, :], d_m[:, :].unsqueeze(2).broadcast_to([P, NT, E]), ALU.subtract).then_inc(r_shift, 1)
            dve.wait_ge(r_exp, 1)
            mark(V.memset(ones_f[:, :], 1.0))
            dve.wait_ge(const2_ready, 1)
            link(V.tensor_reduce(out=d_m[:, :], in_=d_s[:, :, :], axis=X, op=ALU.add))
            link(V.reciprocal(d_m[:, :], d_m[:, :]))
            link(V.tensor_tensor(d_s[:, :, :], d_s[:, :, :], d_m[:, :].unsqueeze(2).broadcast_to([P, NT, E]), ALU.mult))
            for n in range(NT):
                mark(V.max(top_w[:, n, :], d_s[:, n, :]))
            own_.wait()
            for n in range(NT):
                mark(V.max_index(d_ix[:, n, :], top_w[:, n, :], d_s[:, n, :]))
            own_.wait()
            link(V.tensor_copy(d_ixf[:, :, :], d_ix[:, :, 0:TOPK].rearrange("p n k -> p k n")))
            for k in range(TOPK):
                mark(V.tensor_tensor(picked[:, k], d_ixf[:, k, :].unsqueeze(2).broadcast_to([P, NT, E]),
                                     iota_e[:, :].unsqueeze(1).broadcast_to([P, NT, E]), ALU.is_equal))
            own_.wait()
            V.tensor_tensor(cnt_b[:, :, :], picked[:, 0], picked[:, 1], ALU.add).then_inc(r_cnt, 1)
            dve.wait_ge(r_rank, 1)
            mark(V.tensor_copy(rank[:, :, :], psum_a[:, 0:NT * E].rearrange("p (n e) -> p n e", e=E)))
            link(V.tensor_copy(tot[:, :, :], psum_a[:, BANK:BANK + NT * E].rearrange("p (n e) -> p n e", e=E)))
            for e in range(E):
                mark(V.tensor_tensor_scan(out=run[:, :, e], data0=ones_f[:, :], data1=tot[:, :, e], initial=0.0, op0=ALU.mult, op1=ALU.add))
            own_.wait()
            link(V.tensor_tensor(wide[:, 0:NT, :], run[:, NT - 1, :].unsqueeze(1).broadcast_to([P, NT, E]),
                                 iota_rows[:, :].unsqueeze(2).broadcast_to([P, NT, E]), ALU.is_gt))
            link(V.tensor_reduce(out=tiles_of[:, 0, :], in_=wide[:, 0:NT, :].rearrange("p n e -> p e n"), axis=X, op=ALU.add))
            link(V.tensor_tensor_scan(out=tiles_of[:, 1, :], data0=ones_f[:, 0:E], data1=tiles_of[:, 0, :], initial=0.0, op0=ALU.mult, op1=ALU.add))
            link(V.tensor_tensor(tiles_of[:, 2, :], tiles_of[:, 1, :], tiles_of[:, 0, :], ALU.subtract))
            link(V.tensor_scalar(tiles_of[:, 3, :], tiles_of[:, 2, :], float(P), None, ALU.mult))
            link(V.tensor_tensor(wide[:, :, 0:E - 1], tiles_of[:, 2, 1:E].unsqueeze(1).broadcast_to([P, SLOTS, E - 1]),
                                 iota_slot[:, :].unsqueeze(2).broadcast_to([P, SLOTS, E - 1]), ALU.is_le))
            link(V.tensor_reduce(out=slot_f[:, :], in_=wide[:, :, 0:E - 1], axis=X, op=ALU.add))
            mark(V.tensor_copy(slot_expert[:, :], slot_f[:, :]))
            link(V.tensor_tensor(rank[:, :, :], rank[:, :, :], run[:, :, :], ALU.add))
            link(V.tensor_tensor(rank[:, :, :], rank[:, :, :], tot[:, :, :], ALU.subtract))
            link(V.tensor_tensor(rank[:, :, :], rank[:, :, :], tiles_of[:, 3, :].unsqueeze(1).broadcast_to([P, NT, E]), ALU.add))
            for k in range(TOPK):
                link(V.tensor_tensor(picked[:, k], picked[:, k], rank[:, :, :], ALU.mult))
                link(V.tensor_reduce(out=posf[:, k, :], in_=picked[:, k], axis=X, op=ALU.add))
            V.tensor_copy(pos[:, :, :], posf[:, :, :]).then_inc(r_pos, 1)

            t_bank = psum_b[0]
            dve.wait_ge(ids_loaded, 16)
            V.tensor_copy(id_rows[:, :], zero_id[:, :]).then_inc(ids_float, 1)
            dve.wait_ge(ids_turned, 1)
            link(V.tensor_copy(ids_col[:, :], psum_b[3][:, 0:SLOTS]))

            def index_out(j, b, k):
                if not (isinstance(j, int) and j < 2):
                    dve.wait_ge(g_loaded[b], k * 16)
                V.tensor_copy(gather_ix[:, b:b + 1], ids_col[:, bass.ds(j, 1)]).then_inc(g_ix, 1)

            def rows_turned(j, b):
                dve.wait_ge(t_full, j + 1)
                V.tensor_copy(zg_t[:, b, :], t_bank[:, :]).then_inc(t_out, 1)

            def gated(j, b):
                dve.wait_ge(g_silu, j + 1)
                V.tensor_tensor(act_g[:, b, :], silu[:, b, :], psum_a[:, (2 * b + 1) * BANK:(2 * b + 1) * BANK + F], ALU.mult).then_inc(g_out, 1)

            index_out(0, 0, 0)
            index_out(1, 1, 0)
            rows_turned(0, 0)
            for j in range(2):
                index_out(j + 2, j, 1)
                rows_turned(j + 1, 1 - j)
                gated(j, j)
            with dve.Fori(1, SLOTS // 2 - 1) as k:
                for b in range(2):
                    j = k * 2 + b
                    index_out(j + 2, b, k + 1)
                    rows_turned(j + 1, 1 - b)
                    gated(j, b)
            rows_turned(SLOTS - 1, 1)
            gated(SLOTS - 2, 0)
            gated(SLOTS - 1, 1)

            def combine(n, b, k):
                dve.wait_ge(cb_loaded[b], k * 16 + 16)
                dve.wait_ge(c_loaded[b], k * 32 + 32)
                link(V.scalar_tensor_tensor(out=comb[2][:, b, :], in0=comb[0][:, b, :], scalar=top_w[:, bass.ds(n, 1), 0],
                                            in1=comb[2][:, b, :], op0=ALU.mult, op1=ALU.add))
                if not (isinstance(n, int) and n < 2):
                    dve.wait_ge(out_stored[b], k * 16)
                V.scalar_tensor_tensor(out=comb_out[:, b, :], in0=comb[1][:, b, :], scalar=top_w[:, bass.ds(n, 1), 1],
                                       in1=comb[2][:, b, :], op0=ALU.mult, op1=ALU.add).then_inc(c_done, 1)

            combine(0, 0, 0)
            combine(1, 1, 0)
            with dve.Fori(1, NT // 2) as k:
                own_.enter(k - 1, 2)
                for b in range(2):
                    combine(k * 2 + b, b, k)
            own_.leave(NT // 2 - 1)

        @block.gpsimd
        def _(pool):
            own_ = Chain(pool, pool_own)
            link, mark = own_.link, own_.mark
            G = nc.gpsimd

            for r in range(3):
                for part, b in enumerate((bq, bk, bv)):
                    pool.dma_start(b_raw[r:r + 1, part * D:(part + 1) * D], b.rearrange("(a n) -> a n", a=1)).then_inc(bias_loaded, 16)
            pool.dma_start(bo_rows[:, :], bo.partition_broadcast(P)).then_inc(bo_loaded, 16)
            mark(G.memset(ident[:, :], 0.0))
            mark(G.memset(bias3[:, :], 0.0))
            mark(G.memset(ones3[:, :], 1.0))
            mark(G.memset(onehot[:, :], 1.0))
            mark(G.memset(other[:, :, :], 1.0))
            mark(G.memset(own[:, :], 1.0))
            mark(G.memset(neg_half[:, :], -0.5))
            own_.wait()
            mark(G.affine_select(out=ident[:, :], in_=ident[:, :], compare_op=ALU.not_equal, fill=1.0, base=0,
                                 pattern=[[-1, P]], channel_multiplier=1))
            for tile, dims in ((onehot, [[1, P]]), (other, [[0, UG], [1, P]])):
                link(G.affine_select(out=tile[:], in_=tile[:], compare_op=ALU.is_ge, fill=0.0, base=0, pattern=dims, channel_multiplier=-H))
                link(G.affine_select(out=tile[:], in_=tile[:], compare_op=ALU.is_ge, fill=0.0, base=H - 1,
                                     pattern=[[-st, n] for st, n in dims], channel_multiplier=H))
            link(G.affine_select(out=own[:, :], in_=own[:, :], compare_op=ALU.is_ge, fill=0.0, base=0, pattern=[[-H, GT]], channel_multiplier=1))
            link(G.affine_select(out=own[:, :], in_=own[:, :], compare_op=ALU.is_ge, fill=0.0, base=H - 1, pattern=[[H, GT]], channel_multiplier=-1))
            G.tensor_scalar(other[:, :, :], other[:, :, :], 1.0, -MASKED, ALU.subtract, ALU.mult).then_inc(const_ready, 1)

            def inverse_std(col, n):
                pool.wait_ge(stat_ready, n)
                settle(pool)
                link(G.tensor_scalar_add(var_eps[:, col:col + 1], mv[:, col, 1:2], EPS))
                G.tensor_tensor(rstd[:, col:col + 1], var_eps[:, col:col + 1], neg_half[:, :], ALU.pow).then_inc(rstd_ready, 1)

            def residual(i):
                pool.wait_ge(x_loaded, i * 16 + 16)
                G.tensor_tensor(xbo[:, :, :], x_sb[:, :, :], bo_rows[:, :].unsqueeze(1).broadcast_to([P, SUB, D]), ALU.add).then_inc(xbo_ready, 1)

            def body(i, more):
                for s in range(SUB):
                    pool.wait_ge(pr_ready, i * SUB + (s + 1))
                    for u in range(NU):
                        G.tensor_tensor(spread[:, s, u * UG:(u + 1) * UG, :].rearrange("p r (t g) -> p r t g", t=GT),
                                        pr[:, s, u * UG:(u + 1) * UG, :].unsqueeze(2).broadcast_to([P, UG, GT, H]),
                                        own[:, :].unsqueeze(1).unsqueeze(3).broadcast_to([P, UG, GT, H]), ALU.mult).then_inc(spread_ready, 1)
                for s in range(SUB):
                    inverse_std(SUB + s, i * (2 * SUB) + (SUB + s + 1))
                if more:
                    residual(i + 1)
                    for s in range(SUB):
                        inverse_std(s, (i + 1) * (2 * SUB) + (s + 1))

            own_.wait()
            pool.wait_ge(bo_loaded, 16)
            residual(0)
            for s in range(SUB):
                inverse_std(s, s + 1)
            body(0, True)
            POOL_SIGNALS = 2 * SUB
            with pool.Fori(1, NB - 1) as i:
                own_.enter(i - 1, POOL_SIGNALS)
                body(i, True)
            own_.leave(NB - 2)
            body(NB - 1, False)

            pool.wait_ge(base_stored, 16 * NB)
            pool.wait_ge(z_stored, 16 * NB)
            mark(G.iota(iota_e[:, :], [[1, E]], base=0, channel_multiplier=0, allow_small_or_imprecise_dtypes=True))
            mark(G.iota(iota_slot[:, :], [[1, SLOTS]], base=0, channel_multiplier=0, allow_small_or_imprecise_dtypes=True))
            mark(G.iota(iota_rows[:, :], [[P, NT]], base=0, channel_multiplier=0, allow_small_or_imprecise_dtypes=True))
            mark(G.iota(tok_id[:, :], [[P, NT]], base=0, channel_multiplier=1))
            mark(G.memset(zero_id[:, :], 0))
            mark(G.memset(ones_b[:, :], 1.0))
            link(G.memset(upper[:, :], 1.0))
            G.affine_select(out=upper[:, :], in_=upper[:, :], compare_op=ALU.is_gt, fill=0.0, base=0,
                            pattern=[[1, P]], channel_multiplier=-1).then_inc(const2_ready, 1)
            pool.wait_ge(r_pos, 1)
            pool.wait_ge(zero_stored, 16)

            def stage(n, b):
                mark(G.tensor_copy(pos_ix[:, b, :], pos[:, :, bass.ds(n, 1)].rearrange("p k o -> p (k o)")))
                link(G.tensor_copy(tok_ix[:, b:b + 1], tok_id[:, bass.ds(n, 1)]))

            def scatter(n, b, k):
                if not (isinstance(k, int) and k == 0):
                    pool.wait_ge(ids_scattered[b], k * (16 * TOPK))
                stage(n, b)
                settle(pool)
                for pick in range(TOPK):
                    pool.indirect_dma_start(out=token_d[:, :], out_offset=bass.IndirectOffsetOnAxis(ap=pos_ix[:, b, pick:pick + 1], axis=0),
                                            in_=tok_ix[:, b:b + 1], in_offset=None).then_inc(ids_scattered[b], 16)

            for b in range(STAGES):
                scatter(b, b, 0)
            with pool.Fori(1, NT // STAGES) as k:
                own_.enter(k - 1, 2 * STAGES)
                for b in range(STAGES):
                    scatter(k * STAGES + b, b, k)
            own_.leave(NT // STAGES - 1)

            def gather(j, b):
                pool.wait_ge(g_ix, j + 1)
                if not (isinstance(j, int) and j < 2):
                    pool.wait_ge(t_full, j - 1)
                settle(pool)
                pool.indirect_dma_start(out=zg[:, b, :], out_offset=None, in_=z_d[:, :],
                                        in_offset=bass.IndirectOffsetOnAxis(ap=gather_ix[:, b:b + 1], axis=0)).then_inc(g_loaded[b], 16)

            gather(0, 0)
            gather(1, 1)
            with pool.Fori(1, SLOTS // 2) as k:
                for b in range(2):
                    gather(k * 2 + b, b)

            for b in range(2):
                pool.wait_ge(y_stored[b], 16 * (SLOTS // 2))

            def fetch(n, b):
                if not (isinstance(n, int) and n < 2):
                    pool.wait_ge(c_done, n - 1)
                stage(n, b)
                settle(pool)
                for pick in range(TOPK):
                    pool.indirect_dma_start(out=comb[pick][:, b, :], out_offset=None, in_=y_d[:, :],
                                            in_offset=bass.IndirectOffsetOnAxis(ap=pos_ix[:, b, pick:pick + 1], axis=0)).then_inc(c_loaded[b], 16)

            fetch(0, 0)
            fetch(1, 1)
            with pool.Fori(1, NT // 2) as k:
                own_.enter(k - 1, 4)
                for b in range(2):
                    fetch(k * 2 + b, b)
            own_.leave(NT // 2 - 1)


_INS = ["x", "ctx_t", "wq_t", "bq", "wk_t", "bk", "wv_t", "bv", "wo_t", "bo", "wgate_t", "wgu_t", "wdn_t", "wsgu_t", "wsdn_t"]


_OUT = ((16, 256, 512), "float32")


def kernel(**inputs):
    import numpy as _np
    import concourse.bacc as _bacc
    from concourse import mybir as _mybir
    from concourse.bass_utils import run_bass_kernel_spmd as _run

    given = {k.replace("L0_xattn_", "").replace("L0_ffn_", ""): _np.asarray(v) for k, v in inputs.items()}
    arrays = {
        "x": given["x"].reshape(T, D),
        "ctx_t": given["ctx_2048"].reshape(T, D).T,
        "wq_t": given["Wq"].T, "bq": given["bq"],
        "wk_t": given["Wk"].T, "bk": given["bk"],
        "wv_t": given["Wv"].T, "bv": given["bv"],
        "wo_t": given["Wo"].T, "bo": given["bo"],
        "wgate_t": given["gate_weight"].T,
        "wgu_t": given["gate_up_weights"].transpose(2, 0, 1),
        "wdn_t": given["down_weights"].transpose(2, 0, 1),
        "wsgu_t": given["shared_gate_up"].T,
        "wsdn_t": given["shared_down"].T,
    }
    arrays = {f"in_{k}": _np.ascontiguousarray(v) for k, v in arrays.items()}
    nc = _bacc.Bacc("TRN2", target_bir_lowering=False, num_devices=1)
    args = [nc.dram_tensor(f"in_{k}", arrays[f"in_{k}"].shape, _mybir.dt.from_np(arrays[f"in_{k}"].dtype), kind="ExternalInput").ap()
            for k in _INS]
    out = nc.dram_tensor("out_rows", (T, D), _mybir.dt.from_np(_np.dtype(_OUT[1])), kind="ExternalOutput").ap()
    build(nc, *args, out)
    r = _run(nc, [arrays], core_ids=[0])
    return r.results[0]["out_rows"].reshape(_OUT[0])
```

```python
from contextlib import ExitStack

import concourse.bass as bass
from concourse import mybir

F32 = mybir.dt.float32
BF16 = mybir.dt.bfloat16
U32 = mybir.dt.uint32
I32 = mybir.dt.int32
ALU = mybir.AluOpType
ACT = mybir.ActivationFunctionType
X = mybir.AxisListType.X

P = 128
D = 512
KC = D // P
H, HD = 16, 32
T = 16 * 256
NT = T // P
SUB = 2
BT = SUB * P
NB = T // BT
GT = P // H
NG = P // GT
UG = 4
NU = NG // UG
E, F = 8, 352
FS = 704
TOPK = 2
EPS = 1e-5
BANK = 512
SLOTS = T * TOPK // P + E
SH_STEPS = 8
F_CH = [(0, 128), (128, 128), (256, 96)]
FS_CH = [(i * P, min(P, FS - i * P)) for i in range((FS + P - 1) // P)]
GB = 3
SHARED_FIRST = 12
TAIL_TILES = 6
STAGES = 4
MASKED = -(2.0 ** 120)

AHEAD = [("X0", "B0"), ("X1", "B1")]
AHEAD_KQ = [("K0", "B2"), ("K1", "B3"), ("Q0", "B0"), ("Q1", "B1")]
AHEAD_V = [("V0", "B2"), ("V1", "B3")]
BEHIND = [("Z0", "B3"), ("Z1", "B0")]
ROUTE = [("L", "B0")]
TURN_ROUTE = [("LT", "B0")]
SCORES = [(f"S{s}{u}", f"A{u}") for s in range(SUB) for u in range(NU)]
TURN_V = [("VT0", "B1"), ("VT1", "B3")]
TURN_W = [[(f"T{s}{u}", f"A{u}") for u in range(NU)] for s in range(SUB)]
FULL_PASS = (AHEAD + SCORES + AHEAD_KQ + TURN_W[0] + AHEAD_V[:1] + BEHIND + TURN_V[:1] + TURN_W[1] + TURN_V[1:] + ROUTE
             + [("P0", "A0"), AHEAD_V[1], ("P1", "A1")] + TURN_ROUTE + [("O0", "B1"), ("O1", "B2")])
BANK_OF = dict(FULL_PASS)
IS_AHEAD = {name for name, _ in AHEAD + AHEAD_KQ + AHEAD_V}
IS_BEHIND = {name for name, _ in BEHIND + ROUTE + TURN_ROUTE}


def steps_of(i):
    names = [name for name, _ in FULL_PASS]
    if i < 0:
        return [n for n in names if n in IS_AHEAD]
    if i == NB:
        return [n for n in names if n in IS_BEHIND]
    return [n for n in names if not (i == 0 and n in IS_BEHIND) and not (i == NB - 1 and n in IS_AHEAD)]


def earlier_fills(step, i):
    mine = {name for name, bank in FULL_PASS if bank == BANK_OF[step]}
    if isinstance(i, int):
        whole = sum(n in mine for p in range(-1, i) for n in steps_of(p))
        names = steps_of(i)
        return whole + sum(n in mine for n in names[:names.index(step)])
    return (i - 1) * len(mine) + earlier_fills(step, 1)


class Chain:

    def __init__(self, engine, sem):
        self.engine, self.sem, self.n, self.passes = engine, sem, 0, 0

    def enter(self, passes, per_pass):
        self.passes, self.start, self.per_pass = passes * per_pass, self.n, per_pass

    def leave(self, count):
        assert self.n - self.start == self.per_pass, (self.n - self.start, self.per_pass)
        self.n, self.passes = self.start + count * self.per_pass, 0

    def mark(self, instruction):
        self.n += 1
        return instruction.then_inc(self.sem, 1)

    def wait(self):
        self.engine.wait_ge(self.sem, self.passes + self.n)

    def link(self, instruction):
        self.mark(instruction)
        self.wait()


def build(nc, x, ctx_t, wq_t, bq, wk_t, bk, wv_t, bv, wo_t, bo, wgate_t, wgu_t, wdn_t, wsgu_t, wsdn_t, out):
    with ExitStack() as whole:
        def sem(name):
            return whole.enter_context(nc.semaphore(name))

        def dram(name, shape, dt):
            return nc.dram_tensor(name, shape, dt).ap()

        z_d = dram("z_rows", [T, D], F32)
        zt_d = dram("z_columns", [NB, P, KC, BT], F32)
        x1_d = dram("x1_rows", [T, D], F32)
        base_d = dram("base_rows", [T, D], F32)
        y_d = dram("expert_rows", [SLOTS * P, D], F32)
        token_d = dram("slot_tokens", [SLOTS * P, 1], I32)

        def sb(name, shape, dt, stack=whole):
            return stack.enter_context(nc.sbuf_tensor(name, shape, dt))

        psum_a = whole.enter_context(nc.psum_tensor("psum_a", [P, NU * BANK], F32))
        psum_b = [whole.enter_context(nc.psum_tensor(f"psum_b{i}", [P, BANK], F32)) for i in range(4)]

        def bank_ap(step):
            kind, i = BANK_OF[step][0], int(BANK_OF[step][1])
            return psum_a[:, i * BANK:(i + 1) * BANK] if kind == "A" else psum_b[i][:, :]

        ident = sb("ident", [P, P], F32)
        tok_scores = sb("tok_scores", [P, NT, E], F32)
        ids_col = sb("ids_col", [P, SLOTS], I32)
        pos = sb("pos", [P, TOPK, NT], U32)
        top_w = sb("top_w", [P, NT, 8], F32)
        slot_expert = sb("slot_expert", [P, SLOTS], I32)

        wsgu = sb("wsgu", [P, KC, 2 * FS], F32)
        wsdn = sb("wsdn", [P, len(FS_CH), D], F32)

        one = ExitStack()
        wq = sb("wq", [P, KC, D], F32, one)
        wk = sb("wk", [P, KC, D], F32, one)
        wv = sb("wv", [P, KC, D], F32, one)
        wo = sb("wo", [P, KC, D], F32, one)
        wgate = sb("wgate", [P, KC, E], F32, one)
        bias3 = sb("bias3", [P, 4 * D], BF16, one)
        ones3 = sb("ones3", [P, BT], BF16, one)
        onehot = sb("onehot", [GT, P], BF16, one)
        other = sb("other", [GT, UG, P], BF16, one)
        own = sb("own", [P, GT], F32, one)
        neg_half = sb("neg_half", [P, 1], F32, one)
        x_sb = sb("x_sb", [P, SUB, D], F32, one)
        x_res = sb("x_res", [P, SUB, D], F32, one)
        xn = sb("xn", [P, SUB, D], F32, one)
        xn_t = sb("xn_t", [P, KC, BT], F32, one)
        cx_t = sb("cx_t", [P, KC, BT], F32, one)
        q_t = sb("q_t", [HD, BT, H], F32, one)
        k_t = sb("k_t", [HD, BT, H], F32, one)
        v_t = sb("v_t", [HD, BT, H], F32, one)
        v_p = sb("v_p", [P, SUB * NG, HD], F32, one)
        sc = sb("sc", [P, SUB, NG, H], F32, one)
        ex = sc
        pr = sb("pr", [P, SUB, NG, H], F32, one)
        row_max = sb("row_max", [P, SUB, NG], F32, one)
        row_sum = sb("row_sum", [P, SUB, NG], F32, one)
        row_inv = sb("row_inv", [P, SUB, NG], F32, one)
        spread = sb("spread", [P, SUB, NG, P], F32, one)
        spread_t = sb("spread_t", [P, SUB, NG * P], F32, one)
        at_t = xn_t
        x1 = sb("x1", [P, SUB, D], F32, one)
        z = sb("z", [P, SUB, D], F32, one)
        z_t = sb("z_t", [P, KC, BT], F32, one)
        logits_t = sb("logits_t", [E, BT], F32, one)
        stats = sb("stats", [P, 2 * SUB, 6], F32, one)
        mv = sb("mv", [P, 2 * SUB, 2], F32, one)
        var_eps = sb("var_eps", [P, 2 * SUB], F32, one)
        rstd = sb("rstd", [P, 2 * SUB], F32, one)
        b_raw = spread[0:3, 0].rearrange("p g n -> p (g n)")[:, 0:4 * D]
        b_rest = spread[0:3, 1].rearrange("p g n -> p (g n)")[:, 0:4 * D]
        b_part = [spread_t[0:3, 0, 0:4 * D], spread_t[0:3, 1, 0:4 * D]]
        b_bf = z_t[0:3].rearrange("p c t -> p (c t)").bitcast(BF16)
        one.close()

        two = ExitStack()
        wgu = sb("wgu", [P, KC, E * 2 * F], F32, two)
        wdn = sb("wdn", [P, len(F_CH), E * D], F32, two)
        zt_in = sb("zt_in", [P, 2, KC, BT], F32, two)
        base = sb("base", [P, 2, SUB, D], F32, two)
        gather_ix = sb("gather_ix", [P, 2], I32, two)
        pos_ix = sb("pos_ix", [P, STAGES, TOPK], U32, two)
        tok_ix = sb("tok_ix", [P, STAGES], I32, two)

        three = ExitStack()
        gate_act = sb("gate_act", [P, GB, BT], F32, three)
        sh_t = sb("sh_t", [P, len(FS_CH), BT], F32, three)
        iota_e = sb("iota_e", [P, E], F32, three)
        iota_slot = sb("iota_slot", [P, SLOTS], F32, three)
        iota_rows = sb("iota_rows", [P, NT], F32, three)
        tok_id = sb("tok_id", [P, NT], I32, three)
        zero_id = sb("zero_id", [SLOTS, P], I32, three)
        id_rows = sb("id_rows", [SLOTS, P], F32, three)
        upper = sb("upper", [P, P], BF16, three)
        ones_b = sb("ones_b", [P, P], BF16, three)
        d_m = sb("d_m", [P, NT], F32, three)
        d_s = sb("d_s", [P, NT, E], F32, three)
        d_ixf = sb("d_ixf", [P, TOPK, NT], F32, three)
        cnt_b = sb("cnt_b", [P, NT, E], BF16, three)
        tot = sb("tot", [P, NT, E], F32, three)
        run = sb("run", [P, NT, E], F32, three)
        rank = sb("rank", [P, NT, E], F32, three)
        tiles_of = sb("tiles_of", [P, 4, E], F32, three)
        posf = sb("posf", [P, TOPK, NT], F32, three)
        slot_f = sb("slot_f", [P, SLOTS], F32, three)
        ones_f = sb("ones_f", [P, NT], F32, three)
        sh_flat = sh_t[:, :, :].rearrange("p f t -> p (f t)")
        n_picked, n_wide = TOPK * NT * E, SLOTS * E
        picked = sh_flat[:, 0:n_picked].rearrange("p (k n e) -> p k n e", k=TOPK, n=NT)
        wide = sh_flat[:, n_picked:n_picked + n_wide].rearrange("p (j e) -> p j e", e=E)
        d_ix = sh_flat[:, n_picked + n_wide:n_picked + n_wide + NT * 8].bitcast(U32).rearrange("p (n e) -> p n e", e=8)
        three.close()

        four = ExitStack()
        zg = sb("zg", [P, 2, D], F32, four)
        zg_t = sb("zg_t", [P, 2, D], F32, four)
        silu = sb("silu", [P, 2, F], F32, four)
        act_t = sb("act_t", [P, 2, 3 * P], F32, four)
        y_sb = sb("y_sb", [P, 2, D], F32, four)
        four.close()

        comb = [wgu[:, i, 0:2 * D].rearrange("p (b d) -> p b d", b=2) for i in range(3)]
        comb_out = wgu[:, 3, 0:2 * D].rearrange("p (b d) -> p b d", b=2)
        two.close()

        ident_ready = sem("ident_ready")
        const_ready = sem("const_ready")
        wk_loaded, wq_loaded, wv_loaded, wo_loaded, ws_loaded = (sem(f"{n}_loaded") for n in ("wk", "wq", "wv", "wo", "ws"))
        bias_loaded = sem("bias_loaded")
        bias_ready = sem("bias_ready")
        x_loaded = sem("x_loaded")
        res_loaded = sem("res_loaded")
        x1_stored = sem("x1_stored")
        zt_stored = sem("zt_stored")
        cx_loaded = sem("cx_loaded")
        full = {b: sem(f"full_{b}") for b in sorted(set(BANK_OF.values()))}
        drained = {b: sem(f"drained_{b}") for b in full}
        xn_ready = sem("xn_ready")
        stat_ready = sem("stat_ready")
        rstd_ready = sem("rstd_ready")
        shifted = sem("shifted")
        exp_ready = sem("exp_ready")
        pr_ready = sem("pr_ready")
        spread_ready = sem("spread_ready")
        silu_ready = sem("silu_ready")
        sh_loaded = [sem("sh_loaded0"), sem("sh_loaded1")]
        sh_full = sem("sh_full")
        sh_out = sem("sh_out")
        z_ready = sem("z_ready")
        z_stored = sem("z_stored")
        base_stored = [sem("base_stored0"), sem("base_stored1")]
        dve_own = sem("dve_own")
        pool_own = sem("pool_own")

        def wait_full(eng, step, block):
            eng.wait_ge(full[BANK_OF[step]], earlier_fills(step, block) + 1)

        def wait_free(eng, step, block):
            n = earlier_fills(step, block)
            if not (isinstance(n, int) and n == 0):
                eng.wait_ge(drained[BANK_OF[step]], n)

        def wait_drained(eng, step, block):
            eng.wait_ge(drained[BANK_OF[step]], earlier_fills(step, block) + 1)

        waits_met = sem("waits_met")

        def settle(eng):
            eng.sem_inc(waits_met, 1)

        def sums_out(copy, s):
            step = f"P{s}"
            for q in range(4):
                dst = at_t[:, :, s * P:(s + 1) * P].rearrange("p c (j q t) -> p q c j t", q=4, t=GT)[:, q]
                src = bank_ap(step)[HD * q:HD * (q + 1), :].rearrange("p (j t c l) -> p l c j t", t=GT, c=KC, l=4)
                for l in range(4):
                    last = copy(dst[HD * l:HD * (l + 1)], src[:, l])
            last.then_inc(drained[BANK_OF[step]], 1)

        def stat_no(i, which, s):
            if which == 0:
                return SUB * i + s + 1 if isinstance(i, int) and i < 2 else (i - 2) * (2 * SUB) + (2 * SUB + s + 1)
            missing = max(0, i - (NB - 3)) if isinstance(i, int) else 0
            return i * (2 * SUB) + (3 * SUB + s + 1 - SUB * missing)

        w2_loaded = sem("w2_loaded")
        const2_ready = sem("const2_ready")
        r_shift = sem("r_shift")
        r_exp = sem("r_exp")
        r_cnt = sem("r_cnt")
        r_rank = sem("r_rank")
        r_ranked = sem("r_ranked")
        r_pos = sem("r_pos")
        zero_stored = sem("zero_stored")
        ids_scattered = [sem(f"ids_scattered{b}") for b in range(STAGES)]
        ids_loaded = sem("ids_loaded")
        ids_float, ids_turned = sem("ids_float"), sem("ids_turned")
        g_ix = sem("g_ix")
        g_loaded = [sem("g_loaded0"), sem("g_loaded1")]
        t_full, t_out = sem("t_full"), sem("t_out")
        g_full, g_silu, g_out = sem("g_full"), sem("g_silu"), sem("g_out")
        a_full, a_out = sem("a_full"), sem("a_out")
        d_full, d_out = sem("d_full"), sem("d_out")
        y_stored = [sem("y_stored0"), sem("y_stored1")]
        c_loaded = [sem("c_loaded0"), sem("c_loaded1")]
        cb_loaded = [sem("cb_loaded0"), sem("cb_loaded1")]
        c_done = sem("c_done")
        out_stored = [sem("out_stored0"), sem("out_stored1")]

        block = whole.enter_context(nc.Block())

        x_v = x.rearrange("(n s p) d -> n p s d", p=P, s=SUB)
        cx_v = ctx_t.rearrange("(c p) t -> p c t", p=P)

        def rows(dram_ap, i):
            return dram_ap[bass.ds(i * BT, BT), :].rearrange("(s p) d -> p s d", p=P)

        @block.sync
        def _(sp):
            def load_x(i):
                sp.dma_start(x_sb[:, :, :], rows(x, i)).then_inc(x_loaded, 16)

            def load_res(i):
                sp.dma_start(x_res[:, :, :], rows(x, i)).then_inc(res_loaded, 16)

            def load_cx(i):
                sp.dma_start(cx_t[:, :, :], cx_v[:, :, bass.ds(i * BT, BT)]).then_inc(cx_loaded, 16)

            def load_w(w, src, done):
                sp.dma_start(w[:, :, :], src.rearrange("(c p) n -> p c n", p=P)).then_inc(done, 16)

            load_x(0)
            load_cx(0)
            load_w(wk, wk_t, wk_loaded)
            load_w(wq, wq_t, wq_loaded)
            load_w(wv, wv_t, wv_loaded)
            load_res(0)
            sp.wait_ge(xn_ready, SUB)
            load_x(1)
            load_w(wo, wo_t, wo_loaded)
            load_w(wgate, wgate_t, wo_loaded)
            sp.wait_ge(xn_ready, 2 * SUB)
            load_x(2)
            wait_full(sp, "V1", -1)
            load_cx(1)
            load_w(wsgu, wsgu_t, ws_loaded)
            whole_ch = FS // P
            load_w(wsdn[:, 0:whole_ch, :], wsdn_t[0:whole_ch * P, :], ws_loaded)
            sp.dma_start(wsdn[0:FS - whole_ch * P, whole_ch, :], wsdn_t[whole_ch * P:FS, :]).then_inc(ws_loaded, 16)

            def store_columns(i):
                wait_drained(sp, "Z0", i)
                settle(sp)
                wait_drained(sp, "Z1", i)
                settle(sp)
                sp.dma_start(zt_d[bass.ds(i - 1, 1)].rearrange("o p c t -> p (o c t)"), z_t[:, :, :].rearrange("p c t -> p (c t)")).then_inc(zt_stored, 16)

            def body(i, behind, ahead, ahead2, ahead3):
                if behind:
                    store_columns(i)
                if ahead3:
                    sp.wait_ge(xn_ready, (i + 2) * SUB + SUB)
                    load_x(i + 3)
                if ahead2:
                    wait_full(sp, "V1", i)
                    settle(sp)
                    load_cx(i + 2)
                wait_drained(sp, "O1", i)
                settle(sp)
                if ahead:
                    load_res(i + 1)
                sp.dma_start(rows(x1_d, i), x1[:, :, :]).then_inc(x1_stored, 16)
                sp.wait_ge(z_ready, i * SUB + SUB)
                settle(sp)
                sp.dma_start(rows(z_d, i), z[:, :, :]).then_inc(z_stored, 16)

            body(0, False, True, True, True)
            with sp.Fori(1, NB - 3) as i:
                body(i, True, True, True, True)
            body(NB - 3, True, True, True, False)
            body(NB - 2, True, True, False, False)
            body(NB - 1, True, False, False, False)
            store_columns(NB)
            sp.wait_ge(x1_stored, 16 * NB)
            sp.wait_ge(z_stored, 16 * NB)
            sp.wait_ge(zt_stored, 16 * NB)
            wait_drained(sp, "LT", NB)

            def load_block(i, b):
                sp.dma_start(zt_in[:, b, :, :], zt_d[bass.ds(i, 1)].rearrange("o p c t -> p (o c) t")).then_inc(sh_loaded[b], 16)
                sp.dma_start(base[:, b, :, :], rows(x1_d, i)).then_inc(sh_loaded[b], 16)

            def store_base(i, b, k, more):
                sp.wait_ge(sh_out, i * SH_STEPS + SH_STEPS)
                settle(sp)
                sp.dma_start(rows(base_d, i), base[:, b, :, :]).then_inc(base_stored[b], 16)
                if more:
                    sp.wait_ge(base_stored[b], k * 16 + 16)
                    settle(sp)
                    load_block(i + 2, b)

            load_block(0, 0)
            load_block(1, 1)
            sp.dma_start(wgu[:, :, :], wgu_t.rearrange("(c p) e n -> p c (e n)", p=P)).then_inc(w2_loaded, 16)
            for f, (f0, fn) in enumerate(F_CH):
                sp.dma_start(wdn[0:fn, f, :], wdn_t[f0:f0 + fn].rearrange("p e n -> p (e n)")).then_inc(w2_loaded, 16)
            sp.wait_ge(const2_ready, 1)
            sp.dma_start(token_d.rearrange("(j p) o -> j (p o)", p=P), zero_id[:, :]).then_inc(zero_stored, 16)
            with sp.Fori(0, SHARED_FIRST // 2) as k:
                for b in range(2):
                    store_base(k * 2 + b, b, k, True)
            with sp.Fori(0, SLOTS // 2) as k:
                for b in range(2):
                    j = k * 2 + b
                    sp.wait_ge(d_out, j + 1)
                    settle(sp)
                    sp.dma_start(y_d[bass.ds(j * P, P), :], y_sb[:, b, :]).then_inc(y_stored[b], 16)
            def store_out(n, b):
                sp.wait_ge(c_done, n + 1)
                settle(sp)
                sp.dma_start(out[bass.ds(n * P, P), :], comb_out[:, b, :]).then_inc(out_stored[b], 16)

            for k in range((NB - SHARED_FIRST) // 2):
                for b in range(2):
                    for m in range(TAIL_TILES):
                        store_out((2 * k + b) * TAIL_TILES + m, m % 2)
                    i = SHARED_FIRST + 2 * k + b
                    store_base(i, b, i // 2, i + 2 < NB)
            for n in range((NB - SHARED_FIRST) * TAIL_TILES, NT):
                store_out(n, n % 2)
            for b in range(2):
                sp.wait_ge(out_stored[b], 16 * (NT // 2))

        @block.tensor
        def _(pe):
            def mm(o, l, r, start, stop):
                return nc.tensor.matmul(o, l, r, start=start, stop=stop)

            def project(name, w, src, part, i, chunks):
                for c in chunks:
                    step = f"{name}{c // 2}"
                    if c % 2 == 0:
                        wait_free(pe, step, i)
                    oc = bank_ap(step)[:, c % 2 * BT:(c % 2 + 1) * BT]
                    for kc in range(KC):
                        mm(oc, w[:, kc, c * P:(c + 1) * P], src[:, kc, :], kc == 0, False)
                    if isinstance(i, int) and i < 0 and c == 0:
                        pe.wait_ge(bias_ready, {"K": 1, "Q": 2, "V": 3}[name])
                    last = mm(oc, bias3[:, part * D + c * P:part * D + (c + 1) * P], ones3[:, :], False, True)
                    if c % 2 == 1:
                        last.then_inc(full[BANK_OF[step]], 1)

            def turn_x(i):
                for s in range(SUB):
                    step = f"X{s}"
                    wait_free(pe, step, i)
                    pe.wait_ge(xn_ready, (i + 1) * SUB + (s + 1))
                    for kc in range(KC):
                        last = nc.tensor.transpose(bank_ap(step)[:, kc * P:(kc + 1) * P], xn[:, s, kc * P:(kc + 1) * P], ident[:, :])
                    last.then_inc(full[BANK_OF[step]], 1)

            def project_k(i, chunks):
                if chunks[0] == 0:
                    pe.wait_ge(cx_loaded, (i + 1) * 16 + 16)
                project("K", wk, cx_t, 1, i, chunks)

            def project_q(i, chunks):
                if chunks[0] == 0:
                    wait_drained(pe, "X0", i)
                    wait_drained(pe, "X1", i)
                project("Q", wq, xn_t, 0, i, chunks)

            def turn_z(i):
                for s in range(SUB):
                    step = f"Z{s}"
                    wait_free(pe, step, i)
                    pe.wait_ge(z_ready, (i - 1) * SUB + (s + 1))
                    for kc in range(KC):
                        last = nc.tensor.transpose(bank_ap(step)[:, kc * P:(kc + 1) * P], z[:, s, kc * P:(kc + 1) * P], ident[:, :])
                    last.then_inc(full[BANK_OF[step]], 1)

            def route(i):
                wait_free(pe, "L", i)
                wait_drained(pe, "Z0", i)
                wait_drained(pe, "Z1", i)
                for kc in range(KC):
                    last = mm(bank_ap("L")[0:E, 0:BT], wgate[:, kc, :], z_t[:, kc, :], kc == 0, kc == KC - 1)
                last.then_inc(full[BANK_OF["L"]], 1)

            def turn_logits(i):
                wait_free(pe, "LT", i)
                settle(pe)
                for s in range(SUB):
                    last = nc.tensor.transpose(bank_ap("LT")[:, s * E:(s + 1) * E], logits_t[:, s * P:(s + 1) * P], ident[0:E, 0:E])
                last.then_inc(full[BANK_OF["LT"]], 1)

            def scores(s, i, us):
                for u in us:
                    step = f"S{s}{u}"
                    o = bank_ap(step)
                    wait_free(pe, step, i)
                    mm(o, onehot[:, :], other[:, :, :], True, False)
                    for g in range(UG):
                        t0 = s * P + (u * UG + g) * GT
                        last = mm(o[:, g * P:(g + 1) * P], q_t[:, t0:t0 + GT, :], k_t[:, t0:t0 + GT, :], False, g == UG - 1)
                    last.then_inc(full[BANK_OF[step]], 1)

            def v_pairs(s, i):
                step = f"VT{s}"
                wait_free(pe, step, i)
                settle(pe)
                for g in range(NG):
                    t0 = s * P + g * GT
                    last = nc.tensor.transpose(bank_ap(step)[:, g * HD:(g + 1) * HD], v_t[:, t0:t0 + GT, :], ident[0:HD, 0:HD])
                last.then_inc(full[BANK_OF[step]], 1)

            def transpose_weights(s, i):
                for u in range(NU):
                    step = f"T{s}{u}"
                    wait_free(pe, step, i)
                    pe.wait_ge(spread_ready, i * (SUB * NU) + (s * NU + u + 1))
                    for g in range(UG):
                        last = nc.tensor.transpose(bank_ap(step)[:, g * P:(g + 1) * P], spread[:, s, u * UG + g, :], ident[:, :])
                    last.then_inc(full[BANK_OF[step]], 1)

            def attend(s, i):
                step = f"P{s}"
                wait_free(pe, step, i)
                if s == 0:
                    for u in range(NU):
                        wait_drained(pe, f"T1{u}", i)
                    wait_drained(pe, "VT0", i)
                    wait_drained(pe, "VT1", i)
                for g in range(NG):
                    q, j = g % 4, g // 4
                    last = mm(bank_ap(step)[HD * q:HD * (q + 1), j * P:(j + 1) * P], v_p[:, s * NG + g, :],
                              spread_t[:, s, g * P:(g + 1) * P], True, True)
                last.then_inc(full[BANK_OF[step]], 1)

            def project_out(s, i):
                step = f"O{s}"
                wait_free(pe, step, i)
                wait_drained(pe, f"P{s}", i)
                mm(bank_ap(step), ones3[:, 0:P], bias3[:, 3 * D:4 * D], True, False)
                for kc in range(KC):
                    last = mm(bank_ap(step), at_t[:, kc, s * P:(s + 1) * P], wo[:, kc, :], False, kc == KC - 1)
                last.then_inc(full[BANK_OF[step]], 1)

            def body(i, behind, ahead):
                if isinstance(i, int) and i == 0:
                    for step in ("Q0", "Q1", "V0", "V1"):
                        wait_drained(pe, step, -1)
                if ahead:
                    turn_x(i)
                scores(0, i, (0,))
                for n in range(SUB * NU):
                    if n + 1 < SUB * NU:
                        scores((n + 1) // NU, i, ((n + 1) % NU,))
                    if ahead:
                        (project_k if n < KC else project_q)(i, (n % KC,))
                transpose_weights(0, i)
                if ahead:
                    project("V", wv, cx_t, 2, i, (0, 1))
                if behind:
                    turn_z(i)
                v_pairs(0, i)
                transpose_weights(1, i)
                v_pairs(1, i)
                if behind:
                    route(i)
                attend(0, i)
                if ahead:
                    project("V", wv, cx_t, 2, i, (2, 3))
                attend(1, i)
                if behind:
                    turn_logits(i)
                project_out(0, i)
                project_out(1, i)

            pe.wait_ge(ident_ready, 1)
            turn_x(-1)
            pe.wait_ge(wk_loaded, 16)
            project_k(-1, range(KC))
            pe.wait_ge(wq_loaded, 16)
            project_q(-1, range(KC))
            pe.wait_ge(wv_loaded, 16)
            project("V", wv, cx_t, 2, -1, range(KC))
            pe.wait_ge(const_ready, 1)
            pe.wait_ge(bias_ready, 4)
            pe.wait_ge(wo_loaded, 32)
            body(0, False, True)
            with pe.Fori(1, NB - 1) as i:
                body(i, True, True)
            body(NB - 1, True, False)
            turn_z(NB)
            route(NB)
            turn_logits(NB)

            def sh_bank(step):
                return psum_a[:, step * BANK:(step + 1) * BANK] if step < 4 else psum_b[step - 4][:, :]

            def sh_free(i, step):
                if not (isinstance(i, int) and i == 0):
                    pe.wait_ge(sh_out, (i - 1) * SH_STEPS + (step + 1))

            def gate_up(i, b, fs):
                for f in fs:
                    f0, fn = FS_CH[f]
                    sh_free(i, f)
                    for half in range(2):
                        for kc in range(KC):
                            last = mm(sh_bank(f)[0:fn, half * BT:(half + 1) * BT], wsgu[:, kc, half * FS + f0:half * FS + f0 + fn],
                                      zt_in[:, b, kc, :], kc == 0, kc == KC - 1)
                    last.then_inc(sh_full, 1)

            def down(i, b):
                n = len(FS_CH)
                for fs in (range(n - 1), range(n - 1, n)):
                    for s in range(SUB):
                        if fs[0] == 0:
                            sh_free(i, n + s)
                        for f in fs:
                            fn = FS_CH[f][1]
                            if s == 0:
                                pe.wait_ge(sh_out, i * SH_STEPS + (f + 1))
                            last = mm(sh_bank(n + s), sh_t[0:fn, f, s * P:(s + 1) * P], wsdn[0:fn, f, :], f == 0, f == n - 1)
                        if fs[0] == n - 1:
                            last.then_inc(sh_full, 1)

            def shared(i, b, k):
                pe.wait_ge(sh_loaded[b], k * 32 + 32)
                gate_up(i, b, range(len(FS_CH)))
                down(i, b)

            for step in ("P0", "P1", "T12", "T13", "O0", "O1"):
                wait_drained(pe, step, NB - 1)
            wait_drained(pe, "LT", NB)
            wait_drained(pe, "Z0", NB)
            pe.wait_ge(ws_loaded, 48)
            pe.wait_ge(sh_loaded[0], 32)
            gate_up(0, 0, range(4))
            pe.wait_ge(r_cnt, 1)
            pe.wait_ge(const2_ready, 1)
            flat = cnt_b[:, :, :].rearrange("p n e -> p (n e)")
            mm(psum_b[3][:, 0:NT * E], upper[:, :], flat, True, True)
            mm(psum_b[3][:, NT * E:2 * NT * E], ones_b[:, :], flat, True, True).then_inc(r_rank, 1)
            gate_up(0, 0, range(4, 6))
            pe.wait_ge(r_ranked, 1)
            down(0, 0)
            shared(1, 1, 0)
            with pe.Fori(1, SHARED_FIRST // 2) as k:
                for b in range(2):
                    shared(k * 2 + b, b, k)
            pe.wait_ge(sh_out, SHARED_FIRST * SH_STEPS)

            t_bank, a_bank, d_bank = psum_b[0], psum_b[1], psum_b[2]

            def g_bank(b, half):
                return psum_a[:, (2 * b + half) * BANK:(2 * b + half) * BANK + F]

            def turn_rows(j, b, k):
                pe.wait_ge(g_loaded[b], k * 16 + 16)
                if not (isinstance(j, int) and j == 0):
                    pe.wait_ge(t_out, j)
                for kc in range(KC):
                    last = nc.tensor.transpose(t_bank[:, kc * P:(kc + 1) * P], zg[:, b, kc * P:(kc + 1) * P], ident[:, :])
                last.then_inc(t_full, 1)

            def open_expert(j, b):
                e = pe.value_load(slot_expert[0:1, bass.ds(j, 1)], min_val=0, max_val=E - 1)
                pe.wait_ge(t_out, j + 1)
                if not (isinstance(j, int) and j < 2):
                    pe.wait_ge(g_out, j - 1)
                for half in range(2):
                    for kc in range(KC):
                        last = mm(g_bank(b, half), zg_t[:, b, kc * P:(kc + 1) * P], wgu[:, kc, bass.ds(e * (2 * F) + half * F, F)],
                                  kc == 0, kc == KC - 1)
                last.then_inc(g_full, 1)
                return e

            def turn_act(j, b):
                pe.wait_ge(g_out, j + 1)
                if not (isinstance(j, int) and j == 0):
                    pe.wait_ge(a_out, j)
                for f, (f0, fn) in enumerate(F_CH):
                    last = nc.tensor.transpose(a_bank[0:fn, f * P:(f + 1) * P], silu[:, b, f0:f0 + fn], ident[:, :])
                last.then_inc(a_full, 1)

            def close_expert(j, b):
                e = pe.value_load(slot_expert[0:1, bass.ds(j, 1)], min_val=0, max_val=E - 1)
                pe.wait_ge(a_out, j + 1)
                if not (isinstance(j, int) and j == 0):
                    pe.wait_ge(d_out, j)
                for f, (f0, fn) in enumerate(F_CH):
                    last = mm(d_bank[:, :], act_t[0:fn, b, f * P:(f + 1) * P], wdn[0:fn, f, bass.ds(e * D, D)],
                              f == 0, f == len(F_CH) - 1)
                last.then_inc(d_full, 1)

            pe.wait_ge(ids_float, 1)
            nc.tensor.transpose(psum_b[3][:, 0:SLOTS], id_rows[:, :], ident[0:SLOTS, 0:SLOTS]).then_inc(ids_turned, 1)
            pe.wait_ge(w2_loaded, 16 * (1 + len(F_CH)))
            pe.wait_ge(r_pos, 1)
            turn_rows(0, 0, 0)
            open_expert(0, 0)
            turn_rows(1, 1, 0)
            turn_act(0, 0)
            open_expert(1, 1)
            turn_rows(2, 0, 1)
            close_expert(0, 0)
            turn_act(1, 1)
            with pe.Fori(1, SLOTS // 2 - 1) as k:
                for b in range(2):
                    j = k * 2 + b
                    open_expert(j, b)
                    turn_rows(j + 1, 1 - b, k + b)
                    close_expert(j - 1, 1 - b)
                    turn_act(j, b)
            j = SLOTS - 2
            open_expert(j, 0)
            turn_rows(j + 1, 1, SLOTS // 2 - 1)
            close_expert(j - 1, 1)
            turn_act(j, 0)
            open_expert(j + 1, 1)
            close_expert(j, 0)
            turn_act(j + 1, 1)
            close_expert(j + 1, 1)
            pe.wait_ge(d_out, SLOTS)
            for i in range(SHARED_FIRST, NB):
                shared(i, i % 2, i // 2)

        @block.scalar
        def _(act):
            def copy(o, i_):
                return nc.scalar.activation(o, i_, ACT.Copy)

            def heads_out(step, dst, b):
                view = dst[:, :, :].rearrange("p t (b c l) -> p b l c t", b=2, c=2)
                for l in range(4):
                    last = copy(view[:, b, l], bank_ap(step)[HD * l:HD * (l + 1), :].rearrange("p (c t) -> p c t", c=2))
                last.then_inc(drained[BANK_OF[step]], 1)

            def z_out(i):
                if not (isinstance(i, int) and i == 1):
                    act.wait_ge(zt_stored, (i - 1) * 16)
                for s in range(SUB):
                    wait_full(act, f"Z{s}", i)
                    copy(z_t[:, :, s * P:(s + 1) * P], bank_ap(f"Z{s}").rearrange("p (c t) -> p c t", c=KC)).then_inc(drained[BANK_OF[f"Z{s}"]], 1)

            def x_out(i):
                for s in range(SUB):
                    wait_full(act, f"X{s}", i)
                    copy(xn_t[:, :, s * P:(s + 1) * P], bank_ap(f"X{s}").rearrange("p (c t) -> p c t", c=KC)).then_inc(drained[BANK_OF[f"X{s}"]], 1)

            def projected(i, step, dst, b):
                wait_full(act, step, i)
                heads_out(step, dst, b)

            def pairs_out(s, i):
                wait_full(act, f"VT{s}", i)
                copy(v_p[:, s * NG:(s + 1) * NG, :], bank_ap(f"VT{s}").rearrange("p (g d) -> p g d", d=HD)).then_inc(drained[BANK_OF[f"VT{s}"]], 1)

            def weights_out(s, i):
                for u in range(NU):
                    step = f"T{s}{u}"
                    wait_full(act, step, i)
                    copy(spread_t[:, s, u * BANK:(u + 1) * BANK], bank_ap(step)).then_inc(drained[BANK_OF[step]], 1)

            def body(i, behind, ahead):
                if ahead:
                    x_out(i)
                for s in range(SUB):
                    act.wait_ge(shifted, i * SUB + (s + 1))
                    nc.scalar.activation(ex[:, s], sc[:, s], ACT.Exp).then_inc(exp_ready, 1)
                if ahead:
                    wait_full(act, "S13", i)
                    projected(i, "K0", k_t, 0)
                    projected(i, "K1", k_t, 1)
                weights_out(0, i)
                if behind:
                    z_out(i)
                pairs_out(0, i)
                weights_out(1, i)
                pairs_out(1, i)
                if ahead:
                    projected(i, "V1", v_t, 1)
                wait_full(act, "P1", i)
                sums_out(copy, 1)

            for part, b in enumerate((bq, bk, bv, bo)):
                act.dma_start(b_raw[:, part * D:(part + 1) * D], b.partition_broadcast(3)).then_inc(bias_loaded, 16)
            x_out(-1)
            projected(-1, "K0", k_t, 0)
            projected(-1, "K1", k_t, 1)
            projected(-1, "V1", v_t, 1)
            body(0, False, True)
            with act.Fori(1, NB - 1) as i:
                body(i, True, True)
            body(NB - 1, True, False)
            z_out(NB)

            act.wait_ge(r_shift, 1)
            nc.scalar.activation(d_s[:, :, :], d_s[:, :, :], ACT.Exp).then_inc(r_exp, 1)

            def sh_bank(step):
                return psum_a[:, step * BANK:(step + 1) * BANK] if step < 4 else psum_b[step - 4][:, :]

            def gate(i, f):
                fn = FS_CH[f][1]
                act.wait_ge(sh_full, i * SH_STEPS + (f + 1))
                if f >= GB:
                    act.wait_ge(sh_out, i * SH_STEPS + (f - GB + 1))
                nc.scalar.activation(gate_act[0:fn, f % GB, :], sh_bank(f)[0:fn, 0:BT], ACT.Silu).then_inc(silu_ready, 1)

            with act.Fori(0, SHARED_FIRST // 2) as k:
                for b in range(2):
                    for f in range(len(FS_CH)):
                        gate(k * 2 + b, f)

            a_bank, d_bank = psum_b[1], psum_b[2]

            def step(j, b, k):
                act.wait_ge(g_full, j + 1)
                nc.scalar.activation(silu[:, b, :], psum_a[:, 2 * b * BANK:2 * b * BANK + F], ACT.Silu).then_inc(g_silu, 1)
                if not (isinstance(j, int) and j == 0):
                    rows_out(j - 1, 1 - b, k - 1 + b)
                act.wait_ge(a_full, j + 1)
                copy(act_t[:, b, 0:2 * P], a_bank[:, 0:2 * P])
                copy(act_t[0:F_CH[2][1], b, 2 * P:3 * P], a_bank[0:F_CH[2][1], 2 * P:3 * P]).then_inc(a_out, 1)

            def rows_out(j, b, k):
                act.wait_ge(d_full, j + 1)
                if not (isinstance(j, int) and j < 2):
                    act.wait_ge(y_stored[b], k * 16)
                copy(y_sb[:, b, :], d_bank[:, :]).then_inc(d_out, 1)

            for j in range(4):
                step(j, j % 2, j // 2)
            with act.Fori(2, SLOTS // 2) as k:
                for b in range(2):
                    step(k * 2 + b, b, k)
            rows_out(SLOTS - 1, 1, SLOTS // 2 - 1)

            def load_base(n):
                b = n % 2
                if n >= 2:
                    act.wait_ge(c_done, n - 1)
                i = n // SUB
                act.wait_ge(base_stored[i % 2], 16 * (i // 2 + 1))
                act.dma_start(comb[2][:, b, :], base_d[n * P:(n + 1) * P, :]).then_inc(cb_loaded[b], 16)

            load_base(0)
            n = 1
            for i in range(SHARED_FIRST, NB):
                for f in range(len(FS_CH)):
                    gate(i, f)
                    load_base(n)
                    n += 1
            while n < NT:
                load_base(n)
                n += 1

        @block.vector
        def _(dve):
            own_ = Chain(dve, dve_own)
            link, mark = own_.link, own_.mark
            V = nc.vector

            def split_bias(part):
                at = slice(part * D, (part + 1) * D)
                link(V.tensor_copy(b_bf[:, at], b_raw[:, at]))
                link(V.tensor_copy(b_part[0][:, at], b_bf[:, at]))
                link(V.tensor_tensor(b_rest[:, at], b_raw[:, at], b_part[0][:, at], ALU.subtract))
                link(V.tensor_copy(b_bf[:, at], b_rest[:, at]))
                link(V.tensor_copy(b_part[1][:, at], b_bf[:, at]))
                link(V.tensor_tensor(b_rest[:, at], b_rest[:, at], b_part[1][:, at], ALU.subtract))
                link(V.tensor_scalar(b_raw[:, at], b_part[0][:, at], ident[0:3, 0:1], None, ALU.mult))
                link(V.scalar_tensor_tensor(out=b_part[1][:, at], in0=b_part[1][:, at], scalar=ident[0:3, 1:2], in1=b_raw[:, at], op0=ALU.mult, op1=ALU.add))
                link(V.scalar_tensor_tensor(out=b_raw[:, at], in0=b_rest[:, at], scalar=ident[0:3, 2:3], in1=b_part[1][:, at], op0=ALU.mult, op1=ALU.add))
                V.tensor_copy(bias3[0:3, at], b_raw[:, at]).then_inc(bias_ready, 1)

            def x_stats(i):
                dve.wait_ge(x_loaded, i * 16 + 16)
                for s in range(SUB):
                    mark(V.bn_stats(stats[:, s, :], x_sb[:, s, :]))
                own_.wait()
                for s in range(SUB):
                    settle(dve)
                    V.bn_aggr(mv[:, s, :], stats[:, s, :]).then_inc(stat_ready, 1)

            def normalise_x(i):
                for s in range(SUB):
                    dve.wait_ge(rstd_ready, stat_no(i, 0, s))
                    V.tensor_scalar(xn[:, s, :], x_sb[:, s, :], mv[:, s, 0:1], rstd[:, s:s + 1], ALU.subtract, ALU.mult).then_inc(xn_ready, 1)

            def heads_out(step, dst, b):
                view = dst[:, :, :].rearrange("p t (b c l) -> p b l c t", b=2, c=2)
                for l in range(4):
                    last = V.tensor_copy(view[:, b, l], bank_ap(step)[HD * l:HD * (l + 1), :].rearrange("p (c t) -> p c t", c=2))
                last.then_inc(drained[BANK_OF[step]], 1)

            def own_scores(i, s, us):
                for u in us:
                    step = f"S{s}{u}"
                    wait_full(dve, step, i)
                    ins = V.tensor_reduce(out=sc[:, s, u * UG:(u + 1) * UG, :],
                                          in_=bank_ap(step).rearrange("p (r t g) -> p r g t", r=UG, t=GT), axis=X, op=ALU.max)
                    ins.then_inc(drained[BANK_OF[step]], 1)

            def shift(i, s):
                for u in range(NU):
                    wait_drained(dve, f"S{s}{u}", i)
                link(V.tensor_reduce(out=row_max[:, s, :], in_=sc[:, s], axis=X, op=ALU.max))
                V.tensor_tensor(sc[:, s], sc[:, s], row_max[:, s, :].unsqueeze(2).broadcast_to([P, NG, H]), ALU.subtract).then_inc(shifted, 1)

            def softmax(i, s):
                dve.wait_ge(exp_ready, i * SUB + (s + 1))
                link(V.tensor_reduce(out=row_sum[:, s, :], in_=ex[:, s], axis=X, op=ALU.add))
                link(V.reciprocal(row_inv[:, s, :], row_sum[:, s, :]))
                V.tensor_tensor(pr[:, s], ex[:, s], row_inv[:, s, :].unsqueeze(2).broadcast_to([P, NG, H]), ALU.mult).then_inc(pr_ready, 1)

            def logits_out(i):
                wait_full(dve, "L", i)
                V.tensor_copy(logits_t[:, :], bank_ap("L")[0:E, 0:BT]).then_inc(drained[BANK_OF["L"]], 1)

            def turned_logits_out(i):
                wait_full(dve, "LT", i)
                V.tensor_copy(tok_scores[:, bass.ds((i - 1) * SUB, SUB), :], bank_ap("LT")[:, 0:SUB * E].rearrange("p (s e) -> p s e", s=SUB)).then_inc(drained[BANK_OF["LT"]], 1)

            def projected(i, step, dst, b):
                wait_full(dve, step, i)
                heads_out(step, dst, b)

            def body(i, behind, ahead, ahead2):
                own_scores(i, 0, range(NU))
                shift(i, 0)
                if ahead2:
                    x_stats(i + 2)
                own_scores(i, 1, range(2))
                softmax(i, 0)
                own_scores(i, 1, range(2, NU))
                shift(i, 1)
                if ahead2:
                    wait_full(dve, "X1", i)
                    normalise_x(i + 2)
                softmax(i, 1)
                if ahead:
                    projected(i, "Q0", q_t, 0)
                    projected(i, "Q1", q_t, 1)
                wait_full(dve, "VT1", i)
                if ahead:
                    projected(i, "V0", v_t, 0)
                if behind:
                    logits_out(i)
                wait_full(dve, "P0", i)
                sums_out(V.tensor_copy, 0)
                if behind:
                    turned_logits_out(i)
                if not (isinstance(i, int) and i == 0):
                    dve.wait_ge(x1_stored, i * 16)
                    dve.wait_ge(z_stored, i * 16)
                for s in range(SUB):
                    wait_full(dve, f"O{s}", i)
                    dve.wait_ge(res_loaded, i * 16 + 16)
                    V.tensor_tensor(x1[:, s, :], bank_ap(f"O{s}"), x_res[:, s, :], ALU.add).then_inc(drained[BANK_OF[f"O{s}"]], 1)
                    wait_drained(dve, f"O{s}", i)
                    link(V.bn_stats(stats[:, SUB + s, :], x1[:, s, :]))
                    settle(dve)
                    V.bn_aggr(mv[:, SUB + s, :], stats[:, SUB + s, :]).then_inc(stat_ready, 1)
                for s in range(SUB):
                    dve.wait_ge(rstd_ready, stat_no(i, 1, s))
                    V.tensor_scalar(z[:, s, :], x1[:, s, :], mv[:, SUB + s, 0:1], rstd[:, SUB + s:SUB + s + 1], ALU.subtract, ALU.mult).then_inc(z_ready, 1)

            x_stats(0)
            normalise_x(0)
            dve.wait_ge(bias_loaded, 16 * 4)
            dve.wait_ge(ident_ready, 1)
            for part in (1, 0, 2, 3):
                split_bias(part)
            dve.wait_ge(bias_ready, 4)
            projected(-1, "Q0", q_t, 0)
            projected(-1, "Q1", q_t, 1)
            projected(-1, "V0", v_t, 0)
            x_stats(1)
            wait_full(dve, "X1", -1)
            normalise_x(1)
            body(0, False, True, True)
            DVE_SIGNALS = 10
            with dve.Fori(1, NB - 2) as i:
                own_.enter(i - 1, DVE_SIGNALS)
                body(i, True, True, True)
            own_.leave(NB - 3)
            body(NB - 2, True, True, False)
            body(NB - 1, True, False, False)
            logits_out(NB)
            turned_logits_out(NB)
            wait_drained(dve, "LT", NB)
            dve.wait_ge(z_stored, 16 * NB)
            dve.wait_ge(x1_stored, 16 * NB)
            dve.wait_ge(zt_stored, 16 * NB)
            link(V.tensor_reduce(out=d_m[:, :], in_=tok_scores[:, :, :], axis=X, op=ALU.max))
            V.tensor_tensor(d_s[:, :, :], tok_scores[:, :, :], d_m[:, :].unsqueeze(2).broadcast_to([P, NT, E]), ALU.subtract).then_inc(r_shift, 1)
            dve.wait_ge(r_exp, 1)
            mark(V.memset(ones_f[:, :], 1.0))
            dve.wait_ge(const2_ready, 1)
            link(V.tensor_reduce(out=d_m[:, :], in_=d_s[:, :, :], axis=X, op=ALU.add))
            link(V.reciprocal(d_m[:, :], d_m[:, :]))
            link(V.tensor_tensor(d_s[:, :, :], d_s[:, :, :], d_m[:, :].unsqueeze(2).broadcast_to([P, NT, E]), ALU.mult))
            for n in range(NT):
                mark(V.max(top_w[:, n, :], d_s[:, n, :]))
            own_.wait()
            for n in range(NT):
                mark(V.max_index(d_ix[:, n, :], top_w[:, n, :], d_s[:, n, :]))
            own_.wait()
            link(V.tensor_copy(d_ixf[:, :, :], d_ix[:, :, 0:TOPK].rearrange("p n k -> p k n")))
            for k in range(TOPK):
                mark(V.tensor_tensor(picked[:, k], d_ixf[:, k, :].unsqueeze(2).broadcast_to([P, NT, E]),
                                     iota_e[:, :].unsqueeze(1).broadcast_to([P, NT, E]), ALU.is_equal))
            own_.wait()
            V.tensor_tensor(cnt_b[:, :, :], picked[:, 0], picked[:, 1], ALU.add).then_inc(r_cnt, 1)
            dve.wait_ge(r_rank, 1)
            mark(V.tensor_copy(rank[:, :, :], psum_b[3][:, 0:NT * E].rearrange("p (n e) -> p n e", e=E)))
            link(V.tensor_copy(tot[:, :, :], psum_b[3][:, NT * E:2 * NT * E].rearrange("p (n e) -> p n e", e=E)))
            dve.sem_inc(r_ranked, 1)
            for e in range(E):
                mark(V.tensor_tensor_scan(out=run[:, :, e], data0=ones_f[:, :], data1=tot[:, :, e], initial=0.0, op0=ALU.mult, op1=ALU.add))
            own_.wait()
            link(V.tensor_tensor(wide[:, 0:NT, :], run[:, NT - 1, :].unsqueeze(1).broadcast_to([P, NT, E]),
                                 iota_rows[:, :].unsqueeze(2).broadcast_to([P, NT, E]), ALU.is_gt))
            link(V.tensor_reduce(out=tiles_of[:, 0, :], in_=wide[:, 0:NT, :].rearrange("p n e -> p e n"), axis=X, op=ALU.add))
            link(V.tensor_tensor_scan(out=tiles_of[:, 1, :], data0=ones_f[:, 0:E], data1=tiles_of[:, 0, :], initial=0.0, op0=ALU.mult, op1=ALU.add))
            link(V.tensor_tensor(tiles_of[:, 2, :], tiles_of[:, 1, :], tiles_of[:, 0, :], ALU.subtract))
            link(V.tensor_scalar(tiles_of[:, 3, :], tiles_of[:, 2, :], float(P), None, ALU.mult))
            link(V.tensor_tensor(wide[:, :, 0:E - 1], tiles_of[:, 2, 1:E].unsqueeze(1).broadcast_to([P, SLOTS, E - 1]),
                                 iota_slot[:, :].unsqueeze(2).broadcast_to([P, SLOTS, E - 1]), ALU.is_le))
            link(V.tensor_reduce(out=slot_f[:, :], in_=wide[:, :, 0:E - 1], axis=X, op=ALU.add))
            mark(V.tensor_copy(slot_expert[:, :], slot_f[:, :]))
            link(V.tensor_tensor(rank[:, :, :], rank[:, :, :], run[:, :, :], ALU.add))
            link(V.tensor_tensor(rank[:, :, :], rank[:, :, :], tot[:, :, :], ALU.subtract))
            link(V.tensor_tensor(rank[:, :, :], rank[:, :, :], tiles_of[:, 3, :].unsqueeze(1).broadcast_to([P, NT, E]), ALU.add))
            for k in range(TOPK):
                link(V.tensor_tensor(picked[:, k], picked[:, k], rank[:, :, :], ALU.mult))
                link(V.tensor_reduce(out=posf[:, k, :], in_=picked[:, k], axis=X, op=ALU.add))
            V.tensor_copy(pos[:, :, :], posf[:, :, :]).then_inc(r_pos, 1)

            def sh_bank(step):
                return psum_a[:, step * BANK:(step + 1) * BANK] if step < 4 else psum_b[step - 4][:, :]

            def gate_times_up(i, f):
                fn = FS_CH[f][1]
                dve.wait_ge(silu_ready, i * len(FS_CH) + (f + 1))
                V.tensor_tensor(sh_t[0:fn, f, :], gate_act[0:fn, f % GB, :], sh_bank(f)[0:fn, BT:2 * BT], ALU.mult).then_inc(sh_out, 1)

            def add_shared(i, b):
                for s in range(SUB):
                    n = len(FS_CH) + s
                    dve.wait_ge(sh_full, i * SH_STEPS + (n + 1))
                    V.tensor_tensor(base[:, b, s, :], sh_bank(n), base[:, b, s, :], ALU.add).then_inc(sh_out, 1)

            dve.wait_ge(r_pos, 1)
            with dve.Fori(0, SHARED_FIRST // 2) as k:
                for b in range(2):
                    for f in range(len(FS_CH)):
                        gate_times_up(k * 2 + b, f)
                    dve.wait_ge(sh_loaded[b], k * 32 + 32)
                    add_shared(k * 2 + b, b)

            t_bank = psum_b[0]
            dve.wait_ge(ids_loaded, 16)
            V.tensor_copy(id_rows[:, :], zero_id[:, :]).then_inc(ids_float, 1)
            dve.wait_ge(ids_turned, 1)
            link(V.tensor_copy(ids_col[:, :], psum_b[3][:, 0:SLOTS]))

            def index_out(j, b, k):
                if not (isinstance(j, int) and j < 2):
                    dve.wait_ge(g_loaded[b], k * 16)
                V.tensor_copy(gather_ix[:, b:b + 1], ids_col[:, bass.ds(j, 1)]).then_inc(g_ix, 1)

            def rows_turned(j, b):
                dve.wait_ge(t_full, j + 1)
                V.tensor_copy(zg_t[:, b, :], t_bank[:, :]).then_inc(t_out, 1)

            def gated(j, b):
                dve.wait_ge(g_silu, j + 1)
                V.tensor_tensor(silu[:, b, :], silu[:, b, :], psum_a[:, (2 * b + 1) * BANK:(2 * b + 1) * BANK + F], ALU.mult).then_inc(g_out, 1)

            index_out(0, 0, 0)
            index_out(1, 1, 0)
            rows_turned(0, 0)
            for j in range(2):
                index_out(j + 2, j, 1)
                rows_turned(j + 1, 1 - j)
                gated(j, j)
            with dve.Fori(1, SLOTS // 2 - 1) as k:
                for b in range(2):
                    j = k * 2 + b
                    index_out(j + 2, b, k + 1)
                    rows_turned(j + 1, 1 - b)
                    gated(j, b)
            rows_turned(SLOTS - 1, 1)
            gated(SLOTS - 2, 0)
            gated(SLOTS - 1, 1)

            def combine(n, b, k):
                dve.wait_ge(cb_loaded[b], k * 16 + 16)
                dve.wait_ge(c_loaded[b], k * 32 + 32)
                link(V.scalar_tensor_tensor(out=comb[2][:, b, :], in0=comb[0][:, b, :], scalar=top_w[:, bass.ds(n, 1), 0],
                                            in1=comb[2][:, b, :], op0=ALU.mult, op1=ALU.add))
                if not (isinstance(n, int) and n < 2):
                    dve.wait_ge(out_stored[b], k * 16)
                V.scalar_tensor_tensor(out=comb_out[:, b, :], in0=comb[1][:, b, :], scalar=top_w[:, bass.ds(n, 1), 1],
                                       in1=comb[2][:, b, :], op0=ALU.mult, op1=ALU.add).then_inc(c_done, 1)

            n = 0
            for i in range(SHARED_FIRST, NB):
                for f in range(len(FS_CH)):
                    gate_times_up(i, f)
                    combine(n, n % 2, n // 2)
                    n += 1
                dve.wait_ge(sh_loaded[i % 2], (i // 2) * 32 + 32)
                add_shared(i, i % 2)
            while n < NT:
                combine(n, n % 2, n // 2)
                n += 1

        @block.gpsimd
        def _(pool):
            own_ = Chain(pool, pool_own)
            link, mark = own_.link, own_.mark
            G = nc.gpsimd

            def inverse_std(col, n):
                pool.wait_ge(stat_ready, n)
                settle(pool)
                link(G.tensor_scalar_add(var_eps[:, col:col + 1], mv[:, col, 1:2], EPS))
                G.tensor_tensor(rstd[:, col:col + 1], var_eps[:, col:col + 1], neg_half[:, :], ALU.pow).then_inc(rstd_ready, 1)

            mark(G.memset(ident[:, :], 0.0))
            mark(G.memset(neg_half[:, :], -0.5))
            mark(G.memset(ones3[:, :], 1.0))
            link(G.memset(bias3[:, :], 0.0))
            G.affine_select(out=ident[:, :], in_=ident[:, :], compare_op=ALU.not_equal, fill=1.0, base=0,
                            pattern=[[-1, P]], channel_multiplier=1).then_inc(ident_ready, 1)
            for n in range(SUB):
                inverse_std(n, n + 1)
            mark(G.memset(onehot[:, :], 1.0))
            mark(G.memset(other[:, :, :], 1.0))
            link(G.memset(own[:, :], 1.0))
            for tile, dims in ((onehot, [[1, P]]), (other, [[0, UG], [1, P]])):
                link(G.affine_select(out=tile[:], in_=tile[:], compare_op=ALU.is_ge, fill=0.0, base=0, pattern=dims, channel_multiplier=-H))
                link(G.affine_select(out=tile[:], in_=tile[:], compare_op=ALU.is_ge, fill=0.0, base=H - 1,
                                     pattern=[[-st, n] for st, n in dims], channel_multiplier=H))
            link(G.affine_select(out=own[:, :], in_=own[:, :], compare_op=ALU.is_ge, fill=0.0, base=0, pattern=[[-H, GT]], channel_multiplier=1))
            link(G.affine_select(out=own[:, :], in_=own[:, :], compare_op=ALU.is_ge, fill=0.0, base=H - 1, pattern=[[H, GT]], channel_multiplier=-1))
            G.tensor_scalar(other[:, :, :], other[:, :, :], 1.0, -MASKED, ALU.subtract, ALU.mult).then_inc(const_ready, 1)

            def body(i, ahead2):
                if ahead2:
                    for s in range(SUB):
                        inverse_std(s, stat_no(i + 2, 0, s))
                for s in range(SUB):
                    pool.wait_ge(pr_ready, i * SUB + (s + 1))
                    for u in range(NU):
                        G.tensor_tensor(spread[:, s, u * UG:(u + 1) * UG, :].rearrange("p r (t g) -> p r t g", t=GT),
                                        pr[:, s, u * UG:(u + 1) * UG, :].unsqueeze(2).broadcast_to([P, UG, GT, H]),
                                        own[:, :].unsqueeze(1).unsqueeze(3).broadcast_to([P, UG, GT, H]), ALU.mult).then_inc(spread_ready, 1)
                for s in range(SUB):
                    inverse_std(SUB + s, stat_no(i, 1, s))

            for n in range(SUB):
                inverse_std(n, SUB + n + 1)
            body(0, True)
            POOL_SIGNALS = 2 * SUB
            with pool.Fori(1, NB - 2) as i:
                own_.enter(i - 1, POOL_SIGNALS)
                body(i, True)
            own_.leave(NB - 3)
            body(NB - 2, False)
            body(NB - 1, False)

            pool.wait_ge(x1_stored, 16 * NB)
            pool.wait_ge(z_stored, 16 * NB)
            pool.wait_ge(zt_stored, 16 * NB)
            wait_drained(pool, "LT", NB)
            mark(G.iota(iota_e[:, :], [[1, E]], base=0, channel_multiplier=0, allow_small_or_imprecise_dtypes=True))
            mark(G.iota(iota_slot[:, :], [[1, SLOTS]], base=0, channel_multiplier=0, allow_small_or_imprecise_dtypes=True))
            mark(G.iota(iota_rows[:, :], [[P, NT]], base=0, channel_multiplier=0, allow_small_or_imprecise_dtypes=True))
            mark(G.iota(tok_id[:, :], [[P, NT]], base=0, channel_multiplier=1))
            mark(G.memset(zero_id[:, :], 0))
            mark(G.memset(ones_b[:, :], 1.0))
            link(G.memset(upper[:, :], 1.0))
            G.affine_select(out=upper[:, :], in_=upper[:, :], compare_op=ALU.is_gt, fill=0.0, base=0,
                            pattern=[[1, P]], channel_multiplier=-1).then_inc(const2_ready, 1)
            pool.wait_ge(r_pos, 1)
            pool.wait_ge(zero_stored, 16)

            def stage(n, b):
                link(G.tensor_copy(pos_ix[:, b, :], pos[:, :, bass.ds(n, 1)].rearrange("p k o -> p (k o)")))

            def scatter(n, b, k):
                if not (isinstance(k, int) and k == 0):
                    pool.wait_ge(ids_scattered[b], k * (16 * TOPK))
                mark(G.tensor_copy(tok_ix[:, b:b + 1], tok_id[:, bass.ds(n, 1)]))
                stage(n, b)
                settle(pool)
                for pick in range(TOPK):
                    pool.indirect_dma_start(out=token_d[:, :], out_offset=bass.IndirectOffsetOnAxis(ap=pos_ix[:, b, pick:pick + 1], axis=0),
                                            in_=tok_ix[:, b:b + 1], in_offset=None).then_inc(ids_scattered[b], 16)

            for b in range(STAGES):
                scatter(b, b, 0)
            with pool.Fori(1, NT // STAGES) as k:
                own_.enter(k - 1, 2 * STAGES)
                for b in range(STAGES):
                    scatter(k * STAGES + b, b, k)
            own_.leave(NT // STAGES - 1)

            for b in range(STAGES):
                pool.wait_ge(ids_scattered[b], 16 * TOPK * NT // STAGES)
            pool.dma_start(zero_id[:, :], token_d.rearrange("(j p) o -> j (p o)", p=P)).then_inc(ids_loaded, 16)

            def gather(j, b):
                pool.wait_ge(g_ix, j + 1)
                if not (isinstance(j, int) and j < 2):
                    pool.wait_ge(t_full, j - 1)
                settle(pool)
                pool.indirect_dma_start(out=zg[:, b, :], out_offset=None, in_=z_d[:, :],
                                        in_offset=bass.IndirectOffsetOnAxis(ap=gather_ix[:, b:b + 1], axis=0)).then_inc(g_loaded[b], 16)

            gather(0, 0)
            gather(1, 1)
            with pool.Fori(1, SLOTS // 2) as k:
                for b in range(2):
                    gather(k * 2 + b, b)

            for b in range(2):
                pool.wait_ge(y_stored[b], 16 * (SLOTS // 2))

            def fetch(n, b):
                if not (isinstance(n, int) and n < 2):
                    pool.wait_ge(c_done, n - 1)
                stage(n, b)
                settle(pool)
                for pick in range(TOPK):
                    pool.indirect_dma_start(out=comb[pick][:, b, :], out_offset=None, in_=y_d[:, :],
                                            in_offset=bass.IndirectOffsetOnAxis(ap=pos_ix[:, b, pick:pick + 1], axis=0)).then_inc(c_loaded[b], 16)

            fetch(0, 0)
            fetch(1, 1)
            with pool.Fori(1, NT // 2) as k:
                own_.enter(k - 1, 2)
                for b in range(2):
                    fetch(k * 2 + b, b)
            own_.leave(NT // 2 - 1)


_INS = ["x", "ctx_t", "wq_t", "bq", "wk_t", "bk", "wv_t", "bv", "wo_t", "bo", "wgate_t", "wgu_t", "wdn_t", "wsgu_t", "wsdn_t"]


_OUT = ((16, 256, 512), "float32")


def kernel(**inputs):
    import numpy as _np
    import concourse.bacc as _bacc
    from concourse import mybir as _mybir
    from concourse.bass_utils import run_bass_kernel_spmd as _run

    given = {k.replace("L0_xattn_", "").replace("L0_ffn_", ""): _np.asarray(v) for k, v in inputs.items()}
    arrays = {
        "x": given["x"].reshape(T, D),
        "ctx_t": given["ctx_2048"].reshape(T, D).T,
        "wq_t": given["Wq"].T, "bq": given["bq"],
        "wk_t": given["Wk"].T, "bk": given["bk"],
        "wv_t": given["Wv"].T, "bv": given["bv"],
        "wo_t": given["Wo"].T, "bo": given["bo"],
        "wgate_t": given["gate_weight"].T,
        "wgu_t": given["gate_up_weights"].transpose(2, 0, 1),
        "wdn_t": given["down_weights"].transpose(2, 0, 1),
        "wsgu_t": given["shared_gate_up"].T,
        "wsdn_t": given["shared_down"].T,
    }
    arrays = {f"in_{k}": _np.ascontiguousarray(v) for k, v in arrays.items()}
    nc = _bacc.Bacc("TRN2", target_bir_lowering=False, num_devices=1)
    args = [nc.dram_tensor(f"in_{k}", arrays[f"in_{k}"].shape, _mybir.dt.from_np(arrays[f"in_{k}"].dtype), kind="ExternalInput").ap()
            for k in _INS]
    out = nc.dram_tensor("out_rows", (T, D), _mybir.dt.from_np(_np.dtype(_OUT[1])), kind="ExternalOutput").ap()
    build(nc, *args, out)
    r = _run(nc, [arrays], core_ids=[0])
    return r.results[0]["out_rows"].reshape(_OUT[0])
```

```python
from contextlib import ExitStack

import concourse.bass as bass
from concourse import mybir

F32 = mybir.dt.float32
F32R = mybir.dt.float32r
BF16 = mybir.dt.bfloat16
F16 = mybir.dt.float16
U32 = mybir.dt.uint32
I32 = mybir.dt.int32
ALU = mybir.AluOpType
ACT = mybir.ActivationFunctionType
X = mybir.AxisListType.X

P = 128
D = 512
KC = D // P
H, HD = 16, 32
T = 16 * 256
NT = T // P
SUB = 2
BT = SUB * P
NB = T // BT
GT = P // H
NG = P // GT
UG = 4
NU = NG // UG
E, F = 8, 352
FS = 704
TOPK = 2
EPS = 1e-5
BANK = 512
SLOTS = T * TOPK // P + E
SH_STEPS = 8
UNIT = 2 * KC * 2 * F
CONVERT_FROM = 6
F_CH = [(0, 128), (128, 128), (256, 96)]
FS_CH = [(i * P, min(P, FS - i * P)) for i in range((FS + P - 1) // P)]
GB = 3
SHARED_FIRST = 12
TAIL_TILES = [6, 8, 8, 8]
CB = 4
STAGES = 4
MASKED = -(2.0 ** 120)
HI, LO = 0, 1
Z_EXP, W_EXP = 11, 14
EXPONENT = 0x7F800000
SMALLEST = 32

AHEAD = [("X0", "B0"), ("X1", "B1")]
AHEAD_KQ = [("K0", "B2"), ("K1", "B3"), ("Q0", "B0"), ("Q1", "B1")]
AHEAD_V = [("V0", "B2"), ("V1", "B3")]
BEHIND = [("Z0", "B3"), ("Z1", "B0")]
ROUTE = [("L", "B0")]
TURN_ROUTE = [("LT", "B0")]
SCORES = [(f"S{s}{u}", f"A{(u + 2) % NU}") for s in range(SUB) for u in range(NU)]
TURN_V = [("VT0", "B1"), ("VT1", "B3")]
TURN_W = [[(f"T{s}{u}", f"A{(u + 2) % NU}") for u in range(NU)] for s in range(SUB)]
FULL_PASS = (AHEAD + SCORES + AHEAD_KQ + TURN_W[0] + AHEAD_V[:1] + BEHIND + TURN_V[:1] + TURN_W[1] + TURN_V[1:] + ROUTE
             + [("P0", "A0"), ("P1", "A1"), AHEAD_V[1]] + TURN_ROUTE + [("O0", "B1"), ("O1", "B2")])
BANK_OF = dict(FULL_PASS)
IS_AHEAD = {name for name, _ in AHEAD + AHEAD_KQ + AHEAD_V}
IS_BEHIND = {name for name, _ in BEHIND + ROUTE + TURN_ROUTE}


def steps_of(i):
    names = [name for name, _ in FULL_PASS]
    if i < 0:
        return [n for n in names if n in IS_AHEAD]
    if i == NB:
        return [n for n in names if n in IS_BEHIND]
    return [n for n in names if not (i == 0 and n in IS_BEHIND) and not (i == NB - 1 and n in IS_AHEAD)]


def earlier_fills(step, i):
    mine = {name for name, bank in FULL_PASS if bank == BANK_OF[step]}
    if isinstance(i, int):
        whole = sum(n in mine for p in range(-1, i) for n in steps_of(p))
        names = steps_of(i)
        return whole + sum(n in mine for n in names[:names.index(step)])
    return (i - 1) * len(mine) + earlier_fills(step, 1)


class Chain:

    def __init__(self, engine, sem):
        self.engine, self.sem, self.n, self.passes = engine, sem, 0, 0

    def enter(self, passes, per_pass):
        self.passes, self.start, self.per_pass = passes * per_pass, self.n, per_pass

    def leave(self, count):
        assert self.n - self.start == self.per_pass, (self.n - self.start, self.per_pass)
        self.n, self.passes = self.start + count * self.per_pass, 0

    def mark(self, instruction):
        self.n += 1
        return instruction.then_inc(self.sem, 1)

    def wait(self):
        self.engine.wait_ge(self.sem, self.passes + self.n)

    def link(self, instruction):
        self.mark(instruction)
        self.wait()


def build(nc, x, ctx_t, wq_t, bq, wk_t, bk, wv_t, bv, wo_t, bo, wgate_t, wgu_t, wdn_t, wsgu_t, wsdn_t, out):
    with ExitStack() as whole:
        def sem(name):
            return whole.enter_context(nc.semaphore(name))

        def dram(name, shape, dt):
            return nc.dram_tensor(name, shape, dt).ap()

        z_d = dram("z_rows", [T, D], F32)
        zt_d = dram("z_columns", [NB, P, 2 * KC, BT], F16)
        x1_d = dram("x1_rows", [T, D], F32)
        base_d = dram("base_rows", [T, D], F32)
        y_d = dram("expert_rows", [SLOTS * P, D], F32)
        token_d = dram("slot_tokens", [SLOTS * P, 1], I32)

        def sb(name, shape, dt, stack=whole):
            return stack.enter_context(nc.sbuf_tensor(name, shape, dt))

        psum_a = whole.enter_context(nc.psum_tensor("psum_a", [P, NU * BANK], F32))
        psum_b = [whole.enter_context(nc.psum_tensor(f"psum_b{i}", [P, BANK], F32)) for i in range(4)]

        def bank_ap(step):
            kind, i = BANK_OF[step][0], int(BANK_OF[step][1])
            return psum_a[:, i * BANK:(i + 1) * BANK] if kind == "A" else psum_b[i][:, :]

        ident = sb("ident", [P, P], F32)
        tok_scores = sb("tok_scores", [P, NT, E], F32)
        ids_col = sb("ids_col", [P, SLOTS], I32)
        pos = sb("pos", [P, TOPK, NT], U32)
        top_w = sb("top_w", [P, NT, 8], F32)
        slot_expert = sb("slot_expert", [P, SLOTS], I32)
        ws_scale, w_scale = sb("ws_scale", [P, 4], F32), sb("w_scale", [P, 4], F32)

        early = ExitStack()
        x_sb = sb("x_sb", [P, SUB, D], F32, early)
        cx_in = sb("cx_in", [P, KC, BT], F32, early)
        cx_t = sb("cx_t", [P, 2, KC, BT], F32R, early)
        early.close()
        zt_in = sb("zt_in", [P, 2, 2, KC, BT], F16)
        base = sb("base", [P, 2, SUB, D], F32)

        one = ExitStack()
        wq = sb("wq", [P, 2, KC, D], F32R, one)
        wk = sb("wk", [P, 2, KC, D], F32R, one)
        wv = sb("wv", [P, 2, KC, D], F32R, one)
        wo = sb("wo", [P, 2, KC, D], F32R, one)
        wgate = sb("wgate", [P, KC, E], F32, one)
        bias3 = sb("bias3", [P, 4 * D], BF16, one)
        ones3 = sb("ones3", [P, BT], BF16, one)
        onehot = sb("onehot", [GT, P], BF16, one)
        other = sb("other", [GT, P], BF16, one)
        own = sb("own", [P, GT], F32, one)
        neg_half = sb("neg_half", [P, 1], F32, one)
        x_res = sb("x_res", [P, SUB, D], F32, one)
        xn = sb("xn", [P, SUB, D], F32, one)
        xn_t = sb("xn_t", [P, 2, KC, BT], F32R, one)
        v_at = 2 * HD
        qv_t = sb("qv_t", [v_at + HD, BT, H], F32, one)
        q_t, q_masked, v_t = qv_t[0:HD], qv_t[0:HD + GT], qv_t[v_at:v_at + HD]
        k_masked = sb("k_masked", [HD + GT, BT, H], F32, one)
        k_t = k_masked[0:HD]
        v_p = sb("v_p", [P, SUB * NG, HD], F32, one)
        sc = sb("sc", [P, SUB, NG, H], F32, one)
        ex = sc
        pr = sb("pr", [P, SUB, NG, H], F32, one)
        row_max = sb("row_max", [P, SUB, NG], F32, one)
        row_sum = sb("row_sum", [P, SUB, NG], F32, one)
        row_inv = sb("row_inv", [P, SUB, NG], F32, one)
        spread = sb("spread", [P, SUB, NG, P], F32, one)
        spread_t = sb("spread_t", [P, SUB, NG * P], F32, one)
        at_t = xn_t
        x1 = sb("x1", [P, SUB, D], F32, one)
        z = sb("z", [P, SUB, D], F32, one)
        z_t = sb("z_t", [P, KC, BT], F32, one)
        z_parts = sb("z_parts", [P, 2, KC, BT], F16, one)
        logits_t = sb("logits_t", [E, BT], F32, one)
        stats = sb("stats", [P, 2 * SUB, 6], F32, one)
        mv = sb("mv", [P, 2 * SUB, 2], F32, one)
        var_eps = sb("var_eps", [P, 2 * SUB], F32, one)
        rstd = sb("rstd", [P, 2 * SUB], F32, one)
        at_raw = z[:, :, :].rearrange("p s (c t) -> p (s c) t", t=BT)
        ws_rep = xn[:, 0, 0:P]
        w_in = ([spread[:, s].rearrange("p (c r) n -> p c (r n)", c=KC) for s in range(SUB)]
                + [spread_t[:, s].rearrange("p (c n) -> p c n", c=KC) for s in range(SUB)])
        wk_in, wq_in, wv_in, wo_in = w_in
        b_raw = [x1[0:3, 0, :], x1[0:3, 1, :], z[0:3, 0, :], z[0:3, 1, :]]
        b_rest = z_t[0:3, 0:2, :].rearrange("p c t -> p (c t)")
        b_part = [z_t[0:3, 2:4, :].rearrange("p c t -> p (c t)"), z_parts[0:3, 0].rearrange("p c t -> p (c t)").bitcast(F32)]
        b_bf = z_parts[0:3, 1, 0:2].rearrange("p c t -> p (c t)").bitcast(BF16)
        one.close()

        wsgu = sb("wsgu", [P, 2, KC, 2 * FS], F16)
        wsgu_place = ExitStack()
        wsgu_in = sb("wsgu_in", [P, KC, 2 * FS], F32, wsgu_place)
        wsgu_place.close()
        wsdn = sb("wsdn", [P, len(FS_CH), D], F32)

        two = ExitStack()
        wgu_place = ExitStack()
        wgu_in = sb("wgu_in", [P, E + 1, KC, 2 * F], F32, wgu_place)
        wgu_place.close()
        wgu = sb("wgu", [P, E * UNIT], F16, two)
        wdn = sb("wdn", [P, len(F_CH), E * D], F32, two)
        gather_ix = sb("gather_ix", [P, 2], I32, two)
        pos_ix = sb("pos_ix", [P, STAGES, TOPK], U32, two)
        tok_ix = sb("tok_ix", [P, STAGES], I32, two)

        three = ExitStack()
        gate_act = sb("gate_act", [P, GB, BT], F32, three)
        sh_t = sb("sh_t", [P, len(FS_CH), BT], F32, three)
        iota_e = sb("iota_e", [P, E], F32, three)
        iota_slot = sb("iota_slot", [P, SLOTS], F32, three)
        iota_rows = sb("iota_rows", [P, NT], F32, three)
        tok_id = sb("tok_id", [P, NT], I32, three)
        zero_id = sb("zero_id", [SLOTS, P], I32, three)
        id_rows = sb("id_rows", [SLOTS, P], F32, three)
        upper = sb("upper", [P, P], BF16, three)
        ones_b = sb("ones_b", [P, P], BF16, three)
        d_m = sb("d_m", [P, NT], F32, three)
        d_s = sb("d_s", [P, NT, E], F32, three)
        d_ixf = sb("d_ixf", [P, TOPK, NT], F32, three)
        cnt_b = sb("cnt_b", [P, NT, E], BF16, three)
        tot = sb("tot", [P, NT, E], F32, three)
        run = sb("run", [P, NT, E], F32, three)
        rank = sb("rank", [P, NT, E], F32, three)
        tiles_of = sb("tiles_of", [P, 4, E], F32, three)
        posf = sb("posf", [P, TOPK, NT], F32, three)
        slot_f = sb("slot_f", [P, SLOTS], F32, three)
        ones_f = sb("ones_f", [P, NT], F32, three)
        w_max = d_m[:, 0:2 * E]
        w_rep = d_s[:, :, :].rearrange("p n e -> p (n e)")[:, 0:P]
        spare = wdn[:, 1, :]
        n_picked, n_wide = TOPK * NT * E, SLOTS * E
        picked = spare[:, 0:n_picked].rearrange("p (k n e) -> p k n e", k=TOPK, n=NT)
        wide = spare[:, n_picked:n_picked + n_wide].rearrange("p (j e) -> p j e", e=E)
        d_ix = spare[:, n_picked + n_wide:n_picked + n_wide + NT * 8].bitcast(U32).rearrange("p (n e) -> p n e", e=8)
        three.close()

        four = ExitStack()
        zg = sb("zg", [P, 2, D], F32, four)
        zg_t = sb("zg_t", [P, 2, 2, D], F16, four)
        silu = sb("silu", [P, 2, F], F32, four)
        act_t = sb("act_t", [P, 2, 3 * P], F32, four)
        y_sb = sb("y_sb", [P, 2, D], F32, four)
        four.close()

        comb = [wgu_in[:, i].rearrange("p c n -> p (c n)")[:, 0:CB * D].rearrange("p (b d) -> p b d", b=CB) for i in range(4)]
        comb_out = comb[3]
        two.close()

        ident_ready = sem("ident_ready")
        const_ready = sem("const_ready")
        mask_ready = sem("mask_ready")
        wk_loaded, wq_loaded, wv_loaded, wo_loaded, ws_loaded = (sem(f"{n}_loaded") for n in ("wk", "wq", "wv", "wo", "ws"))
        bias_loaded = sem("bias_loaded")
        bias_ready = sem("bias_ready")
        x_loaded = sem("x_loaded")
        res_loaded = sem("res_loaded")
        x1_stored = sem("x1_stored")
        zt_stored = sem("zt_stored")
        cx_loaded = sem("cx_loaded")
        wk_split, wq_split, wv_split, wo_split = (sem(f"{n}_split") for n in ("wk", "wq", "wv", "wo"))
        cx_split = sem("cx_split")
        xt_high = sem("xt_high")
        w_high = sem("w_high")
        at_split = sem("at_split")
        full = {b: sem(f"full_{b}") for b in sorted(set(BANK_OF.values()))}
        drained = {b: sem(f"drained_{b}") for b in full}
        xn_ready = sem("xn_ready")
        stat_ready = sem("stat_ready")
        rstd_ready = sem("rstd_ready")
        shifted = sem("shifted")
        exp_ready = sem("exp_ready")
        pr_ready = sem("pr_ready")
        spread_ready = sem("spread_ready")
        silu_ready = sem("silu_ready")
        sh_loaded = [sem("sh_loaded0"), sem("sh_loaded1")]
        sh_full = sem("sh_full")
        sh_out = sem("sh_out")
        z_ready = sem("z_ready")
        z_stored = sem("z_stored")
        base_stored = [sem("base_stored0"), sem("base_stored1")]
        dve_own = sem("dve_own")
        pool_own = sem("pool_own")

        def wait_full(eng, step, block):
            eng.wait_ge(full[BANK_OF[step]], earlier_fills(step, block) + 1)

        def wait_free(eng, step, block):
            n = earlier_fills(step, block)
            if not (isinstance(n, int) and n == 0):
                eng.wait_ge(drained[BANK_OF[step]], n)

        def wait_drained(eng, step, block):
            eng.wait_ge(drained[BANK_OF[step]], earlier_fills(step, block) + 1)

        waits_met = sem("waits_met")

        def settle(eng):
            eng.sem_inc(waits_met, 1)

        def low(eng, lo, whole_values, hi):
            return eng.tensor_tensor(lo, whole_values, hi.bitcast(F32), ALU.subtract)

        def tiles_after(f, tiles):
            return (f + 1) * tiles // len(FS_CH) - f * tiles // len(FS_CH)

        def sums_out(copy, s):
            step = f"P{s}"
            for q in range(4):
                dst = at_raw[:, :, s * P:(s + 1) * P].rearrange("p c (j q t) -> p q c j t", q=4, t=GT)[:, q]
                src = bank_ap(step)[HD * q:HD * (q + 1), :].rearrange("p (j t c l) -> p l c j t", t=GT, c=KC, l=4)
                for l in range(4):
                    last = copy(dst[HD * l:HD * (l + 1)], src[:, l])
            last.then_inc(drained[BANK_OF[step]], 1)

        def stat_no(i, which, s):
            if which == 0:
                return SUB * i + s + 1 if isinstance(i, int) and i < 2 else (i - 2) * (2 * SUB) + (2 * SUB + s + 1)
            missing = max(0, i - (NB - 3)) if isinstance(i, int) else 0
            return i * (2 * SUB) + (3 * SUB + s + 1 - SUB * missing)

        wsdn_loaded = sem("wsdn_loaded")
        ws_rep_ready, ws_rep_turned = sem("ws_rep_ready"), sem("ws_rep_turned")
        ws_scaled = sem("ws_scaled")
        ws_high, ws_low = sem("ws_high"), sem("ws_low")
        zt_high = sem("zt_high")
        wgu_loaded, wdn_loaded = sem("wgu_loaded"), sem("wdn_loaded")
        w_rep_ready, w_rep_turned = sem("w_rep_ready"), sem("w_rep_turned")
        w_high16 = sem("w_high16")
        w_low16 = sem("w_low16")
        zg_high = sem("zg_high")
        const2_ready = sem("const2_ready")
        r_shift = sem("r_shift")
        r_exp = sem("r_exp")
        r_cnt = sem("r_cnt")
        r_rank = sem("r_rank")
        r_ranked = sem("r_ranked")
        r_pos = sem("r_pos")
        zero_stored = sem("zero_stored")
        ids_scattered = [sem(f"ids_scattered{b}") for b in range(STAGES)]
        ids_loaded = sem("ids_loaded")
        ids_float, ids_turned = sem("ids_float"), sem("ids_turned")
        g_ix = sem("g_ix")
        g_loaded = [sem("g_loaded0"), sem("g_loaded1")]
        t_full, t_out = sem("t_full"), sem("t_out")
        g_full, g_silu, g_out = sem("g_full"), sem("g_silu"), sem("g_out")
        a_full, a_out = sem("a_full"), sem("a_out")
        d_full, d_out = sem("d_full"), sem("d_out")
        y_stored = [sem("y_stored0"), sem("y_stored1")]
        c_loaded = [sem(f"c_loaded{b}") for b in range(CB)]
        cb_loaded = [sem(f"cb_loaded{b}") for b in range(CB)]
        c_done = sem("c_done")
        out_stored = [sem(f"out_stored{b}") for b in range(CB)]

        block = whole.enter_context(nc.Block())

        cx_v = ctx_t.rearrange("(c p) t -> p c t", p=P)

        def rows(dram_ap, i):
            return dram_ap[bass.ds(i * BT, BT), :].rearrange("(s p) d -> p s d", p=P)

        @block.sync
        def _(sp):
            def load_x(i):
                sp.dma_start(x_sb[:, :, :], rows(x, i)).then_inc(x_loaded, 16)

            def load_res(i):
                sp.dma_start(x_res[:, :, :], rows(x, i)).then_inc(res_loaded, 16)

            def load_cx(i):
                sp.dma_start(cx_in[:, :, :], cx_v[:, :, bass.ds(i * BT, BT)]).then_inc(cx_loaded, 16)

            def load_w(w, src, done):
                sp.dma_start(w, src.rearrange("(c p) n -> p c n", p=P)).then_inc(done, 16)

            load_x(0)
            load_cx(0)
            load_w(wk_in, wk_t, wk_loaded)
            load_w(wq_in, wq_t, wq_loaded)
            load_w(wv_in, wv_t, wv_loaded)
            load_res(0)
            sp.wait_ge(xn_ready, SUB)
            load_x(1)
            load_w(wo_in, wo_t, wo_loaded)
            load_w(wgate[:, :, :], wgate_t, wo_loaded)
            sp.wait_ge(cx_split, 1)
            load_cx(1)
            sp.wait_ge(xn_ready, 2 * SUB)
            load_x(2)
            sp.wait_ge(cx_split, 2)
            load_cx(2)

            def store_columns(i):
                wait_drained(sp, "Z0", i)
                settle(sp)
                wait_drained(sp, "Z1", i)
                settle(sp)
                sp.dma_start(zt_d[bass.ds(i - 1, 1)].rearrange("o p c t -> p (o c t)"), z_parts[:, :, :, :].rearrange("p h c t -> p (h c t)")).then_inc(zt_stored, 16)

            def body(i, behind, ahead, ahead2, ahead3):
                if behind:
                    store_columns(i)
                if ahead3:
                    sp.wait_ge(xn_ready, (i + 2) * SUB + SUB)
                    load_x(i + 3)
                if ahead3:
                    sp.wait_ge(cx_split, i + 3)
                    settle(sp)
                    load_cx(i + 3)
                wait_drained(sp, "O1", i)
                settle(sp)
                if ahead:
                    load_res(i + 1)
                sp.dma_start(rows(x1_d, i), x1[:, :, :]).then_inc(x1_stored, 16)
                sp.wait_ge(z_ready, i * SUB + SUB)
                settle(sp)
                sp.dma_start(rows(z_d, i), z[:, :, :]).then_inc(z_stored, 16)

            def load_block(i, b):
                sp.dma_start(zt_in[:, b].rearrange("p h c t -> p (h c) t"), zt_d[bass.ds(i, 1)].rearrange("o p c t -> p (o c) t")).then_inc(sh_loaded[b], 16)
                sp.dma_start(base[:, b, :, :], rows(x1_d, i)).then_inc(sh_loaded[b], 16)

            body(0, False, True, True, True)
            with sp.Fori(1, NB - 3) as i:
                body(i, True, True, True, True)
            body(NB - 3, True, True, True, False)
            body(NB - 2, True, True, False, False)
            wait_full(sp, "V1", NB - 2)
            load_w(wsgu_in[:, :, :], wsgu_t, ws_loaded)
            sp.wait_ge(cx_split, NB)
            sp.wait_ge(xn_ready, NB * SUB)
            sp.wait_ge(zt_stored, 16 * 2)
            sp.wait_ge(x1_stored, 16 * 2)
            load_block(0, 0)
            load_block(1, 1)
            body(NB - 1, True, False, False, False)
            sp.wait_ge(ws_low, KC)
            whole_ch = FS // P
            load_w(wsdn[:, 0:whole_ch, :], wsdn_t[0:whole_ch * P, :], wsdn_loaded)
            sp.dma_start(wsdn[0:FS - whole_ch * P, whole_ch, :], wsdn_t[whole_ch * P:FS, :]).then_inc(wsdn_loaded, 16)
            store_columns(NB)
            sp.wait_ge(x1_stored, 16 * NB)
            sp.wait_ge(z_stored, 16 * NB)
            sp.wait_ge(zt_stored, 16 * NB)
            wait_drained(sp, "LT", NB)

            def store_base(i, b, k, more):
                sp.wait_ge(sh_out, i * SH_STEPS + SH_STEPS)
                settle(sp)
                sp.dma_start(rows(base_d, i), base[:, b, :, :]).then_inc(base_stored[b], 16)
                if more:
                    sp.wait_ge(base_stored[b], k * 16 + 16)
                    settle(sp)
                    load_block(i + 2, b)

            for e in range(E):
                sp.dma_start(wgu_in[:, e + 1], wgu_t[:, e, :].rearrange("(c p) n -> p c n", p=P)).then_inc(wgu_loaded, 16)
            sp.wait_ge(const2_ready, 1)
            sp.dma_start(token_d.rearrange("(j p) o -> j (p o)", p=P), zero_id[:, :]).then_inc(zero_stored, 16)
            converted = CONVERT_FROM + E // 2
            with sp.Fori(0, converted // 2) as k:
                for b in range(2):
                    store_base(k * 2 + b, b, k, True)
            sp.wait_ge(w_low16, 1 + 2 * E)
            for f, (f0, fn) in enumerate(F_CH):
                sp.dma_start(wdn[0:fn, f, :], wdn_t[f0:f0 + fn].rearrange("p e n -> p (e n)")).then_inc(wdn_loaded, 16)
            for i in range(converted, SHARED_FIRST):
                store_base(i, i % 2, i // 2, True)
            with sp.Fori(0, SLOTS // 2) as k:
                for b in range(2):
                    j = k * 2 + b
                    sp.wait_ge(d_out, j + 1)
                    settle(sp)
                    sp.dma_start(y_d[bass.ds(j * P, P), :], y_sb[:, b, :]).then_inc(y_stored[b], 16)
            def store_out(n, b):
                sp.wait_ge(c_done, n + 1)
                settle(sp)
                sp.dma_start(out[bass.ds(n * P, P), :], comb_out[:, b, :]).then_inc(out_stored[b], 16)

            n = 0
            for i, tiles in zip(range(SHARED_FIRST, NB), TAIL_TILES):
                for _ in range(tiles):
                    store_out(n, n % CB)
                    n += 1
                store_base(i, i % 2, i // 2, i + 2 < NB)
            while n < NT:
                store_out(n, n % CB)
                n += 1
            for b in range(CB):
                sp.wait_ge(out_stored[b], 16 * (NT // CB))

        @block.tensor
        def _(pe):
            def mm(o, l, r, start, stop):
                return nc.tensor.matmul(o, l, r, start=start, stop=stop)

            PARTS = ((HI, HI), (HI, LO), (LO, HI))

            def project(name, w, src, part, i, chunks):
                for c in chunks:
                    step = f"{name}{c // 2}"
                    if c % 2 == 0:
                        wait_free(pe, step, i)
                    oc = bank_ap(step)[:, c % 2 * BT:(c % 2 + 1) * BT]
                    for kc in range(KC):
                        for wp, sp_ in PARTS:
                            mm(oc, w[:, wp, kc, c * P:(c + 1) * P], src[:, sp_, kc, :],
                               kc == 0 and (wp, sp_) == PARTS[0], False)
                    if isinstance(i, int) and i < 0 and c == 0:
                        pe.wait_ge(bias_ready, {"K": 1, "Q": 2, "V": 3}[name])
                    last = mm(oc, bias3[:, part * D + c * P:part * D + (c + 1) * P], ones3[:, :], False, True)
                    if c % 2 == 1:
                        last.then_inc(full[BANK_OF[step]], 1)

            def turn_x(i):
                for s in range(SUB):
                    step = f"X{s}"
                    wait_free(pe, step, i)
                    pe.wait_ge(xn_ready, (i + 1) * SUB + (s + 1))
                    for kc in range(KC):
                        last = nc.tensor.transpose(bank_ap(step)[:, kc * P:(kc + 1) * P], xn[:, s, kc * P:(kc + 1) * P], ident[:, :])
                    last.then_inc(full[BANK_OF[step]], 1)

            def project_k(i, chunks):
                if chunks[0] == 0:
                    pe.wait_ge(cx_split, i + 2)
                project("K", wk, cx_t, 1, i, chunks)

            def project_q(i, chunks):
                if chunks[0] == 0:
                    wait_drained(pe, "X0", i)
                    wait_drained(pe, "X1", i)
                project("Q", wq, xn_t, 0, i, chunks)

            def turn_z(i):
                for s in range(SUB):
                    step = f"Z{s}"
                    wait_free(pe, step, i)
                    pe.wait_ge(z_ready, (i - 1) * SUB + (s + 1))
                    for kc in range(KC):
                        last = nc.tensor.transpose(bank_ap(step)[:, kc * P:(kc + 1) * P], z[:, s, kc * P:(kc + 1) * P], ident[:, :])
                    last.then_inc(full[BANK_OF[step]], 1)

            def route(i):
                wait_free(pe, "L", i)
                wait_drained(pe, "Z0", i)
                wait_drained(pe, "Z1", i)
                for kc in range(KC):
                    last = mm(bank_ap("L")[0:E, 0:BT], wgate[:, kc, :], z_t[:, kc, :], kc == 0, kc == KC - 1)
                last.then_inc(full[BANK_OF["L"]], 1)

            def turn_logits(i):
                wait_free(pe, "LT", i)
                settle(pe)
                for s in range(SUB):
                    last = nc.tensor.transpose(bank_ap("LT")[:, s * E:(s + 1) * E], logits_t[:, s * P:(s + 1) * P], ident[0:E, 0:E])
                last.then_inc(full[BANK_OF["LT"]], 1)

            def scores(s, i, us):
                for u in us:
                    step = f"S{s}{u}"
                    o = bank_ap(step)
                    wait_free(pe, step, i)
                    for g in range(UG):
                        t0 = s * P + (u * UG + g) * GT
                        last = mm(o[:, g * P:(g + 1) * P], q_masked[:, t0:t0 + GT, :], k_masked[:, t0:t0 + GT, :], True, True)
                    last.then_inc(full[BANK_OF[step]], 1)

            def v_pairs(s, i):
                step = f"VT{s}"
                wait_free(pe, step, i)
                settle(pe)
                for g in range(NG):
                    t0 = s * P + g * GT
                    last = nc.tensor.transpose(bank_ap(step)[:, g * HD:(g + 1) * HD], v_t[:, t0:t0 + GT, :], ident[v_at:v_at + HD, v_at:v_at + HD])
                last.then_inc(full[BANK_OF[step]], 1)

            def transpose_weights(s, i):
                for u in range(NU):
                    step = f"T{s}{u}"
                    wait_free(pe, step, i)
                    pe.wait_ge(spread_ready, i * (SUB * NU) + (s * NU + u + 1))
                    for g in range(UG):
                        last = nc.tensor.transpose(bank_ap(step)[:, g * P:(g + 1) * P], spread[:, s, u * UG + g, :], ident[:, :])
                    last.then_inc(full[BANK_OF[step]], 1)

            def attend(s, i):
                step = f"P{s}"
                wait_free(pe, step, i)
                if s == 0:
                    for u in range(NU):
                        wait_drained(pe, f"T1{u}", i)
                    wait_drained(pe, "VT0", i)
                    wait_drained(pe, "VT1", i)
                for g in range(NG):
                    q, j = g % 4, g // 4
                    last = mm(bank_ap(step)[HD * q:HD * (q + 1), j * P:(j + 1) * P], v_p[:, s * NG + g, :],
                              spread_t[:, s, g * P:(g + 1) * P], True, True)
                last.then_inc(full[BANK_OF[step]], 1)

            def project_out(s, i):
                step = f"O{s}"
                wait_free(pe, step, i)
                if isinstance(i, int) and i == NB - 1:
                    pe.wait_ge(ws_scaled, 1)
                pe.wait_ge(at_split, i * SUB + (s + 1))
                mm(bank_ap(step), ones3[:, 0:P], bias3[:, 3 * D:4 * D], True, False)
                for kc in range(KC):
                    for ap, wp in PARTS:
                        last = mm(bank_ap(step), at_t[:, ap, kc, s * P:(s + 1) * P], wo[:, wp, kc, :],
                                  False, kc == KC - 1 and (ap, wp) == PARTS[-1])
                last.then_inc(full[BANK_OF[step]], 1)

            def body(i, behind, ahead):
                if isinstance(i, int) and i == 0:
                    for step in ("Q0", "Q1"):
                        wait_drained(pe, step, -1)
                    scores(0, 0, (0,))
                if ahead:
                    turn_x(i)
                for n in range(SUB * NU):
                    if n + 1 < SUB * NU:
                        scores((n + 1) // NU, i, ((n + 1) % NU,))
                    if ahead:
                        (project_k if n < KC else project_q)(i, (n % KC,))
                transpose_weights(0, i)
                if ahead:
                    project("V", wv, cx_t, 2, i, (0, 1))
                if behind:
                    turn_z(i)
                if isinstance(i, int) and i == 0:
                    for step in ("V0", "V1"):
                        wait_drained(pe, step, -1)
                v_pairs(0, i)
                transpose_weights(1, i)
                v_pairs(1, i)
                if isinstance(i, int) and i == NB - 1:
                    wait_free(pe, "O1", i)
                    pe.wait_ge(ws_rep_ready, 1)
                    nc.tensor.transpose(bank_ap("O1")[:, 0:P], ws_rep, ident[:, :]).then_inc(ws_rep_turned, 1)
                if behind:
                    route(i)
                attend(0, i)
                attend(1, i)
                if ahead:
                    project("V", wv, cx_t, 2, i, (2, 3))
                if behind:
                    turn_logits(i)
                if isinstance(i, int) and i == 0:
                    wait_drained(pe, "Q0", 0)
                if ahead:
                    scores(0, i + 1, (0,))
                if isinstance(i, int) and i == 0:
                    pe.wait_ge(wo_split, 1)
                    pe.wait_ge(bias_ready, 4)
                project_out(0, i)
                project_out(1, i)

            pe.wait_ge(ident_ready, 1)
            turn_x(-1)
            pe.wait_ge(wk_split, 1)
            project_k(-1, range(KC))
            pe.wait_ge(wq_split, 1)
            project_q(-1, range(KC))
            pe.wait_ge(wv_split, 1)
            project("V", wv, cx_t, 2, -1, range(KC))
            pe.wait_ge(mask_ready, 2)
            pe.wait_ge(wo_loaded, 32)
            body(0, False, True)
            with pe.Fori(1, NB - 1) as i:
                body(i, True, True)
            def sh_bank(step):
                return psum_a[:, step * BANK:(step + 1) * BANK] if step < 4 else psum_b[step - 4][:, :]

            def sh_free(i, step):
                if not (isinstance(i, int) and i == 0):
                    pe.wait_ge(sh_out, (i - 1) * SH_STEPS + (step + 1))

            def gate_up(i, b, fs):
                for f in fs:
                    f0, fn = FS_CH[f]
                    sh_free(i, f)
                    for half in range(2):
                        for kc in range(KC):
                            for wp, zp in PARTS:
                                last = mm(sh_bank(f)[0:fn, half * BT:(half + 1) * BT], wsgu[:, wp, kc, half * FS + f0:half * FS + f0 + fn],
                                          zt_in[:, b, zp, kc, :], kc == 0 and (wp, zp) == PARTS[0], kc == KC - 1 and (wp, zp) == PARTS[-1])
                    last.then_inc(sh_full, 1)

            def down(i, b):
                n = len(FS_CH)
                for fs in (range(n - 1), range(n - 1, n)):
                    for s in range(SUB):
                        if fs[0] == 0:
                            sh_free(i, n + s)
                        for f in fs:
                            fn = FS_CH[f][1]
                            if s == 0:
                                pe.wait_ge(sh_out, i * SH_STEPS + (f + 1))
                            last = mm(sh_bank(n + s), sh_t[0:fn, f, s * P:(s + 1) * P], wsdn[0:fn, f, :], f == 0, f == n - 1)
                        if fs[0] == n - 1:
                            last.then_inc(sh_full, 1)

            def shared(i, b, k):
                pe.wait_ge(sh_loaded[b], k * 32 + 32)
                gate_up(i, b, range(len(FS_CH)))
                down(i, b)

            body(NB - 1, True, False)
            for step in ("P0", "P1", "T10", "T11"):
                wait_drained(pe, step, NB - 1)
            pe.wait_ge(ws_low, KC)
            pe.wait_ge(sh_loaded[0], 32)
            gate_up(0, 0, range(2))
            turn_z(NB)
            gate_up(0, 0, range(2, 4))
            route(NB)
            turn_logits(NB)
            for step, i in (("O0", NB - 1), ("O1", NB - 1), ("LT", NB), ("Z0", NB)):
                wait_drained(pe, step, i)
            gate_up(0, 0, range(4, 6))
            pe.wait_ge(wsdn_loaded, 32)
            down(0, 0)
            pe.wait_ge(sh_loaded[1], 32)
            gate_up(1, 1, range(4))
            pe.wait_ge(sh_out, SH_STEPS)
            pe.wait_ge(r_cnt, 1)
            pe.wait_ge(const2_ready, 1)
            flat = cnt_b[:, :, :].rearrange("p n e -> p (n e)")
            mm(psum_b[3][:, 0:NT * E], upper[:, :], flat, True, True)
            mm(psum_b[3][:, NT * E:2 * NT * E], ones_b[:, :], flat, True, True).then_inc(r_rank, 1)
            gate_up(1, 1, range(4, 6))
            pe.wait_ge(r_ranked, 1)
            down(1, 1)
            for i in range(2, 4):
                shared(i, i % 2, i // 2)
            pe.wait_ge(sh_loaded[0], 2 * 32 + 32)
            gate_up(4, 0, range(4))
            pe.wait_ge(sh_out, 4 * SH_STEPS)
            pe.wait_ge(w_rep_ready, 1)
            nc.tensor.transpose(psum_b[3][:, 0:P], w_rep, ident[:, :]).then_inc(w_rep_turned, 1)
            gate_up(4, 0, range(4, 6))
            pe.wait_ge(w_low16, 1)
            down(4, 0)
            shared(5, 1, 2)
            with pe.Fori(3, SHARED_FIRST // 2) as k:
                for b in range(2):
                    shared(k * 2 + b, b, k)
            pe.wait_ge(sh_out, SHARED_FIRST * SH_STEPS)

            t_bank, a_bank, d_bank = psum_b[0], psum_b[1], psum_b[2]

            def g_bank(b, half):
                return psum_a[:, (2 * b + half) * BANK:(2 * b + half) * BANK + F]

            def turn_rows(j, b, k):
                pe.wait_ge(g_loaded[b], k * 16 + 16)
                if not (isinstance(j, int) and j == 0):
                    pe.wait_ge(t_out, j)
                for kc in range(KC):
                    last = nc.tensor.transpose(t_bank[:, kc * P:(kc + 1) * P], zg[:, b, kc * P:(kc + 1) * P], ident[:, :])
                last.then_inc(t_full, 1)

            def open_expert(j, b):
                e = pe.value_load(slot_expert[0:1, bass.ds(j, 1)], min_val=0, max_val=E - 1)
                pe.wait_ge(t_out, j + 1)
                if not (isinstance(j, int) and j < 2):
                    pe.wait_ge(g_out, j - 1)
                for kc in range(KC):
                    for zp, wp in PARTS:
                        for half in range(2):
                            last = mm(g_bank(b, half), zg_t[:, b, zp, kc * P:(kc + 1) * P],
                                      wgu[:, bass.ds(e * UNIT + ((wp * KC + kc) * 2 + half) * F, F)],
                                      kc == 0 and (zp, wp) == PARTS[0], kc == KC - 1 and (zp, wp) == PARTS[-1])
                last.then_inc(g_full, 1)
                return e

            def turn_act(j, b):
                pe.wait_ge(g_out, j + 1)
                if not (isinstance(j, int) and j == 0):
                    pe.wait_ge(a_out, j)
                for f, (f0, fn) in enumerate(F_CH):
                    last = nc.tensor.transpose(a_bank[0:fn, f * P:(f + 1) * P], silu[:, b, f0:f0 + fn], ident[:, :])
                last.then_inc(a_full, 1)

            def close_expert(j, b):
                e = pe.value_load(slot_expert[0:1, bass.ds(j, 1)], min_val=0, max_val=E - 1)
                pe.wait_ge(a_out, j + 1)
                if not (isinstance(j, int) and j == 0):
                    pe.wait_ge(d_out, j)
                for f, (f0, fn) in enumerate(F_CH):
                    last = mm(d_bank[:, :], act_t[0:fn, b, f * P:(f + 1) * P], wdn[0:fn, f, bass.ds(e * D, D)],
                              f == 0, f == len(F_CH) - 1)
                last.then_inc(d_full, 1)

            pe.wait_ge(ids_float, 1)
            nc.tensor.transpose(psum_b[3][:, 0:SLOTS], id_rows[:, :], ident[0:SLOTS, 0:SLOTS]).then_inc(ids_turned, 1)
            pe.wait_ge(w_low16, 1 + 2 * E)
            pe.wait_ge(wdn_loaded, 16 * len(F_CH))
            pe.wait_ge(r_pos, 1)
            turn_rows(0, 0, 0)
            open_expert(0, 0)
            turn_rows(1, 1, 0)
            turn_act(0, 0)
            open_expert(1, 1)
            turn_rows(2, 0, 1)
            close_expert(0, 0)
            turn_act(1, 1)
            with pe.Fori(1, SLOTS // 2 - 1) as k:
                for b in range(2):
                    j = k * 2 + b
                    open_expert(j, b)
                    turn_rows(j + 1, 1 - b, k + b)
                    close_expert(j - 1, 1 - b)
                    turn_act(j, b)
            j = SLOTS - 2
            open_expert(j, 0)
            turn_rows(j + 1, 1, SLOTS // 2 - 1)
            close_expert(j - 1, 1)
            turn_act(j, 0)
            open_expert(j + 1, 1)
            close_expert(j, 0)
            turn_act(j + 1, 1)
            close_expert(j + 1, 1)
            pe.wait_ge(d_out, SLOTS)
            for i in range(SHARED_FIRST, NB):
                shared(i, i % 2, i // 2)

        @block.scalar
        def _(act):
            def copy(o, i_):
                return nc.scalar.activation(o, i_, ACT.Copy)

            def heads_out(step, dst, b):
                view = dst[:, :, :].rearrange("p t (b c l) -> p b l c t", b=2, c=2)
                for l in range(4):
                    last = copy(view[:, b, l], bank_ap(step)[HD * l:HD * (l + 1), :].rearrange("p (c t) -> p c t", c=2))
                last.then_inc(drained[BANK_OF[step]], 1)

            def z_out(i):
                if not (isinstance(i, int) and i == 1):
                    act.wait_ge(zt_stored, (i - 1) * 16)
                for s in range(SUB):
                    wait_full(act, f"Z{s}", i)
                    turned = bank_ap(f"Z{s}").rearrange("p (c t) -> p c t", c=KC)
                    copy(z_t[:, :, s * P:(s + 1) * P], turned)
                    nc.scalar.activation(z_parts[:, HI, :, s * P:(s + 1) * P], turned, ACT.Copy, scale=2.0 ** Z_EXP).then_inc(zt_high, 1)

            def x_out(i):
                for s in range(SUB):
                    wait_full(act, f"X{s}", i)
                    copy(xn_t[:, HI, :, s * P:(s + 1) * P], bank_ap(f"X{s}").rearrange("p (c t) -> p c t", c=KC)).then_inc(xt_high, 1)

            def projected(i, step, dst, b):
                wait_full(act, step, i)
                heads_out(step, dst, b)

            def shared_high(kcs):
                for kc in kcs:
                    nc.scalar.activation(wsgu[:, HI, kc, :], wsgu_in[:, kc, :], ACT.Copy, scale=ws_scale[:, 2:3]).then_inc(ws_high, 1)

            def pairs_out(s, i):
                wait_full(act, f"VT{s}", i)
                copy(v_p[:, s * NG:(s + 1) * NG, :], bank_ap(f"VT{s}").rearrange("p (g d) -> p g d", d=HD)).then_inc(drained[BANK_OF[f"VT{s}"]], 1)

            def weights_out(s, i):
                for u in range(NU):
                    step = f"T{s}{u}"
                    wait_full(act, step, i)
                    copy(spread_t[:, s, u * BANK:(u + 1) * BANK], bank_ap(step)).then_inc(drained[BANK_OF[step]], 1)

            def body(i, behind, ahead):
                if ahead:
                    x_out(i)
                for s in range(SUB):
                    act.wait_ge(shifted, i * SUB + (s + 1))
                    nc.scalar.activation(ex[:, s], sc[:, s], ACT.Exp).then_inc(exp_ready, 1)
                if ahead:
                    wait_full(act, "S13", i)
                    projected(i, "K0", k_t, 0)
                    projected(i, "K1", k_t, 1)
                weights_out(0, i)
                if behind:
                    z_out(i)
                pairs_out(0, i)
                weights_out(1, i)
                pairs_out(1, i)
                if isinstance(i, int) and i == NB - 1:
                    act.wait_ge(ws_scaled, 1)
                    shared_high((0, 1))
                wait_full(act, "P1", i)
                if isinstance(i, int) and i == 0:
                    act.wait_ge(bias_ready, 4)
                else:
                    act.wait_ge(z_stored, i * 16)
                sums_out(copy, 1)
                if ahead:
                    projected(i, "V1", v_t, 1)

            for part, b in enumerate((bq, bk, bv, bo)):
                act.dma_start(b_raw[part], b.partition_broadcast(3)).then_inc(bias_loaded, 16)
            def weights_high(w, w_in, loaded, count):
                act.wait_ge(loaded, count)
                copy(w[:, HI], w_in).then_inc(w_high, 1)

            weights_high(wk, wk_in, wk_loaded, 16)
            x_out(-1)
            weights_high(wq, wq_in, wq_loaded, 16)
            weights_high(wv, wv_in, wv_loaded, 16)
            projected(-1, "K0", k_t, 0)
            projected(-1, "K1", k_t, 1)
            weights_high(wo, wo_in, wo_loaded, 32)
            act.wait_ge(const_ready, 1)
            for rows_below, factor in ((qv_t[HD:HD + GT], onehot), (k_masked[HD:HD + GT], other)):
                copy(rows_below.rearrange("p (g t) h -> p g (t h)", t=GT), factor[:, :].unsqueeze(1).broadcast_to([GT, BT // GT, P])).then_inc(mask_ready, 1)
            projected(-1, "V1", v_t, 1)
            body(0, False, True)
            with act.Fori(1, NB - 1) as i:
                body(i, True, True)
            body(NB - 1, True, False)
            shared_high((2, 3))
            z_out(NB)

            act.wait_ge(r_shift, 1)
            nc.scalar.activation(d_s[:, :, :], d_s[:, :, :], ACT.Exp).then_inc(r_exp, 1)

            def sh_bank(step):
                return psum_a[:, step * BANK:(step + 1) * BANK] if step < 4 else psum_b[step - 4][:, :]

            def gate(i, f):
                fn = FS_CH[f][1]
                act.wait_ge(sh_full, i * SH_STEPS + (f + 1))
                if f >= GB:
                    act.wait_ge(sh_out, i * SH_STEPS + (f - GB + 1))
                nc.scalar.activation(gate_act[0:fn, f % GB, :], sh_bank(f)[0:fn, 0:BT], ACT.Silu, scale=ws_scale[0:fn, 3:4]).then_inc(silu_ready, 1)

            def half_of(i, f):
                e = (i - CONVERT_FROM) * 2 + f // 2
                return e, f % 2 * 2

            def weights_high16(i, f):
                e, c = half_of(i, f)
                act.wait_ge(w_low16, e * 2 + 1)
                act.activation(wgu[:, bass.ds(e * UNIT + c * 2 * F, 4 * F)], wgu_in[:, bass.ds(e + 1, 1), c:c + 2, :].rearrange("p o c n -> p (o c n)"),
                               ACT.Copy, scale=w_scale[:, 2:3]).then_inc(w_high16, 1)

            for first, end, converts in ((0, CONVERT_FROM, False), (CONVERT_FROM, CONVERT_FROM + E // 2, True),
                                         (CONVERT_FROM + E // 2, SHARED_FIRST, False)):
                with act.Fori(first // 2, end // 2) as k:
                    for b in range(2):
                        for f in range(len(FS_CH)):
                            gate(k * 2 + b, f)
                            if converts and f < 4:
                                weights_high16(k * 2 + b, f)

            a_bank, d_bank = psum_b[1], psum_b[2]

            def rows_high(j, b):
                act.wait_ge(t_full, j + 1)
                nc.scalar.activation(zg_t[:, b, HI, :], psum_b[0][:, :], ACT.Copy, scale=2.0 ** Z_EXP).then_inc(zg_high, 1)

            def step(j, b, k):
                act.wait_ge(g_full, j + 1)
                nc.scalar.activation(silu[:, b, :], psum_a[:, 2 * b * BANK:2 * b * BANK + F], ACT.Silu, scale=w_scale[:, 3:4]).then_inc(g_silu, 1)
                if not (isinstance(j, int) and j == SLOTS - 1):
                    rows_high(j + 1, 1 - b)
                if not (isinstance(j, int) and j == 0):
                    rows_out(j - 1, 1 - b, k - 1 + b)
                act.wait_ge(a_full, j + 1)
                copy(act_t[:, b, 0:2 * P], a_bank[:, 0:2 * P])
                copy(act_t[0:F_CH[2][1], b, 2 * P:3 * P], a_bank[0:F_CH[2][1], 2 * P:3 * P]).then_inc(a_out, 1)

            def rows_out(j, b, k):
                act.wait_ge(d_full, j + 1)
                if not (isinstance(j, int) and j < 2):
                    act.wait_ge(y_stored[b], k * 16)
                copy(y_sb[:, b, :], d_bank[:, :]).then_inc(d_out, 1)

            rows_high(0, 0)
            for j in range(4):
                step(j, j % 2, j // 2)
            with act.Fori(2, SLOTS // 2 - 1) as k:
                for b in range(2):
                    step(k * 2 + b, b, k)
            for j in range(SLOTS - 2, SLOTS):
                step(j, j % 2, j // 2)
            rows_out(SLOTS - 1, 1, SLOTS // 2 - 1)

            def load_base(n):
                b = n % CB
                if n >= CB:
                    act.wait_ge(c_done, n - CB + 1)
                i = n // SUB
                act.wait_ge(base_stored[i % 2], 16 * (i // 2 + 1))
                act.dma_start(comb[2][:, b, :], base_d[n * P:(n + 1) * P, :]).then_inc(cb_loaded[b], 16)

            load_base(0)
            load_base(1)
            n = 2
            for i, tiles in zip(range(SHARED_FIRST, NB), TAIL_TILES):
                for f in range(len(FS_CH)):
                    gate(i, f)
                    for _ in range(tiles_after(f, tiles)):
                        if n < SUB * i:
                            load_base(n)
                            n += 1
            while n < NT:
                load_base(n)
                n += 1

        @block.vector
        def _(dve):
            own_ = Chain(dve, dve_own)
            link, mark = own_.link, own_.mark
            V = nc.vector

            def split_bias(part):
                raw = b_raw[part]
                link(V.tensor_copy(b_bf, raw))
                link(V.tensor_copy(b_part[0], b_bf))
                link(V.tensor_tensor(b_rest, raw, b_part[0], ALU.subtract))
                link(V.tensor_copy(b_bf, b_rest))
                link(V.tensor_copy(b_part[1], b_bf))
                link(V.tensor_tensor(b_rest, b_rest, b_part[1], ALU.subtract))
                link(V.tensor_scalar(raw, b_part[0], ident[0:3, 0:1], None, ALU.mult))
                link(V.scalar_tensor_tensor(out=b_part[1], in0=b_part[1], scalar=ident[0:3, 1:2], in1=raw, op0=ALU.mult, op1=ALU.add))
                link(V.scalar_tensor_tensor(out=raw, in0=b_rest, scalar=ident[0:3, 2:3], in1=b_part[1], op0=ALU.mult, op1=ALU.add))
                V.tensor_copy(bias3[0:3, part * D:(part + 1) * D], raw).then_inc(bias_ready, 1)

            def x_stats(i):
                dve.wait_ge(x_loaded, i * 16 + 16)
                for s in range(SUB):
                    mark(V.bn_stats(stats[:, s, :], x_sb[:, s, :]))
                own_.wait()
                for s in range(SUB):
                    settle(dve)
                    V.bn_aggr(mv[:, s, :], stats[:, s, :]).then_inc(stat_ready, 1)

            def normalise_x(i):
                for s in range(SUB):
                    dve.wait_ge(rstd_ready, stat_no(i, 0, s))
                    V.tensor_scalar(xn[:, s, :], x_sb[:, s, :], mv[:, s, 0:1], rstd[:, s:s + 1], ALU.subtract, ALU.mult).then_inc(xn_ready, 1)

            def heads_out(step, dst, b):
                view = dst[:, :, :].rearrange("p t (b c l) -> p b l c t", b=2, c=2)
                for l in range(4):
                    last = V.tensor_copy(view[:, b, l], bank_ap(step)[HD * l:HD * (l + 1), :].rearrange("p (c t) -> p c t", c=2))
                last.then_inc(drained[BANK_OF[step]], 1)

            def own_scores(i, s, us):
                for u in us:
                    step = f"S{s}{u}"
                    wait_full(dve, step, i)
                    ins = V.tensor_reduce(out=sc[:, s, u * UG:(u + 1) * UG, :],
                                          in_=bank_ap(step).rearrange("p (r t g) -> p r g t", r=UG, t=GT), axis=X, op=ALU.max)
                    ins.then_inc(drained[BANK_OF[step]], 1)

            def shift(i, s):
                for u in range(NU):
                    wait_drained(dve, f"S{s}{u}", i)
                link(V.tensor_reduce(out=row_max[:, s, :], in_=sc[:, s], axis=X, op=ALU.max))
                V.tensor_tensor(sc[:, s], sc[:, s], row_max[:, s, :].unsqueeze(2).broadcast_to([P, NG, H]), ALU.subtract).then_inc(shifted, 1)

            def softmax(i, s):
                dve.wait_ge(exp_ready, i * SUB + (s + 1))
                link(V.tensor_reduce(out=row_sum[:, s, :], in_=ex[:, s], axis=X, op=ALU.add))
                link(V.reciprocal(row_inv[:, s, :], row_sum[:, s, :]))
                V.tensor_tensor(pr[:, s], ex[:, s], row_inv[:, s, :].unsqueeze(2).broadcast_to([P, NG, H]), ALU.mult).then_inc(pr_ready, 1)

            def find_scale(scale, turned):
                power, up, down = (scale[:, n:n + 1].bitcast(U32) for n in (1, 2, 3))
                link(V.tensor_reduce(out=scale[:, 0:1], in_=turned, axis=X, op=ALU.max))
                link(V.tensor_scalar(power, scale[:, 0:1].bitcast(U32), EXPONENT, None, ALU.bitwise_and))
                link(V.tensor_scalar(power, power, float(SMALLEST << 23), None, ALU.max))
                mark(V.tensor_scalar(up, power, -1.0, float((2 * 127 + W_EXP) << 23), ALU.mult, ALU.add))
                link(V.tensor_scalar(down, power, float((W_EXP + Z_EXP) << 23), None, ALU.subtract))

            def z_low(i):
                for s in range(SUB):
                    dve.wait_ge(zt_high, (i - 1) * SUB + (s + 1))
                    V.scalar_tensor_tensor(out=z_parts[:, LO, :, s * P:(s + 1) * P], in0=bank_ap(f"Z{s}").rearrange("p (c t) -> p c t", c=KC),
                                           scalar=2.0 ** Z_EXP, in1=z_parts[:, HI, :, s * P:(s + 1) * P],
                                           op0=ALU.mult, op1=ALU.subtract).then_inc(drained[BANK_OF[f"Z{s}"]], 1)

            def logits_out(i):
                wait_full(dve, "L", i)
                V.tensor_copy(logits_t[:, :], bank_ap("L")[0:E, 0:BT]).then_inc(drained[BANK_OF["L"]], 1)

            def turned_logits_out(i):
                wait_full(dve, "LT", i)
                V.tensor_copy(tok_scores[:, bass.ds((i - 1) * SUB, SUB), :], bank_ap("LT")[:, 0:SUB * E].rearrange("p (s e) -> p s e", s=SUB)).then_inc(drained[BANK_OF["LT"]], 1)

            def projected(i, step, dst, b):
                wait_full(dve, step, i)
                heads_out(step, dst, b)

            def shared_low(kc):
                dve.wait_ge(ws_high, kc + 1)
                V.scalar_tensor_tensor(out=wsgu[:, LO, kc, :], in0=wsgu_in[:, kc, :], scalar=ws_scale[:, 2:3], in1=wsgu[:, HI, kc, :],
                                       op0=ALU.mult, op1=ALU.subtract).then_inc(ws_low, 1)

            def body(i, behind, ahead, ahead2):
                if ahead:
                    x_low(i)
                own_scores(i, 0, range(NU))
                shift(i, 0)
                if ahead2:
                    x_stats(i + 2)
                own_scores(i, 1, range(2))
                softmax(i, 0)
                own_scores(i, 1, range(2, NU))
                shift(i, 1)
                if ahead2:
                    wait_full(dve, "X1", i)
                    normalise_x(i + 2)
                softmax(i, 1)
                if ahead:
                    projected(i, "Q0", q_t, 0)
                    projected(i, "Q1", q_t, 1)
                if isinstance(i, int) and i == 0:
                    split_bias(3)
                    dve.wait_ge(bias_ready, 4)
                if behind:
                    z_low(i)
                if isinstance(i, int) and i == NB - 1:
                    dve.wait_ge(ws_loaded, 16)
                    link(V.tensor_reduce(out=ws_scale[:, 0:1], in_=wsgu_in[:, :, :].rearrange("p c n -> p (c n)"), axis=X, op=ALU.max, apply_absolute_value=True))
                    V.tensor_copy(ws_rep, ws_scale[:, 0:1].broadcast_to([P, P])).then_inc(ws_rep_ready, 1)
                    dve.wait_ge(ws_rep_turned, 1)
                    find_scale(ws_scale, bank_ap("O1")[:, 0:P])
                    dve.sem_inc(ws_scaled, 1)
                wait_full(dve, "VT1", i)
                if ahead:
                    projected(i, "V0", v_t, 0)
                if behind:
                    logits_out(i)
                wait_full(dve, "P0", i)
                if not (isinstance(i, int) and i == 0):
                    dve.wait_ge(x1_stored, i * 16)
                    dve.wait_ge(z_stored, i * 16)
                sums_out(V.tensor_copy, 0)
                for s in range(SUB):
                    hi, lo = (at_t[:, part, :, s * P:(s + 1) * P] for part in (HI, LO))
                    raw = at_raw[:, :, s * P:(s + 1) * P]
                    wait_drained(dve, f"P{s}", i)
                    link(V.tensor_copy(hi, raw))
                    low(V, lo, raw, hi).then_inc(at_split, 1)
                if behind:
                    turned_logits_out(i)
                for s in range(SUB):
                    if isinstance(i, int) and i == NB - 1:
                        shared_low(2 * s)
                        shared_low(2 * s + 1)
                    wait_full(dve, f"O{s}", i)
                    dve.wait_ge(res_loaded, i * 16 + 16)
                    V.tensor_tensor(x1[:, s, :], bank_ap(f"O{s}"), x_res[:, s, :], ALU.add).then_inc(drained[BANK_OF[f"O{s}"]], 1)
                    wait_drained(dve, f"O{s}", i)
                    link(V.bn_stats(stats[:, SUB + s, :], x1[:, s, :]))
                    settle(dve)
                    V.bn_aggr(mv[:, SUB + s, :], stats[:, SUB + s, :]).then_inc(stat_ready, 1)
                for s in range(SUB):
                    dve.wait_ge(rstd_ready, stat_no(i, 1, s))
                    V.tensor_scalar(z[:, s, :], x1[:, s, :], mv[:, SUB + s, 0:1], rstd[:, SUB + s:SUB + s + 1], ALU.subtract, ALU.mult).then_inc(z_ready, 1)

            def x_low(i):
                for s in range(SUB):
                    dve.wait_ge(xt_high, (i + 1) * SUB + (s + 1))
                    low(V, xn_t[:, LO, :, s * P:(s + 1) * P], bank_ap(f"X{s}").rearrange("p (c t) -> p c t", c=KC),
                        xn_t[:, HI, :, s * P:(s + 1) * P]).then_inc(drained[BANK_OF[f"X{s}"]], 1)

            x_stats(0)
            normalise_x(0)
            dve.wait_ge(w_high, 1)
            low(V, wk[:, LO], wk_in, wk[:, HI]).then_inc(wk_split, 1)
            x_low(-1)
            dve.wait_ge(bias_loaded, 16 * 4)
            dve.wait_ge(ident_ready, 1)
            split_bias(1)
            split_bias(0)
            split_bias(2)
            x_stats(1)
            wait_full(dve, "X1", -1)
            normalise_x(1)
            projected(-1, "Q0", q_t, 0)
            projected(-1, "Q1", q_t, 1)
            projected(-1, "V0", v_t, 0)
            body(0, False, True, True)
            DVE_SIGNALS = 12
            with dve.Fori(1, NB - 2) as i:
                own_.enter(i - 1, DVE_SIGNALS)
                body(i, True, True, True)
            own_.leave(NB - 3)
            body(NB - 2, True, True, False)
            body(NB - 1, True, False, False)
            z_low(NB)
            logits_out(NB)
            turned_logits_out(NB)
            wait_drained(dve, "LT", NB)
            dve.wait_ge(z_stored, 16 * NB)
            dve.wait_ge(x1_stored, 16 * NB)
            dve.wait_ge(zt_stored, 16 * NB)
            link(V.tensor_reduce(out=d_m[:, :], in_=tok_scores[:, :, :], axis=X, op=ALU.max))
            V.tensor_tensor(d_s[:, :, :], tok_scores[:, :, :], d_m[:, :].unsqueeze(2).broadcast_to([P, NT, E]), ALU.subtract).then_inc(r_shift, 1)

            def sh_bank(step):
                return psum_a[:, step * BANK:(step + 1) * BANK] if step < 4 else psum_b[step - 4][:, :]

            def gate_times_up(i, f):
                fn = FS_CH[f][1]
                dve.wait_ge(silu_ready, i * len(FS_CH) + (f + 1))
                V.scalar_tensor_tensor(out=sh_t[0:fn, f, :], in0=sh_bank(f)[0:fn, BT:2 * BT], scalar=ws_scale[0:fn, 3:4],
                                       in1=gate_act[0:fn, f % GB, :], op0=ALU.mult, op1=ALU.mult).then_inc(sh_out, 1)

            def add_shared(i, b):
                for s in range(SUB):
                    n = len(FS_CH) + s
                    dve.wait_ge(sh_full, i * SH_STEPS + (n + 1))
                    V.tensor_tensor(base[:, b, s, :], sh_bank(n), base[:, b, s, :], ALU.add).then_inc(sh_out, 1)

            def largest(u):
                mark(V.tensor_reduce(out=w_max[:, u:u + 1], in_=wgu_in[:, 1 + u // 2, u % 2 * 2:u % 2 * 2 + 2, :].rearrange("p c n -> p (c n)"),
                                     axis=X, op=ALU.max, apply_absolute_value=True))

            def weights_low16(i, f):
                e, c = (i - CONVERT_FROM) * 2 + f // 2, f % 2 * 2
                dve.wait_ge(w_high16, (i - CONVERT_FROM) * 4 + (f + 1))
                V.scalar_tensor_tensor(out=wgu[:, bass.ds(e * UNIT + (KC + c) * 2 * F, 4 * F)], in0=wgu_in[:, bass.ds(e + 1, 1), c:c + 2, :].rearrange("p o c n -> p (o c n)"),
                                       scalar=w_scale[:, 2:3], in1=wgu[:, bass.ds(e * UNIT + c * 2 * F, 4 * F)], op0=ALU.mult, op1=ALU.subtract).then_inc(w_low16, 1)

            def shared_block(i, b, k, after):
                for f in range(len(FS_CH)):
                    gate_times_up(i, f)
                    after(f)
                dve.wait_ge(sh_loaded[b], k * 32 + 32)
                add_shared(i, b)

            def nothing(f):
                pass

            shared_block(0, 0, 0, nothing)
            dve.wait_ge(r_exp, 1)
            mark(V.memset(ones_f[:, :], 1.0))
            dve.wait_ge(const2_ready, 1)
            link(V.tensor_reduce(out=d_m[:, :], in_=d_s[:, :, :], axis=X, op=ALU.add))
            link(V.reciprocal(d_m[:, :], d_m[:, :]))
            link(V.tensor_tensor(d_s[:, :, :], d_s[:, :, :], d_m[:, :].unsqueeze(2).broadcast_to([P, NT, E]), ALU.mult))
            for n in range(NT):
                mark(V.max(top_w[:, n, :], d_s[:, n, :]))
            own_.wait()
            for n in range(NT):
                mark(V.max_index(d_ix[:, n, :], top_w[:, n, :], d_s[:, n, :]))
            own_.wait()
            link(V.tensor_copy(d_ixf[:, :, :], d_ix[:, :, 0:TOPK].rearrange("p n k -> p k n")))
            for k in range(TOPK):
                mark(V.tensor_tensor(picked[:, k], d_ixf[:, k, :].unsqueeze(2).broadcast_to([P, NT, E]),
                                     iota_e[:, :].unsqueeze(1).broadcast_to([P, NT, E]), ALU.is_equal))
            own_.wait()
            V.tensor_tensor(cnt_b[:, :, :], picked[:, 0], picked[:, 1], ALU.add).then_inc(r_cnt, 1)
            dve.wait_ge(r_rank, 1)
            mark(V.tensor_copy(rank[:, :, :], psum_b[3][:, 0:NT * E].rearrange("p (n e) -> p n e", e=E)))
            link(V.tensor_copy(tot[:, :, :], psum_b[3][:, NT * E:2 * NT * E].rearrange("p (n e) -> p n e", e=E)))
            dve.sem_inc(r_ranked, 1)
            shared_block(1, 1, 0, nothing)
            for e in range(E):
                mark(V.tensor_tensor_scan(out=run[:, :, e], data0=ones_f[:, :], data1=tot[:, :, e], initial=0.0, op0=ALU.mult, op1=ALU.add))
            own_.wait()
            link(V.tensor_tensor(wide[:, 0:NT, :], run[:, NT - 1, :].unsqueeze(1).broadcast_to([P, NT, E]),
                                 iota_rows[:, :].unsqueeze(2).broadcast_to([P, NT, E]), ALU.is_gt))
            link(V.tensor_reduce(out=tiles_of[:, 0, :], in_=wide[:, 0:NT, :].rearrange("p n e -> p e n"), axis=X, op=ALU.add))
            link(V.tensor_tensor_scan(out=tiles_of[:, 1, :], data0=ones_f[:, 0:E], data1=tiles_of[:, 0, :], initial=0.0, op0=ALU.mult, op1=ALU.add))
            link(V.tensor_tensor(tiles_of[:, 2, :], tiles_of[:, 1, :], tiles_of[:, 0, :], ALU.subtract))
            link(V.tensor_scalar(tiles_of[:, 3, :], tiles_of[:, 2, :], float(P), None, ALU.mult))
            link(V.tensor_tensor(wide[:, :, 0:E - 1], tiles_of[:, 2, 1:E].unsqueeze(1).broadcast_to([P, SLOTS, E - 1]),
                                 iota_slot[:, :].unsqueeze(2).broadcast_to([P, SLOTS, E - 1]), ALU.is_le))
            link(V.tensor_reduce(out=slot_f[:, :], in_=wide[:, :, 0:E - 1], axis=X, op=ALU.add))
            mark(V.tensor_copy(slot_expert[:, :], slot_f[:, :]))
            link(V.tensor_tensor(rank[:, :, :], rank[:, :, :], run[:, :, :], ALU.add))
            link(V.tensor_tensor(rank[:, :, :], rank[:, :, :], tot[:, :, :], ALU.subtract))
            link(V.tensor_tensor(rank[:, :, :], rank[:, :, :], tiles_of[:, 3, :].unsqueeze(1).broadcast_to([P, NT, E]), ALU.add))
            for k in range(TOPK):
                link(V.tensor_tensor(picked[:, k], picked[:, k], rank[:, :, :], ALU.mult))
                link(V.tensor_reduce(out=posf[:, k, :], in_=picked[:, k], axis=X, op=ALU.add))
            V.tensor_copy(pos[:, :, :], posf[:, :, :]).then_inc(r_pos, 1)

            dve.wait_ge(wgu_loaded, 16 * E)
            for i in (2, 3):
                units = iter(range((i - 2) * E, (i - 1) * E))
                shared_block(i, i % 2, i // 2, lambda f: [largest(next(units)) for _ in range(2 if f % 3 == 2 else 1)])
            own_.wait()
            link(V.tensor_reduce(out=w_scale[:, 0:1], in_=w_max, axis=X, op=ALU.max))
            V.tensor_copy(w_rep, w_scale[:, 0:1].broadcast_to([P, P])).then_inc(w_rep_ready, 1)

            def routed_scale():
                dve.wait_ge(w_rep_turned, 1)
                find_scale(w_scale, psum_b[3][:, 0:P])
                dve.sem_inc(w_low16, 1)

            shared_block(4, 0, 2, lambda f: routed_scale() if f == 3 else None)
            shared_block(5, 1, 2, nothing)
            for first, end, converts in ((CONVERT_FROM, CONVERT_FROM + E // 2, True), (CONVERT_FROM + E // 2, SHARED_FIRST, False)):
                with dve.Fori(first // 2, end // 2) as k:
                    for b in range(2):
                        shared_block(k * 2 + b, b, k, lambda f: weights_low16(k * 2 + b, f) if converts and f < 4 else None)

            t_bank = psum_b[0]
            dve.wait_ge(ids_loaded, 16)
            V.tensor_copy(id_rows[:, :], zero_id[:, :]).then_inc(ids_float, 1)
            dve.wait_ge(ids_turned, 1)
            link(V.tensor_copy(ids_col[:, :], psum_b[3][:, 0:SLOTS]))

            def index_out(j, b, k):
                if not (isinstance(j, int) and j < 2):
                    dve.wait_ge(g_loaded[b], k * 16)
                V.tensor_copy(gather_ix[:, b:b + 1], ids_col[:, bass.ds(j, 1)]).then_inc(g_ix, 1)

            def rows_low(j, b):
                dve.wait_ge(zg_high, j + 1)
                V.scalar_tensor_tensor(out=zg_t[:, b, LO, :], in0=t_bank[:, :], scalar=2.0 ** Z_EXP, in1=zg_t[:, b, HI, :],
                                       op0=ALU.mult, op1=ALU.subtract).then_inc(t_out, 1)

            def gated(j, b):
                dve.wait_ge(g_silu, j + 1)
                V.scalar_tensor_tensor(out=silu[:, b, :], in0=psum_a[:, (2 * b + 1) * BANK:(2 * b + 1) * BANK + F], scalar=w_scale[:, 3:4],
                                       in1=silu[:, b, :], op0=ALU.mult, op1=ALU.mult).then_inc(g_out, 1)

            index_out(0, 0, 0)
            index_out(1, 1, 0)
            rows_low(0, 0)
            for j in range(2):
                index_out(j + 2, j, 1)
                gated(j, j)
                rows_low(j + 1, 1 - j)
            with dve.Fori(1, SLOTS // 2 - 1) as k:
                for b in range(2):
                    j = k * 2 + b
                    index_out(j + 2, b, k + 1)
                    gated(j, b)
                    rows_low(j + 1, 1 - b)
            gated(SLOTS - 2, 0)
            rows_low(SLOTS - 1, 1)
            gated(SLOTS - 1, 1)

            def combine(n, b, k):
                dve.wait_ge(cb_loaded[b], k * 16 + 16)
                dve.wait_ge(c_loaded[b], k * 32 + 32)
                link(V.scalar_tensor_tensor(out=comb[2][:, b, :], in0=comb[0][:, b, :], scalar=top_w[:, bass.ds(n, 1), 0],
                                            in1=comb[2][:, b, :], op0=ALU.mult, op1=ALU.add))
                if n >= CB:
                    dve.wait_ge(out_stored[b], k * 16)
                V.scalar_tensor_tensor(out=comb_out[:, b, :], in0=comb[1][:, b, :], scalar=top_w[:, bass.ds(n, 1), 1],
                                       in1=comb[2][:, b, :], op0=ALU.mult, op1=ALU.add).then_inc(c_done, 1)

            n = 0
            for i, tiles in zip(range(SHARED_FIRST, NB), TAIL_TILES):
                for f in range(len(FS_CH)):
                    gate_times_up(i, f)
                    for _ in range(tiles_after(f, tiles)):
                        combine(n, n % CB, n // CB)
                        n += 1
                dve.wait_ge(sh_loaded[i % 2], (i // 2) * 32 + 32)
                add_shared(i, i % 2)
            while n < NT:
                combine(n, n % CB, n // CB)
                n += 1

        @block.gpsimd
        def _(pool):
            own_ = Chain(pool, pool_own)
            link, mark = own_.link, own_.mark
            G = nc.gpsimd

            def inverse_std(col, n):
                pool.wait_ge(stat_ready, n)
                settle(pool)
                link(G.tensor_scalar_add(var_eps[:, col:col + 1], mv[:, col, 1:2], EPS))
                G.tensor_tensor(rstd[:, col:col + 1], var_eps[:, col:col + 1], neg_half[:, :], ALU.pow).then_inc(rstd_ready, 1)

            mark(G.memset(ident[:, :], 0.0))
            mark(G.memset(neg_half[:, :], -0.5))
            mark(G.memset(ones3[:, :], 1.0))
            link(G.memset(bias3[:, :], 0.0))
            G.affine_select(out=ident[:, :], in_=ident[:, :], compare_op=ALU.not_equal, fill=1.0, base=0,
                            pattern=[[-1, P]], channel_multiplier=1).then_inc(ident_ready, 1)
            for n in range(SUB):
                inverse_std(n, n + 1)

            def split_context(i):
                if not (isinstance(i, int) and i == 0):
                    wait_full(pool, "V1", i - 2)
                    settle(pool)
                pool.wait_ge(cx_loaded, i * 16 + 16)
                settle(pool)
                link(G.tensor_copy(cx_t[:, HI], cx_in[:, :, :]))
                low(G, cx_t[:, LO], cx_in[:, :, :], cx_t[:, HI]).then_inc(cx_split, 1)

            split_context(0)

            def weights_low(n, w, w_in, done):
                pool.wait_ge(w_high, n)
                low(G, w[:, LO], w_in, w[:, HI]).then_inc(done, 1)

            weights_low(2, wq, wq_in, wq_split)
            weights_low(3, wv, wv_in, wv_split)
            mark(G.memset(onehot[:, :], 1.0))
            mark(G.memset(other[:, :], 1.0))
            link(G.memset(own[:, :], 1.0))
            for tile, dims in ((onehot, [[1, P]]), (other, [[1, P]])):
                link(G.affine_select(out=tile[:], in_=tile[:], compare_op=ALU.is_ge, fill=0.0, base=0, pattern=dims, channel_multiplier=-H))
                link(G.affine_select(out=tile[:], in_=tile[:], compare_op=ALU.is_ge, fill=0.0, base=H - 1,
                                     pattern=[[-st, n] for st, n in dims], channel_multiplier=H))
            link(G.affine_select(out=own[:, :], in_=own[:, :], compare_op=ALU.is_ge, fill=0.0, base=0, pattern=[[-H, GT]], channel_multiplier=1))
            link(G.affine_select(out=own[:, :], in_=own[:, :], compare_op=ALU.is_ge, fill=0.0, base=H - 1, pattern=[[H, GT]], channel_multiplier=-1))
            G.tensor_scalar(other[:, :], other[:, :], 1.0, -MASKED, ALU.subtract, ALU.mult).then_inc(const_ready, 1)

            def body(i, ahead2):
                if ahead2:
                    for s in range(SUB):
                        inverse_std(s, stat_no(i + 2, 0, s))
                for s in range(SUB):
                    pool.wait_ge(pr_ready, i * SUB + (s + 1))
                    for u in range(NU):
                        G.tensor_tensor(spread[:, s, u * UG:(u + 1) * UG, :].rearrange("p r (t g) -> p r t g", t=GT),
                                        pr[:, s, u * UG:(u + 1) * UG, :].unsqueeze(2).broadcast_to([P, UG, GT, H]),
                                        own[:, :].unsqueeze(1).unsqueeze(3).broadcast_to([P, UG, GT, H]), ALU.mult).then_inc(spread_ready, 1)
                if ahead2:
                    split_context(i + 2)
                for s in range(SUB):
                    inverse_std(SUB + s, stat_no(i, 1, s))

            for n in range(SUB):
                inverse_std(n, SUB + n + 1)
            split_context(1)
            weights_low(4, wo, wo_in, wo_split)
            body(0, True)
            POOL_SIGNALS = 2 * SUB + 1
            with pool.Fori(1, NB - 2) as i:
                own_.enter(i - 1, POOL_SIGNALS)
                body(i, True)
            own_.leave(NB - 3)
            body(NB - 2, False)
            body(NB - 1, False)

            pool.wait_ge(x1_stored, 16 * NB)
            pool.wait_ge(z_stored, 16 * NB)
            pool.wait_ge(zt_stored, 16 * NB)
            wait_drained(pool, "LT", NB)
            mark(G.iota(iota_e[:, :], [[1, E]], base=0, channel_multiplier=0, allow_small_or_imprecise_dtypes=True))
            mark(G.iota(iota_slot[:, :], [[1, SLOTS]], base=0, channel_multiplier=0, allow_small_or_imprecise_dtypes=True))
            mark(G.iota(iota_rows[:, :], [[P, NT]], base=0, channel_multiplier=0, allow_small_or_imprecise_dtypes=True))
            mark(G.iota(tok_id[:, :], [[P, NT]], base=0, channel_multiplier=1))
            mark(G.memset(zero_id[:, :], 0))
            mark(G.memset(ones_b[:, :], 1.0))
            link(G.memset(upper[:, :], 1.0))
            G.affine_select(out=upper[:, :], in_=upper[:, :], compare_op=ALU.is_gt, fill=0.0, base=0,
                            pattern=[[1, P]], channel_multiplier=-1).then_inc(const2_ready, 1)
            pool.wait_ge(r_pos, 1)
            pool.wait_ge(zero_stored, 16)

            def stage(n, b):
                link(G.tensor_copy(pos_ix[:, b, :], pos[:, :, bass.ds(n, 1)].rearrange("p k o -> p (k o)")))

            def scatter(n, b, k):
                if not (isinstance(k, int) and k == 0):
                    pool.wait_ge(ids_scattered[b], k * (16 * TOPK))
                mark(G.tensor_copy(tok_ix[:, b:b + 1], tok_id[:, bass.ds(n, 1)]))
                stage(n, b)
                settle(pool)
                for pick in range(TOPK):
                    pool.indirect_dma_start(out=token_d[:, :], out_offset=bass.IndirectOffsetOnAxis(ap=pos_ix[:, b, pick:pick + 1], axis=0),
                                            in_=tok_ix[:, b:b + 1], in_offset=None).then_inc(ids_scattered[b], 16)

            for b in range(STAGES):
                scatter(b, b, 0)
            with pool.Fori(1, NT // STAGES) as k:
                own_.enter(k - 1, 2 * STAGES)
                for b in range(STAGES):
                    scatter(k * STAGES + b, b, k)
            own_.leave(NT // STAGES - 1)

            for b in range(STAGES):
                pool.wait_ge(ids_scattered[b], 16 * TOPK * NT // STAGES)
            pool.dma_start(zero_id[:, :], token_d.rearrange("(j p) o -> j (p o)", p=P)).then_inc(ids_loaded, 16)

            def gather(j, b):
                pool.wait_ge(g_ix, j + 1)
                if not (isinstance(j, int) and j < 2):
                    pool.wait_ge(t_full, j - 1)
                settle(pool)
                pool.indirect_dma_start(out=zg[:, b, :], out_offset=None, in_=z_d[:, :],
                                        in_offset=bass.IndirectOffsetOnAxis(ap=gather_ix[:, b:b + 1], axis=0)).then_inc(g_loaded[b], 16)

            gather(0, 0)
            gather(1, 1)
            with pool.Fori(1, SLOTS // 2) as k:
                for b in range(2):
                    gather(k * 2 + b, b)

            for b in range(2):
                pool.wait_ge(y_stored[b], 16 * (SLOTS // 2))

            def fetch(n, b):
                if not (isinstance(n, int) and n < CB):
                    pool.wait_ge(c_done, n - CB + 1)
                stage(n, b)
                settle(pool)
                for pick in range(TOPK):
                    pool.indirect_dma_start(out=comb[pick][:, b, :], out_offset=None, in_=y_d[:, :],
                                            in_offset=bass.IndirectOffsetOnAxis(ap=pos_ix[:, b, pick:pick + 1], axis=0)).then_inc(c_loaded[b], 16)

            for b in range(CB):
                fetch(b, b)
            with pool.Fori(1, NT // CB) as k:
                own_.enter(k - 1, CB)
                for b in range(CB):
                    fetch(k * CB + b, b)
            own_.leave(NT // CB - 1)


_INS = ["x", "ctx_t", "wq_t", "bq", "wk_t", "bk", "wv_t", "bv", "wo_t", "bo", "wgate_t", "wgu_t", "wdn_t", "wsgu_t", "wsdn_t"]


_OUT = ((16, 256, 512), "float32")


def kernel(**inputs):
    import numpy as _np
    import concourse.bacc as _bacc
    from concourse import mybir as _mybir
    from concourse.bass_utils import run_bass_kernel_spmd as _run

    given = {k.replace("L0_xattn_", "").replace("L0_ffn_", ""): _np.asarray(v) for k, v in inputs.items()}
    arrays = {
        "x": given["x"].reshape(T, D),
        "ctx_t": given["ctx_2048"].reshape(T, D).T,
        "wq_t": given["Wq"].T, "bq": given["bq"],
        "wk_t": given["Wk"].T, "bk": given["bk"],
        "wv_t": given["Wv"].T, "bv": given["bv"],
        "wo_t": given["Wo"].T, "bo": given["bo"],
        "wgate_t": given["gate_weight"].T,
        "wgu_t": given["gate_up_weights"].transpose(2, 0, 1),
        "wdn_t": given["down_weights"].transpose(2, 0, 1),
        "wsgu_t": given["shared_gate_up"].T,
        "wsdn_t": given["shared_down"].T,
    }
    arrays = {f"in_{k}": _np.ascontiguousarray(v) for k, v in arrays.items()}
    nc = _bacc.Bacc("TRN2", target_bir_lowering=False, num_devices=1)
    args = [nc.dram_tensor(f"in_{k}", arrays[f"in_{k}"].shape, _mybir.dt.from_np(arrays[f"in_{k}"].dtype), kind="ExternalInput").ap()
            for k in _INS]
    out = nc.dram_tensor("out_rows", (T, D), _mybir.dt.from_np(_np.dtype(_OUT[1])), kind="ExternalOutput").ap()
    build(nc, *args, out)
    r = _run(nc, [arrays], core_ids=[0])
    return r.results[0]["out_rows"].reshape(_OUT[0])
```
